# Optimizing a Trainium2 kernel written in Bass

```python
import numpy as np
import jax
import jax.numpy as jnp

def _softmax(x, axis=-1):
    return jax.nn.softmax(x, axis=axis)

def _gelu(x):
    return jax.nn.gelu(x, approximate=True)

def _silu(x):
    return jax.nn.silu(x)

def _sigmoid(x):
    return jax.nn.sigmoid(x)

def _layernorm(x, axis=-1, eps=1e-05):
    m = jnp.mean(x, axis=axis, keepdims=True)
    v = jnp.var(x, axis=axis, keepdims=True)
    return (x - m) / jnp.sqrt(v + eps)

def _scatter_add(tgt, idx, src, axis=0):
    return tgt.at[idx].add(src)

def _segment_sum(src, seg, n):
    return jax.ops.segment_sum(src, seg, n)
kernel_name = 'mk_xattn_ffn_d4_seqx_r8_0a8bfd'

def setup_inputs(seed: int=0):
    np.random.seed(seed)
    _w = jnp.asarray

    def _rec_inputs():
        import jax
        import jax.numpy as jnp
        _rk = jax.random.key(seed)
        x = 0.000341 + 1 * jax.random.normal(jax.random.fold_in(_rk, 1), (8, 128, 256), jnp.float32)
        _lenS = 128 - jax.random.randint(jax.random.fold_in(_rk, 7), (8,), 0, max(1, 128 // 4) + 1, jnp.int32)
        _lenS2 = 128 - jax.random.randint(jax.random.fold_in(_rk, 8), (8,), 0, max(1, 128 // 4) + 1, jnp.int32)
        _ctx_2048P = jax.random.normal(jax.random.fold_in(_rk, 11), (8, 16, 256), jnp.float32)
        _ctx_2048c = jax.random.dirichlet(jax.random.fold_in(_rk, 511), 0.3 * jnp.ones((16,), jnp.float32), (8, 128))
        _ctx_2048t = jnp.einsum('bsk,bkd->bsd', _ctx_2048c, _ctx_2048P)
        _ctx_2048t = _ctx_2048t * jax.lax.rsqrt(jnp.mean(jnp.square(_ctx_2048t)) + 1e-12) * 0.953939
        ctx_2048 = -1.47943e-05 + 1.00017 * (_ctx_2048t + 0.3 * jax.random.normal(jax.random.fold_in(_rk, 611), (8, 128, 256), jnp.float32))
        _validS = jnp.arange(128)[None, :] < _lenS[:, None]
        _validS2 = jnp.arange(128)[None, :] < _lenS2[:, None]
        _causal = jnp.tril(jnp.ones((128, 128), dtype=bool))
        mask_BxS2_bk0 = jnp.logical_not(jnp.broadcast_to(_validS2[:, :], (8, 128)))
        mask_1x1x2048x2048_if1 = jnp.where(jnp.ones((1, 1, 256, 256), dtype=bool), 1, 0).astype(jnp.int32)
        return (x, ctx_2048, mask_BxS2_bk0, mask_1x1x2048x2048_if1)
    x, ctx_2048, mask_BxS2_bk0, mask_1x1x2048x2048_if1 = _rec_inputs()

    def _L0_xattn_setup():
        import jax, jax.numpy as jnp
        import numpy as np

        def _wkv(time_decay, time_first, k, v):
            w = -jnp.exp(time_decay)
            u = time_first
            B, T, C = k.shape
            aa = jnp.zeros((B, C), dtype=k.dtype)
            bb = jnp.zeros((B, C), dtype=k.dtype)
            pp = jnp.full((B, C), -1e+38, dtype=k.dtype)

            def step(carry, kv_t):
                aa, bb, pp = carry
                kt, vt = kv_t
                ww = u + kt
                q = jnp.maximum(pp, ww)
                e1 = jnp.exp(pp - q)
                e2 = jnp.exp(ww - q)
                y_t = (e1 * aa + e2 * vt) / (e1 * bb + e2)
                ww2 = pp + w
                q2 = jnp.maximum(ww2, kt)
                e1b = jnp.exp(ww2 - q2)
                e2b = jnp.exp(kt - q2)
                new_carry = (e1b * aa + e2b * vt, e1b * bb + e2b, q2)
                return (new_carry, y_t)
            ks = jnp.transpose(k, (1, 0, 2))
            vs = jnp.transpose(v, (1, 0, 2))
            _, ys = jax.lax.scan(step, (aa, bb, pp), (ks, vs))
            return jnp.transpose(ys, (1, 0, 2))
        key = jax.random.key(seed)
        k1, k2, k3, k4 = jax.random.split(key, 4)
        B, T, C = (8, 128, 256)
        return {'batch_size': B, 'seq_len': T, 'embedding_dim': C, 'time_decay': jax.random.normal(k1, (C,), dtype=jnp.float32), 'time_first': jax.random.normal(k2, (C,), dtype=jnp.float32), 'k': jax.random.normal(k3, (B, T, C), dtype=jnp.float32), 'v': jax.random.normal(k4, (B, T, C), dtype=jnp.float32)}
    _L0_xattn_all = _L0_xattn_setup()
    _L0_xattn_in = {k: v for k, v in _L0_xattn_all.items() if k in ('time_decay', 'time_first')}
    del _L0_xattn_all

    def _L0_ffn_setup():
        import jax, jax.numpy as jnp
        import numpy as np
        EPS_LN = 1e-05
        EPS_ACT = 1e-05
        EPS_W = 1e-08

        def _layer_norm(x):
            mu = jnp.mean(x, axis=-1, keepdims=True)
            xc = x - mu
            var = jnp.mean(xc * xc, axis=-1, keepdims=True)
            return xc * jax.lax.rsqrt(var + EPS_LN)

        def _activation_quant(x):
            scale = 127.0 / jnp.clip(jnp.max(jnp.abs(x), axis=-1, keepdims=True), EPS_ACT)
            return jnp.clip(jnp.round(x * scale), -128, 127) / scale

        def _weight_quant(w):
            scale = jnp.clip(jnp.mean(jnp.abs(w)), EPS_W)
            return jnp.clip(jnp.round(w / scale), -1, 1) * scale

        def _bitlinear(x, w, b):
            xn = _layer_norm(x)
            xq = _activation_quant(xn)
            wq = _weight_quant(w)
            return jnp.einsum('bsd,fd->bsf', xq, wq) + b
        key = jax.random.key(seed)
        k1, k2, k3, k4, k5 = jax.random.split(key, 5)
        d_model, d_ff = (256, 1024)
        B, S = (4, 256)
        x = jax.random.normal(k1, (B, S, d_model), dtype=jnp.float32)
        lim1 = 1.0 / np.sqrt(d_model)
        lim2 = 1.0 / np.sqrt(d_ff)
        w1 = jax.random.uniform(k2, (d_ff, d_model), jnp.float32, -lim1, lim1)
        b1 = jax.random.uniform(k3, (d_ff,), jnp.float32, -lim1, lim1)
        w2 = jax.random.uniform(k4, (d_model, d_ff), jnp.float32, -lim2, lim2)
        b2 = jax.random.uniform(k5, (d_model,), jnp.float32, -lim2, lim2)
        return {'x': x, 'w1': w1, 'b1': b1, 'w2': w2, 'b2': b2}
    _L0_ffn_all = _L0_ffn_setup()
    _L0_ffn_in = {k: v for k, v in _L0_ffn_all.items() if k in ('w1', 'b1', 'w2', 'b2')}
    del _L0_ffn_all

    def _L1_xattn_setup():
        import jax, jax.numpy as jnp
        import numpy as np
        N_HEAD = 8
        key = jax.random.key(seed)
        k1, k2, k3 = jax.random.split(key, 3)
        b, d, m = (4, 128, 256)
        c, n = (128, 256)
        q = jax.random.normal(k1, (b, d, m), dtype=jnp.float32)
        k = jax.random.normal(k2, (d // d * b, d, n), dtype=jnp.float32).reshape(b, d, n)
        v = jax.random.normal(k3, (b, c, n), dtype=jnp.float32)
        return {'q': q, 'k': k, 'v': v}
    _L1_xattn_all = _L1_xattn_setup()
    _L1_xattn_in = {k: v for k, v in _L1_xattn_all.items() if k in ()}
    del _L1_xattn_all

    def _L1_ffn_setup():
        import jax, jax.numpy as jnp
        import numpy as np
        FP8_MAX = 448.0
        GLOBAL_DIV = 448.0 * 6.0

        def _fp8(x):
            return x.astype(jnp.float8_e4m3fn).astype(jnp.float32)

        def _reorder_quantize_x(x, idx):
            scale = jnp.max(jnp.abs(x)) / GLOBAL_DIV
            xr = (x / scale)[:, idx]
            scale_x = jnp.max(jnp.abs(xr), axis=1, keepdims=True) / FP8_MAX
            qx = _fp8(xr / scale_x)
            return (qx, scale_x, scale)

        def _qlinear(qx, scale_x, scale, W, idx, out_idx=None):
            Wr = W[:, idx]
            w_scale = jnp.max(jnp.abs(Wr), axis=1, keepdims=True) / FP8_MAX
            qw = _fp8(Wr / w_scale)
            y = qx * scale_x @ (qw * w_scale).T * scale
            if out_idx is not None:
                y = y[:, out_idx]
            return y
        key = jax.random.key(seed)
        ks = jax.random.split(key, 6)
        B, S, H, I = (2, 128, 256, 704)
        return {'x': jax.random.normal(ks[0], (B, S, H), jnp.float32), 'w_gate': jax.random.normal(ks[1], (I, H), jnp.float32) * 0.02, 'w_up': jax.random.normal(ks[2], (I, H), jnp.float32) * 0.02, 'w_down': jax.random.normal(ks[3], (H, I), jnp.float32) * 0.02, 'up_reorder_index': jax.random.permutation(ks[4], jnp.arange(H, dtype=jnp.int64)), 'down_reorder_index': jax.random.permutation(ks[5], jnp.arange(I, dtype=jnp.int64))}
    _L1_ffn_all = _L1_ffn_setup()
    _L1_ffn_in = {k: v for k, v in _L1_ffn_all.items() if k in ('w_gate', 'w_up', 'w_down', 'up_reorder_index', 'down_reorder_index')}
    del _L1_ffn_all

    def _L2_xattn_setup():
        import jax, jax.numpy as jnp
        import numpy as np
        key = jax.random.key(seed)
        k1, k2, k3 = jax.random.split(key, 3)
        B, S, D, M = (8, 256, 256, 128)
        hidden_states = jax.random.normal(k1, (B, S, D), dtype=jnp.float32)
        memory_tokens = jax.random.normal(k2, (B, M, D), dtype=jnp.float32)
        memory_mask = jax.random.randint(k3, (B, M), 0, 2).astype(jnp.bool_)
        return {'hidden_states': hidden_states, 'memory_tokens': memory_tokens, 'memory_mask': memory_mask}
    _L2_xattn_all = _L2_xattn_setup()
    _L2_xattn_in = {k: v for k, v in _L2_xattn_all.items() if k in ()}
    del _L2_xattn_all

    def _L2_ffn_setup():
        import jax, jax.numpy as jnp
        import numpy as np
        HIDDEN = 256
        INTER = 128
        N_EXPERTS = 64
        TOP_K = 8
        B, T = (1, 64)
        key = jax.random.key(seed)
        k_x, k_r, k_g, k_u, k_d = jax.random.split(key, 5)
        s_in = 1.0 / np.sqrt(HIDDEN)
        s_mid = 1.0 / np.sqrt(INTER)
        return {'x': jax.random.normal(k_x, (B, T, HIDDEN), dtype=jnp.float32), 'w_router': jax.random.normal(k_r, (HIDDEN, N_EXPERTS), dtype=jnp.float32) * s_in, 'w_gate': jax.random.normal(k_g, (N_EXPERTS, HIDDEN, INTER), dtype=jnp.float32) * s_in, 'w_up': jax.random.normal(k_u, (N_EXPERTS, HIDDEN, INTER), dtype=jnp.float32) * s_in, 'w_down': jax.random.normal(k_d, (N_EXPERTS, INTER, HIDDEN), dtype=jnp.float32) * s_mid}
    _L2_ffn_all = _L2_ffn_setup()
    _L2_ffn_in = {k: v for k, v in _L2_ffn_all.items() if k in ('w_router', 'w_gate', 'w_up', 'w_down')}
    del _L2_ffn_all

    def _L3_xattn_setup():
        import jax, jax.numpy as jnp
        import numpy as np
        import math
        CHANNELS = 128
        N_HEADS = 16
        K_CHANNELS = CHANNELS // N_HEADS
        ROPE_D = int(K_CHANNELS * 0.5)
        B, T = (4, 256)

        def apply_rope(x, d, base=10000.0):
            t = x.shape[2]
            theta = 1.0 / base ** (jnp.arange(0, d, 2, dtype=jnp.float32) / d)
            idx_theta = jnp.arange(t, dtype=jnp.float32)[:, None] * theta[None, :]
            idx_theta2 = jnp.concatenate([idx_theta, idx_theta], axis=-1)
            cos = jnp.cos(idx_theta2)[None, None, :, :]
            sin = jnp.sin(idx_theta2)[None, None, :, :]
            x_rope, x_pass = (x[..., :d], x[..., d:])
            d2 = d // 2
            neg_half = jnp.concatenate([-x_rope[..., d2:], x_rope[..., :d2]], axis=-1)
            x_rope = x_rope * cos + neg_half * sin
            return jnp.concatenate([x_rope, x_pass], axis=-1)
        key = jax.random.key(seed)
        ks = jax.random.split(key, 12)
        xavier = math.sqrt(6.0 / (CHANNELS + CHANNELS))
        inp = {'x': jax.random.normal(ks[0], (B, CHANNELS, T), dtype=jnp.float32), 'c': jax.random.normal(ks[1], (B, CHANNELS, T), dtype=jnp.float32), 'attn_mask': jnp.ones((1, 1, T, T), dtype=jnp.int32), 'wq': jax.random.uniform(ks[2], (CHANNELS, CHANNELS), jnp.float32, -xavier, xavier), 'bq': jnp.zeros((CHANNELS,), jnp.float32), 'wk': jax.random.uniform(ks[3], (CHANNELS, CHANNELS), jnp.float32, -xavier, xavier), 'bk': jnp.zeros((CHANNELS,), jnp.float32), 'wv': jax.random.uniform(ks[4], (CHANNELS, CHANNELS), jnp.float32, -xavier, xavier), 'bv': jnp.zeros((CHANNELS,), jnp.float32), 'wo': jax.random.normal(ks[5], (CHANNELS, CHANNELS), jnp.float32) * (1.0 / math.sqrt(CHANNELS)), 'bo': jnp.zeros((CHANNELS,), jnp.float32)}
        return inp
    _L3_xattn_all = _L3_xattn_setup()
    _L3_xattn_in = {k: v for k, v in _L3_xattn_all.items() if k in ('wq', 'bq', 'wk', 'bk', 'wv', 'bv', 'wo', 'bo')}
    del _L3_xattn_all

    def _L3_ffn_setup():
        import jax, jax.numpy as jnp
        import numpy as np
        B, S, H, E, I, TOPK = (1, 128, 256, 16, 128, 2)
        SCALE = 1.0
        key = jax.random.key(seed)
        k0, k1, k2, k3 = jax.random.split(key, 4)
        hidden_states = jax.random.normal(k0, (B, S, H), dtype=jnp.float32)
        gate_w = jax.random.normal(k1, (E, H), dtype=jnp.float32) * 0.02
        gate_up_proj = jax.random.normal(k2, (E, H, 2 * I), dtype=jnp.float32) / np.sqrt(H)
        down_proj = jax.random.normal(k3, (E, I, H), dtype=jnp.float32) / np.sqrt(I)
        return {'hidden_states': hidden_states, 'gate_w': gate_w, 'gate_up_proj': gate_up_proj, 'down_proj': down_proj}
    _L3_ffn_all = _L3_ffn_setup()
    _L3_ffn_in = {k: v for k, v in _L3_ffn_all.items() if k in ('gate_w', 'gate_up_proj', 'down_proj')}
    del _L3_ffn_all
    return {'x': x, 'ctx_2048': ctx_2048, 'mask_BxS2_bk0': mask_BxS2_bk0, 'mask_1x1x2048x2048_if1': mask_1x1x2048x2048_if1, 'L0_xattn_time_decay': _L0_xattn_in['time_decay'], 'L0_xattn_time_first': _L0_xattn_in['time_first'], 'L0_ffn_w1': _L0_ffn_in['w1'], 'L0_ffn_b1': _L0_ffn_in['b1'], 'L0_ffn_w2': _L0_ffn_in['w2'], 'L0_ffn_b2': _L0_ffn_in['b2'], 'L1_ffn_w_gate': _L1_ffn_in['w_gate'], 'L1_ffn_w_up': _L1_ffn_in['w_up'], 'L1_ffn_w_down': _L1_ffn_in['w_down'], 'L1_ffn_up_reorder_index': _L1_ffn_in['up_reorder_index'], 'L1_ffn_down_reorder_index': _L1_ffn_in['down_reorder_index'], 'L2_ffn_w_router': _L2_ffn_in['w_router'], 'L2_ffn_w_gate': _L2_ffn_in['w_gate'], 'L2_ffn_w_up': _L2_ffn_in['w_up'], 'L2_ffn_w_down': _L2_ffn_in['w_down'], 'L3_xattn_wq': _L3_xattn_in['wq'], 'L3_xattn_bq': _L3_xattn_in['bq'], 'L3_xattn_wk': _L3_xattn_in['wk'], 'L3_xattn_bk': _L3_xattn_in['bk'], 'L3_xattn_wv': _L3_xattn_in['wv'], 'L3_xattn_bv': _L3_xattn_in['bv'], 'L3_xattn_wo': _L3_xattn_in['wo'], 'L3_xattn_bo': _L3_xattn_in['bo'], 'L3_ffn_gate_w': _L3_ffn_in['gate_w'], 'L3_ffn_gate_up_proj': _L3_ffn_in['gate_up_proj'], 'L3_ffn_down_proj': _L3_ffn_in['down_proj']}

def reference(x, ctx_2048, mask_BxS2_bk0, mask_1x1x2048x2048_if1, L0_xattn_time_decay, L0_xattn_time_first, L0_ffn_w1, L0_ffn_b1, L0_ffn_w2, L0_ffn_b2, L1_ffn_w_gate, L1_ffn_w_up, L1_ffn_w_down, L1_ffn_up_reorder_index, L1_ffn_down_reorder_index, L2_ffn_w_router, L2_ffn_w_gate, L2_ffn_w_up, L2_ffn_w_down, L3_xattn_wq, L3_xattn_bq, L3_xattn_wk, L3_xattn_bk, L3_xattn_wv, L3_xattn_bv, L3_xattn_wo, L3_xattn_bo, L3_ffn_gate_w, L3_ffn_gate_up_proj, L3_ffn_down_proj):
    import jax
    import jax.numpy as jnp

    def _L0_xattn_ref(batch_size, seq_len, embedding_dim, time_decay, time_first, k, v):
        import jax, jax.numpy as jnp
        import numpy as np

        def _wkv(time_decay, time_first, k, v):
            w = -jnp.exp(time_decay)
            u = time_first
            B, T, C = k.shape
            aa = jnp.zeros((B, C), dtype=k.dtype)
            bb = jnp.zeros((B, C), dtype=k.dtype)
            pp = jnp.full((B, C), -1e+38, dtype=k.dtype)

            def step(carry, kv_t):
                aa, bb, pp = carry
                kt, vt = kv_t
                ww = u + kt
                q = jnp.maximum(pp, ww)
                e1 = jnp.exp(pp - q)
                e2 = jnp.exp(ww - q)
                y_t = (e1 * aa + e2 * vt) / (e1 * bb + e2)
                ww2 = pp + w
                q2 = jnp.maximum(ww2, kt)
                e1b = jnp.exp(ww2 - q2)
                e2b = jnp.exp(kt - q2)
                new_carry = (e1b * aa + e2b * vt, e1b * bb + e2b, q2)
                return (new_carry, y_t)
            ks = jnp.transpose(k, (1, 0, 2))
            vs = jnp.transpose(v, (1, 0, 2))
            _, ys = jax.lax.scan(step, (aa, bb, pp), (ks, vs))
            return jnp.transpose(ys, (1, 0, 2))
        assert seq_len <= 128
        return _wkv(time_decay, time_first, k, v)

    def _L0_ffn_ref(x, w1, b1, w2, b2):
        import jax, jax.numpy as jnp
        import numpy as np
        EPS_LN = 1e-05
        EPS_ACT = 1e-05
        EPS_W = 1e-08

        def _layer_norm(x):
            mu = jnp.mean(x, axis=-1, keepdims=True)
            xc = x - mu
            var = jnp.mean(xc * xc, axis=-1, keepdims=True)
            return xc * jax.lax.rsqrt(var + EPS_LN)

        def _activation_quant(x):
            scale = 127.0 / jnp.clip(jnp.max(jnp.abs(x), axis=-1, keepdims=True), EPS_ACT)
            return jnp.clip(jnp.round(x * scale), -128, 127) / scale

        def _weight_quant(w):
            scale = jnp.clip(jnp.mean(jnp.abs(w)), EPS_W)
            return jnp.clip(jnp.round(w / scale), -1, 1) * scale

        def _bitlinear(x, w, b):
            xn = _layer_norm(x)
            xq = _activation_quant(xn)
            wq = _weight_quant(w)
            return jnp.einsum('bsd,fd->bsf', xq, wq) + b
        h = _bitlinear(x, w1, b1)
        h = jax.nn.gelu(h, approximate=False)
        return _bitlinear(h, w2, b2)

    def _L1_xattn_ref(q, k, v):
        import jax, jax.numpy as jnp
        import numpy as np
        N_HEAD = 8
        b, d, m = q.shape
        c = v.shape[1]
        h = N_HEAD
        qh = q.reshape(b * h, d // h, m)
        kh = k.reshape(b * h, d // h, -1)
        vh = v.reshape(b * h, c // h, -1)
        scale = 1.0 / jnp.sqrt(jnp.asarray(d // h, dtype=q.dtype))
        qk = jnp.einsum('bdm,bdn->bmn', qh, kh) * scale
        sm = jax.nn.softmax(qk, axis=-1)
        ret = jnp.einsum('bmn,bcn->bcm', sm, vh)
        return ret.reshape(b, c, m)

    def _L1_ffn_ref(x, w_gate, w_up, w_down, up_reorder_index, down_reorder_index):
        import jax, jax.numpy as jnp
        import numpy as np
        FP8_MAX = 448.0
        GLOBAL_DIV = 448.0 * 6.0

        def _fp8(x):
            return x.astype(jnp.float8_e4m3fn).astype(jnp.float32)

        def _reorder_quantize_x(x, idx):
            scale = jnp.max(jnp.abs(x)) / GLOBAL_DIV
            xr = (x / scale)[:, idx]
            scale_x = jnp.max(jnp.abs(xr), axis=1, keepdims=True) / FP8_MAX
            qx = _fp8(xr / scale_x)
            return (qx, scale_x, scale)

        def _qlinear(qx, scale_x, scale, W, idx, out_idx=None):
            Wr = W[:, idx]
            w_scale = jnp.max(jnp.abs(Wr), axis=1, keepdims=True) / FP8_MAX
            qw = _fp8(Wr / w_scale)
            y = qx * scale_x @ (qw * w_scale).T * scale
            if out_idx is not None:
                y = y[:, out_idx]
            return y
        B, S, H = x.shape
        xf = x.reshape(B * S, H)
        qx, sx, sc = _reorder_quantize_x(xf, up_reorder_index)
        g = _qlinear(qx, sx, sc, w_gate, up_reorder_index, out_idx=down_reorder_index)
        u = _qlinear(qx, sx, sc, w_up, up_reorder_index, out_idx=down_reorder_index)
        t = jax.nn.silu(g) * u
        qt, st, sct = _reorder_quantize_x(t, down_reorder_index)
        y = _qlinear(qt, st, sct, w_down, down_reorder_index)
        return y.reshape(B, S, H)

    def _L2_xattn_ref(hidden_states, memory_tokens, memory_mask):
        import jax, jax.numpy as jnp
        import numpy as np
        B, S, D = hidden_states.shape
        scale = 1.0 / jnp.sqrt(jnp.asarray(D, hidden_states.dtype))
        scores = jnp.einsum('bsd,bmd->bsm', hidden_states, memory_tokens) * scale
        neg_inf = jnp.asarray(-1e+30, scores.dtype)
        scores = jnp.where(memory_mask[:, None, :], scores, neg_inf)
        attn = jax.nn.softmax(scores, axis=-1)
        readout = jnp.einsum('bsm,bmd->bsd', attn, memory_tokens)
        valid_b = jnp.any(memory_mask, axis=-1)
        out = jnp.where(valid_b[:, None, None], readout, jnp.zeros_like(readout))
        return out

    def _L2_ffn_ref(x, w_router, w_gate, w_up, w_down):
        import jax, jax.numpy as jnp
        import numpy as np
        HIDDEN = 256
        INTER = 128
        N_EXPERTS = 64
        TOP_K = 8
        B, T = (1, 64)
        Bb, Tt, D = x.shape
        xf = x.reshape(-1, D)
        N = xf.shape[0]
        logits = xf @ w_router
        topk_scores, topk_idx = jax.lax.top_k(logits, TOP_K)
        topk_gates = jax.nn.softmax(topk_scores, axis=-1)
        combine = jnp.zeros((N, N_EXPERTS), dtype=xf.dtype)
        combine = combine.at[jnp.arange(N)[:, None], topk_idx].add(topk_gates)
        h = jnp.einsum('td,edi->tei', xf, w_gate)
        u = jnp.einsum('td,edi->tei', xf, w_up)
        a = jax.nn.silu(h) * u
        out = jnp.einsum('tei,eid,te->td', a, w_down, combine)
        return out.reshape(Bb, Tt, D)

    def _L3_xattn_ref(x, c, attn_mask, wq, bq, wk, bk, wv, bv, wo, bo):
        import jax, jax.numpy as jnp
        import numpy as np
        import math
        CHANNELS = 128
        N_HEADS = 16
        K_CHANNELS = CHANNELS // N_HEADS
        ROPE_D = int(K_CHANNELS * 0.5)
        B, T = (4, 256)

        def apply_rope(x, d, base=10000.0):
            t = x.shape[2]
            theta = 1.0 / base ** (jnp.arange(0, d, 2, dtype=jnp.float32) / d)
            idx_theta = jnp.arange(t, dtype=jnp.float32)[:, None] * theta[None, :]
            idx_theta2 = jnp.concatenate([idx_theta, idx_theta], axis=-1)
            cos = jnp.cos(idx_theta2)[None, None, :, :]
            sin = jnp.sin(idx_theta2)[None, None, :, :]
            x_rope, x_pass = (x[..., :d], x[..., d:])
            d2 = d // 2
            neg_half = jnp.concatenate([-x_rope[..., d2:], x_rope[..., :d2]], axis=-1)
            x_rope = x_rope * cos + neg_half * sin
            return jnp.concatenate([x_rope, x_pass], axis=-1)
        b, _, t_t = x.shape
        t_s = c.shape[2]
        q = jnp.einsum('oi,bit->bot', wq, x) + bq[None, :, None]
        k = jnp.einsum('oi,bit->bot', wk, c) + bk[None, :, None]
        v = jnp.einsum('oi,bit->bot', wv, c) + bv[None, :, None]

        def split_heads(z, t):
            return z.reshape(b, N_HEADS, K_CHANNELS, t).transpose(0, 1, 3, 2)
        q = split_heads(q, t_t)
        k = split_heads(k, t_s)
        v = split_heads(v, t_s)
        q = apply_rope(q, ROPE_D)
        k = apply_rope(k, ROPE_D)
        scores = jnp.einsum('bhqc,bhkc->bhqk', q, k) / math.sqrt(K_CHANNELS)
        scores = jnp.where(attn_mask == 0, jnp.float32(-10000.0), scores)
        p_attn = jax.nn.softmax(scores, axis=-1)
        out = jnp.einsum('bhqk,bhkc->bhqc', p_attn, v)
        out = out.transpose(0, 1, 3, 2).reshape(b, CHANNELS, t_t)
        out = jnp.einsum('oi,bit->bot', wo, out) + bo[None, :, None]
        return out

    def _L3_ffn_ref(hidden_states, gate_w, gate_up_proj, down_proj):
        import jax, jax.numpy as jnp
        import numpy as np
        B, S, H, E, I, TOPK = (1, 128, 256, 16, 128, 2)
        SCALE = 1.0
        b, s, h = hidden_states.shape
        e = gate_w.shape[0]
        x = hidden_states.reshape(-1, h)
        logits = jnp.matmul(x.astype(jnp.float32), gate_w.T.astype(jnp.float32))
        p = jax.nn.sigmoid(logits)
        p = p / jnp.sum(p, axis=-1, keepdims=True)
        w, idx = jax.lax.top_k(p, TOPK)
        w = w / jnp.sum(w, axis=-1, keepdims=True)
        w = w * SCALE
        combine = jnp.sum(jax.nn.one_hot(idx, e, dtype=w.dtype) * w[..., None], axis=1)
        gu = jnp.einsum('th,ehf->etf', x, gate_up_proj)
        gate, up = jnp.split(gu, 2, axis=-1)
        inter = jax.nn.silu(gate) * up
        y = jnp.einsum('eti,eih->eth', inter, down_proj)
        out = jnp.einsum('eth,te->th', y, combine.astype(y.dtype))
        return out.reshape(b, s, h)
    x = x + _L0_xattn_ref(8, 128, 256, L0_xattn_time_decay, L0_xattn_time_first, _layernorm(x, axis=-1), ctx_2048)
    x = x + _L0_ffn_ref(_layernorm(x, axis=-1), L0_ffn_w1, L0_ffn_b1, L0_ffn_w2, L0_ffn_b2)
    x = x + _L1_xattn_ref(_layernorm(x, axis=-1), ctx_2048, ctx_2048)
    x = x + _L1_ffn_ref(_layernorm(x, axis=-1), L1_ffn_w_gate, L1_ffn_w_up, L1_ffn_w_down, L1_ffn_up_reorder_index, L1_ffn_down_reorder_index)
    x = x + _L2_xattn_ref(_layernorm(x, axis=-1), ctx_2048, mask_BxS2_bk0)
    x = x + _L2_ffn_ref(_layernorm(x, axis=-1), L2_ffn_w_router, L2_ffn_w_gate, L2_ffn_w_up, L2_ffn_w_down)
    x = x + _L3_xattn_ref(_layernorm(x, axis=-1), ctx_2048, mask_1x1x2048x2048_if1, L3_xattn_wq, L3_xattn_bq, L3_xattn_wk, L3_xattn_bk, L3_xattn_wv, L3_xattn_bv, L3_xattn_wo, L3_xattn_bo)
    x = x + _L3_ffn_ref(_layernorm(x, axis=-1), L3_ffn_gate_w, L3_ffn_gate_up_proj, L3_ffn_down_proj)
    return x

_drawn_inputs = setup_inputs


def setup_inputs(seed=0):
    import zlib

    import numpy as np

    out = dict(_drawn_inputs(seed))
    spreads = {'L3_xattn_bq': (0.0, 0.338),
     'L3_xattn_bk': (0.0, 0.726),
     'L3_xattn_bv': (0.0, 0.1),
     'L3_xattn_bo': (0.0, 0.1)}
    factors = {}
    for name, (base, spread) in spreads.items():
        noise = np.random.default_rng([zlib.crc32(name.encode()), seed]).standard_normal(out[name].shape)
        drawn = base * np.exp(spread * noise) if base else spread * noise
        out[name] = jnp.asarray(drawn.astype(out[name].dtype))
    for name, factor in factors.items():
        out[name] = (out[name] * factor).astype(out[name].dtype)
    return out
```

```python
from contextlib import ExitStack
from functools import partial

import numpy as np
import concourse.bass as bass
from concourse import mybir

F32 = mybir.dt.float32
F32R = mybir.dt.float32r
BF16 = mybir.dt.bfloat16
I32 = mybir.dt.int32
U8 = mybir.dt.uint8
ALU = mybir.AluOpType
ACT = mybir.ActivationFunctionType
AXX = mybir.AxisListType.X

P = 128
B, T, D = 8, 128, 256
DC = D // P
EPS = 1e-5
ROUND = 1.5 * 2.0 ** 23
LOWEST = -1e38
FF = 1024
FC = FF // P


class Chain:

    def __init__(self, engine, semaphore, start=0):
        self.engine, self.semaphore, self.value = engine, semaphore, start

    def step(self, instruction):
        instruction.then_inc(self.semaphore, 1)
        self.value = self.value + 1
        return self

    def wait(self):
        self.engine.wait_ge(self.semaphore, self.value)


def layer_norm_rows(dve, chain, core, b):
    chain.step(dve.bn_stats(core.bn[:, b, :], core.x_sb[:, b, :]))
    chain.wait()
    dve.bn_aggr(core.mean_var[:, b, :], core.bn[:, b, :]).then_inc(core.x_stats, 1)


def rstd_row(pool, chain, core, layer, b, scale=1.0, shift=EPS):
    pool.wait_ge(core.x_stats, layer * B + b + 1)
    chain.step(pool.tensor_scalar(core.var_eps[:, b, :], core.mean_var[:, b, 1:2], scale, shift, ALU.mult, ALU.add))
    chain.wait()
    pool.tensor_tensor(core.rstd[:, b, :], core.var_eps[:, b, :], core.minus_half[:, 0:1], ALU.pow)\
        .then_inc(core.rstd_ready, 1)


def wkv_layer(nc, core, layer, ins, sb, sem):
    TP = T + 1
    k_pad = sb("wkv_k", [P, DC, B, TP], F32)
    decay = sb("wkv_decay", [P, DC, B, TP], F32)
    peak = sb("wkv_peak", [P, DC, B, TP], F32)
    e_old = sb("wkv_e_old", [P, B, TP], F32)
    e_new = sb("wkv_e_new", [P, B, TP], F32)
    ev_new = sb("wkv_ev_new", [P, B, TP], F32)
    aa = sb("wkv_aa", [P, B, TP], F32)
    bb = sb("wkv_bb", [P, B, TP], F32)
    d_old = sb("wkv_d_old", [P, B, T], F32)
    d_new = sb("wkv_d_new", [P, B, T], F32)
    q_max = sb("wkv_q_max", [P, B, T], F32)
    o_old = sb("wkv_o_old", [P, B, T], F32)
    o_bb = sb("wkv_o_bb", [P, B, T], F32)
    o_new = sb("wkv_o_new", [P, B, T], F32)
    ov_new = sb("wkv_ov_new", [P, B, T], F32)
    recip = sb("wkv_recip", [P, B, T], F32)
    y_t = sb("wkv_y", [P, DC, B, T], F32)
    xn = sb("wkv_xn", [P, B, D], F32)
    td_tf = sb("wkv_td_tf", [P, 2, DC], F32)
    w_exp = sb("wkv_w_exp", [P, DC], F32)

    td_loaded, dve_step, act_step, pool_step = sem("wkv_td_loaded"), sem("wkv_dve"), sem("wkv_act"), sem("wkv_pool")
    xn_ready, xn_turned, k_ready = sem("wkv_xn_ready"), sem("wkv_xn_turned"), sem("wkv_k_ready")
    w_ready, decay_ready = sem("wkv_w_ready"), sem("wkv_decay_ready")
    diff_ready, exp_ready, new_v_ready = sem("wkv_diff_ready"), sem("wkv_exp_ready"), sem("wkv_new_v_ready")
    y_ready, y_turned, chunk_done = sem("wkv_y_ready"), sem("wkv_y_turned"), sem("wkv_chunk_done")

    def turned(c):
        return core.psum[:, 2 * c:2 * c + 2, :].rearrange("p n (b t) -> p (n b) t", t=T)

    def y_rows(b):
        return core.psum[:, 4 + b // 2, (b % 2) * D:(b % 2 + 1) * D]

    def sync(sp):
        sp.dma_start(td_tf[:, 0, :], ins["td"]).then_inc(td_loaded, 16)
        sp.dma_start(td_tf[:, 1, :], ins["tf"]).then_inc(td_loaded, 16)

    def gpsimd(pool):
        ch = Chain(pool, pool_step)
        ch.step(pool.memset(decay[:, :, :, :], 0.0))
        ch.step(pool.memset(k_pad[:, :, :, 0:1], LOWEST))
        ch.step(pool.memset(e_old[:, :, 0:1], 0.0))
        ch.step(pool.memset(e_new[:, :, 0:1], 0.0))
        for b in range(B):
            rstd_row(pool, ch, core, layer, b)
        pool.wait_ge(w_ready, 1)
        for c in range(DC):
            ch.step(pool.tensor_scalar(decay[:, c], decay[:, c], w_exp[:, c:c + 1], None, ALU.add))
        ch.wait()
        pool.memset(decay[:, :, :, 0:1], 2 * LOWEST).then_inc(decay_ready, 1)
        pool.wait_ge(core.ctx_t_loaded, 16)
        for c in range(DC):
            v = core.ctx_t[:, c, :, :]
            pool.wait_ge(exp_ready, 4 * c + 2)
            if c:
                pool.wait_ge(dve_step, core.wkv_scanned_aa)
            ch.step(pool.tensor_tensor(ev_new[:, :, 1:TP], e_new[:, :, 1:TP], v, ALU.mult))
            pool.memset(ev_new[:, :, 0:1], 0.0).then_inc(new_v_ready, 1)
            pool.wait_ge(exp_ready, 4 * c + 4)
            pool.tensor_tensor(ov_new[:, :, :], o_new[:, :, :], v, ALU.mult).then_inc(new_v_ready, 1)

    def vector(dve):
        ch = Chain(dve, dve_step)
        for b in range(B):
            dve.wait_ge(core.rstd_ready, layer * B + b + 1)
            dve.tensor_scalar(xn[:, b, :], core.x_sb[:, b, :], core.mean_var[:, b, 0:1], core.rstd[:, b, :],
                              ALU.subtract, ALU.mult).then_inc(xn_ready, 1)
        dve.wait_ge(k_ready, 0 + 4)
        dve.tensor_scalar(w_exp[:, :], w_exp[:, :], -1.0, None, ALU.mult).then_inc(w_ready, 1)
        dve.wait_ge(decay_ready, 1)
        dve.wait_ge(td_loaded, 32)
        for c in range(DC):
            u, w = td_tf[:, 1, c:c + 1], w_exp[:, c:c + 1]
            k, pp, pp_next = k_pad[:, c, :, 1:TP], peak[:, c, :, 0:T], peak[:, c, :, 1:TP]
            ch.step(dve.tensor_tensor_scan(peak[:, c].rearrange("p b t -> p (b t)"), decay[:, c].rearrange("p b t -> p (b t)"),
                                           k_pad[:, c].rearrange("p b t -> p (b t)"), LOWEST, ALU.add, ALU.max))
            ch.wait()
            if c:
                dve.wait_ge(exp_ready, 4 * c)
            dve.scalar_tensor_tensor(d_old[:, :, :], pp, w, pp_next, ALU.add, ALU.subtract).then_inc(diff_ready, 1)
            dve.tensor_tensor(d_new[:, :, :], k, pp_next, ALU.subtract).then_inc(diff_ready, 1)
            ch.step(dve.scalar_tensor_tensor(q_max[:, :, :], k, u, pp, ALU.add, ALU.max))
            ch.wait()
            dve.wait_ge(exp_ready, 4 * c + 2)
            dve.tensor_tensor(d_old[:, :, :], pp, q_max[:, :, :], ALU.subtract).then_inc(diff_ready, 1)
            dve.scalar_tensor_tensor(d_new[:, :, :], k, u, q_max[:, :, :], ALU.add, ALU.subtract).then_inc(diff_ready, 1)
            ch.step(dve.tensor_tensor_scan(bb[:].rearrange("p b t -> p (b t)"), e_old[:].rearrange("p b t -> p (b t)"),
                                           e_new[:].rearrange("p b t -> p (b t)"), 0.0, ALU.mult, ALU.add))
            ch.wait()
            dve.wait_ge(exp_ready, 4 * c + 4)
            ch.step(dve.tensor_tensor(o_bb[:, :, :], o_old[:, :, :], bb[:, :, 0:T], ALU.mult))
            ch.wait()
            ch.step(dve.tensor_tensor(o_bb[:, :, :], o_bb[:, :, :], o_new[:, :, :], ALU.add))
            ch.wait()
            ch.step(dve.reciprocal(recip[:, :, :], o_bb[:, :, :]))
            dve.wait_ge(new_v_ready, 2 * c + 1)
            ch.step(dve.tensor_tensor_scan(aa[:].rearrange("p b t -> p (b t)"), e_old[:].rearrange("p b t -> p (b t)"),
                                           ev_new[:].rearrange("p b t -> p (b t)"), 0.0, ALU.mult, ALU.add))
            ch.wait()
            if c == 0:
                core.wkv_scanned_aa = ch.value
            ch.step(dve.tensor_tensor(o_old[:, :, :], o_old[:, :, :], aa[:, :, 0:T], ALU.mult))
            ch.wait()
            dve.wait_ge(new_v_ready, 2 * c + 2)
            ch.step(dve.tensor_tensor(o_old[:, :, :], o_old[:, :, :], ov_new[:, :, :], ALU.add))
            ch.wait()
            dve.tensor_tensor(y_t[:, c], o_old[:, :, :], recip[:, :, :], ALU.mult).then_inc(y_ready, 1)
        for b in range(B):
            if b % 2 == 0:
                dve.wait_ge(y_turned, b // 2 + 1)
            ch.step(dve.tensor_tensor(core.x_sb[:, b, :], core.x_sb[:, b, :], y_rows(b), ALU.add))
            ch.wait()
            layer_norm_rows(dve, ch, core, b)

    def scalar(act):
        act.wait_ge(td_loaded, 32)
        act.activation(w_exp[:, :], td_tf[:, 0, :], ACT.Exp).then_inc(act_step, 1)
        act.wait_ge(pool_step, 2)
        for half in range(2):
            act.wait_ge(xn_turned, half + 1)
            for c in range(DC):
                act.activation(k_pad[:, c, 4 * half:4 * half + 4, 1:TP], turned(c)[:, 4 * half:4 * half + 4, :],
                               ACT.Copy).then_inc(k_ready, 1)
        for c in range(DC):
            if c:
                act.wait_ge(y_ready, c)
            act.wait_ge(diff_ready, 4 * c + 1)
            act.activation(e_old[:, :, 1:TP], d_old[:, :, :], ACT.Exp).then_inc(exp_ready, 1)
            act.wait_ge(diff_ready, 4 * c + 2)
            act.activation(e_new[:, :, 1:TP], d_new[:, :, :], ACT.Exp).then_inc(exp_ready, 1)
            act.wait_ge(diff_ready, 4 * c + 3)
            act.activation(o_old[:, :, :], d_old[:, :, :], ACT.Exp).then_inc(exp_ready, 1)
            act.wait_ge(diff_ready, 4 * c + 4)
            act.activation(o_new[:, :, :], d_new[:, :, :], ACT.Exp).then_inc(exp_ready, 1)

    def tensor(pe):
        pe.wait_ge(core.const_loaded, 16)
        for b in range(B):
            pe.wait_ge(xn_ready, b + 1)
            for c in range(DC):
                last = pe.transpose(turned(c)[:, b, :], xn[:, b, c * P:(c + 1) * P], core.ident[:, :])
            if b % 4 == 3:
                last.then_inc(xn_turned, 1)
        pe.wait_ge(y_ready, DC)
        for b in range(B):
            for c in range(DC):
                last = pe.transpose(y_rows(b)[:, c * P:(c + 1) * P], y_t[:, c, b, :], core.ident[:, :])
            if b % 2:
                last.then_inc(y_turned, 1)

    return dict(sync=sync, gpsimd=gpsimd, vector=vector, scalar=scalar, tensor=tensor)


def ternary_ffn_layer(nc, core, layer, ins, sb, sem):
    w1 = sb("w1", [P, DC, FF], F32)
    w2 = sb("w2", [P, FC, D], F32)
    w1_q = sb("w1_q", [P, DC, FF], BF16)
    w2_q = sb("w2_q", [P, FC, D], BF16)
    b1 = sb("b1_rows", [P, FF], F32)
    b2 = sb("b2_rows", [P, D], F32)
    w_sums = sb("w_sums", [P, 2], F32)
    w_scale = sb("w_scale", [P, 2], F32)
    w_inv = sb("w_inv", [P, 2], F32)
    xc = sb("bf_xc", [P, 2, D], F32)
    xq = sb("bf_xq", [P, 2, D], BF16)
    xq_t = sb("bf_xq_t", [P, 2, DC, P], BF16)
    stat = sb("bf_stat", [P, 2, 8], F32)
    stat2 = sb("bf_stat2", [P, 2, 8], F32)
    back1 = sb("bf_back1", [P, 2, 1], F32)
    back2 = sb("bf_back2", [P, 2, 1], F32)
    h = sb("bf_h", [P, 2, FF], F32)
    g = sb("bf_g", [P, 2, FF], F32)
    gc = sb("bf_gc", [P, 2, FF], F32)
    a_t = sb("bf_a_t", [P, 2, FC, P], BF16)
    bn2 = sb("bf_bn2", [P, 2, 2, 6], F32)
    mv2 = sb("bf_mv2", [P, 2, 2], F32)
    ve2 = sb("bf_ve2", [P, 2, 1], F32)
    r2 = sb("bf_r2", [P, 2, 1], F32)
    neg_mean = sb("bf_neg_mean", [P, 2, 1], F32)
    out_rows = sb("bf_out", [P, 2, D], F32)
    neg_round = sb("bf_neg_round", [P, 1], F32)

    loaded = [sem(f"bf_loaded{i}") for i in range(4)]
    dve_step, pool_step, sums_ready, totals_ready, inv_ready = (
        sem("bf_dve"), sem("bf_pool"), sem("bf_sums"), sem("bf_totals"), sem("bf_inv"))
    w_ready = sem("bf_w_ready")
    xq_ready, xq_turned, xq_t_ready, h_done = sem("bf_xq_ready"), sem("bf_xq_turned"), sem("bf_xq_t_ready"), sem("bf_h_done")
    h_ready, g_ready, mv_ready, r2_ready, mean_ready, gc_ready = (
        sem("bf_h_ready"), sem("bf_g_ready"), sem("bf_mv_ready"), sem("bf_r2_ready"), sem("bf_mean_ready"), sem("bf_gc_ready"))
    aq_ready, a_turned, a_t_ready, y_done = sem("bf_aq_ready"), sem("bf_a_turned"), sem("bf_a_t_ready"), sem("bf_y_done")

    def h_ps(j):
        return core.psum[:, 2 * j:2 * j + 2, :].rearrange("p n f -> p (n f)")

    a_ps = core.psum[:, 4:6, :].rearrange("p n (k t) -> p (n k) t", t=P)
    xq_ps = core.psum[:, 6, :].bitcast(BF16)
    y_ps = core.psum[:, 7, 0:D]
    tot_ps = core.psum[:, 7, 256:258]

    def sync(sp):
        if layer:
            sp.wait_ge(core.x_stats, (layer + 1) * B)
        sp.dma_start(w1[:], ins["w1_t"]).then_inc(loaded[0], 16)
        sp.dma_start(w2[:], ins["w2_t"]).then_inc(loaded[1], 16)
        sp.dma_start(b1[:, :], ins["b1"].to_broadcast([P, FF])).then_inc(loaded[2], 16)
        sp.dma_start(b2[:, :], ins["b2"].to_broadcast([P, D])).then_inc(loaded[3], 16)

    def gpsimd(pool):
        ch = Chain(pool, pool_step)
        for b in range(B):
            rstd_row(pool, ch, core, layer, b, 1.0 + EPS, EPS * EPS)
        for b in range(B):
            j = b % 2
            pool.wait_ge(mv_ready, b + 1)
            ch.step(pool.tensor_scalar(ve2[:, j, :], mv2[:, j, 1:2], EPS, None, ALU.add))
            ch.wait()
            pool.tensor_tensor(r2[:, j, :], ve2[:, j, :], core.minus_half[:, 0:1], ALU.pow).then_inc(r2_ready, 1)

    def scales(dve, ch, st, absmax, rstd, back, w_scale_col):
        ch.step(dve.tensor_scalar(st[:, 1:2], absmax, rstd, 1e-5, ALU.mult, ALU.max))
        ch.wait()
        ch.step(dve.reciprocal(st[:, 3:4], st[:, 1:2]))
        ch.step(dve.tensor_scalar(back, st[:, 1:2], w_scale_col, 1.0 / 127.0, ALU.mult, ALU.mult))
        ch.wait()
        ch.step(dve.tensor_scalar(st[:, 2:3], st[:, 3:4], rstd, 127.0, ALU.mult, ALU.mult))
        ch.wait()

    def vector(dve):
        ch = Chain(dve, dve_step)
        dve.wait_ge(core.x_stats, (layer + 1) * B)
        dve.wait_ge(core.rstd_ready, layer * B + 1)
        for i, w in enumerate((w1, w2)):
            dve.wait_ge(loaded[i], 16)
            ch.step(dve.tensor_reduce(w_sums[:, i:i + 1], w[:].rearrange("p a b -> p (a b)"), AXX, ALU.add,
                                      apply_absolute_value=True))
        ch.step(dve.memset(neg_round[:, :], -ROUND))
        ch.wait()
        dve.sem_inc(sums_ready, 1)
        dve.wait_ge(totals_ready, 1)
        ch.step(dve.tensor_scalar(w_scale[:, :], tot_ps, 1.0 / (FF * D), 1e-8, ALU.mult, ALU.max))
        ch.wait()
        ch.step(dve.reciprocal(w_inv[:, :], w_scale[:, :]))
        ch.wait()
        for i, (w, q) in enumerate(((w1, w1_q), (w2, w2_q))):
            w, q = w[:].rearrange("p a b -> p (a b)"), q[:].rearrange("p a b -> p (a b)")
            ch.step(dve.tensor_scalar(w, w, w_inv[:, i:i + 1], 1.0, ALU.mult, ALU.min))
            ch.wait()
            ch.step(dve.tensor_scalar(w, w, -1.0, ROUND, ALU.max, ALU.add))
            ch.wait()
            dve.tensor_scalar(q, w, ROUND, None, ALU.subtract).then_inc(w_ready, 1)

        def quantize_x(b):
            j = b % 2
            dve.wait_ge(core.rstd_ready, layer * B + b + 1)
            ch.step(dve.tensor_scalar(xc[:, j, :], core.x_sb[:, b, :], core.mean_var[:, b, 0:1], None, ALU.subtract))
            ch.wait()
            ch.step(dve.tensor_reduce(stat[:, j, 0:1], xc[:, j, :], AXX, ALU.max, apply_absolute_value=True))
            ch.wait()
            scales(dve, ch, stat[:, j, :], stat[:, j, 0:1], core.rstd[:, b, :], back1[:, j, :], w_scale[:, 0:1])
            ch.step(dve.tensor_scalar(xc[:, j, :], xc[:, j, :], stat[:, j, 2:3], ROUND, ALU.mult, ALU.add))
            ch.wait()
            if b >= 2:
                dve.wait_ge(xq_turned, b - 1)
            dve.tensor_scalar(xq[:, j, :], xc[:, j, :], ROUND, None, ALU.subtract).then_inc(xq_ready, 1)

        def add_bias(b):
            j = b % 2
            dve.wait_ge(h_done, b + 1)
            if b >= 2:
                dve.wait_ge(g_ready, b - 1)
            dve.scalar_tensor_tensor(h[:, j, :], h_ps(j), back1[:, j, :], b1[:, :], ALU.mult, ALU.add).then_inc(h_ready, 1)

        def quantize_inner(b):
            j = b % 2
            dve.wait_ge(g_ready, b + 1)
            for n in range(2):
                ch.step(dve.bn_stats(bn2[:, j, n, :], g[:, j, n * 512:(n + 1) * 512]))
            ch.wait()
            if b >= 2:
                dve.wait_ge(gc_ready, b - 1)
            dve.bn_aggr(mv2[:, j, :], bn2[:, j].rearrange("p a b -> p (a b)")).then_inc(mv_ready, 1)
            dve.wait_ge(mv_ready, b + 1)
            dve.tensor_scalar(neg_mean[:, j, :], mv2[:, j, 0:1], -1.0, None, ALU.mult).then_inc(mean_ready, 1)
            if b:
                add_to_x(b - 1)
            dve.wait_ge(gc_ready, b + 1)
            ch.step(dve.tensor_reduce(stat2[:, j, 0:1], gc[:, j, :], AXX, ALU.max, apply_absolute_value=True))
            ch.wait()
            dve.wait_ge(r2_ready, b + 1)
            scales(dve, ch, stat2[:, j, :], stat2[:, j, 0:1], r2[:, j, :], back2[:, j, :], w_scale[:, 1:2])
            dve.tensor_scalar(gc[:, j, :], gc[:, j, :], stat2[:, j, 2:3], ROUND, ALU.mult, ALU.add).then_inc(aq_ready, 1)

        def add_to_x(b):
            j = b % 2
            dve.wait_ge(y_done, b + 1)
            ch.step(dve.scalar_tensor_tensor(out_rows[:, j, :], y_ps, back2[:, j, :], b2[:, :], ALU.mult, ALU.add))
            ch.wait()
            ch.step(dve.tensor_tensor(core.x_sb[:, b, :], core.x_sb[:, b, :], out_rows[:, j, :], ALU.add))
            ch.wait()
            layer_norm_rows(dve, ch, core, b)

        dve.wait_ge(loaded[2], 16)
        dve.wait_ge(loaded[3], 16)
        quantize_x(0)
        quantize_x(1)
        add_bias(0)
        for b in range(B):
            if b + 1 < B:
                add_bias(b + 1)
            if b + 2 < B:
                quantize_x(b + 2)
            quantize_inner(b)
        add_to_x(B - 1)

    def scalar(act):
        def turned_x(b):
            act.wait_ge(xq_turned, b + 1)
            if b >= 2:
                act.wait_ge(h_done, b - 1)
            act.activation(xq_t[:, b % 2].rearrange("p a b -> p (a b)"), xq_ps[:, 0:D], ACT.Copy).then_inc(xq_t_ready, 1)

        def gelu(b):
            j = b % 2
            act.wait_ge(h_ready, b + 1)
            if b >= 2:
                act.wait_ge(gc_ready, b - 1)
            act.activation(g[:, j, :], h[:, j, :], ACT.Gelu).then_inc(g_ready, 1)

        def center(b):
            j = b % 2
            act.wait_ge(mean_ready, b + 1)
            if b >= 2:
                act.wait_ge(a_turned, b - 1)
            act.activation(gc[:, j, :], g[:, j, :], ACT.Identity, bias=neg_mean[:, j, :]).then_inc(gc_ready, 1)

        def turned_inner(b):
            act.wait_ge(a_turned, b + 1)
            if b >= 2:
                act.wait_ge(y_done, b - 1)
            act.activation(a_t[:, b % 2].rearrange("p a b -> p (a b)"), a_ps.rearrange("p a b -> p (a b)"),
                           ACT.Identity, bias=neg_round[:, 0:1]).then_inc(a_t_ready, 1)

        act.wait_ge(sums_ready, 1)
        turned_x(0)
        turned_x(1)
        gelu(0)
        for b in range(B):
            if b + 2 < B:
                turned_x(b + 2)
            center(b)
            if b + 1 < B:
                gelu(b + 1)
            turned_inner(b)

    def tensor(pe):
        def turn_x(b):
            pe.wait_ge(xq_ready, b + 1)
            if b:
                pe.wait_ge(xq_t_ready, b)
            for c in range(DC):
                last = pe.transpose(xq_ps[:, c * P:(c + 1) * P], xq[:, b % 2, c * P:(c + 1) * P], core.ident_bf[:, :])
            last.then_inc(xq_turned, 1)

        def product1(b):
            j = b % 2
            pe.wait_ge(xq_t_ready, b + 1)
            if b >= 2:
                pe.wait_ge(h_ready, b - 1)
            for n in range(2):
                for c in range(DC):
                    last = pe.matmul(h_ps(j)[:, n * 512:(n + 1) * 512], xq_t[:, j, c, :], w1_q[:, c, n * 512:(n + 1) * 512],
                                     start=(c == 0), stop=(c == DC - 1))
            last.then_inc(h_done, 1)

        def turn_inner(b):
            pe.wait_ge(aq_ready, b + 1)
            if b:
                pe.wait_ge(a_t_ready, b)
            for k in range(FC):
                last = pe.transpose(a_ps[:, k, :], gc[:, b % 2, k * P:(k + 1) * P], core.ident[:, :])
            last.then_inc(a_turned, 1)

        def product2(b):
            pe.wait_ge(a_t_ready, b + 1)
            if b:
                pe.wait_ge(core.x_stats, (layer + 1) * B + b)
            for k in range(FC):
                last = pe.matmul(y_ps, a_t[:, b % 2, k, :], w2_q[:, k, :], start=(k == 0), stop=(k == FC - 1))
            last.then_inc(y_done, 1)

        pe.wait_ge(sums_ready, 1)
        pe.matmul(tot_ps, core.ones[:, :], w_sums[:, :], start=True, stop=True).then_inc(totals_ready, 1)
        pe.wait_ge(core.ident_bf_ready, 1)
        turn_x(0)
        pe.wait_ge(w_ready, 2)
        product1(0)
        turn_x(1)
        product1(1)
        for b in range(B):
            if b + 2 < B:
                turn_x(b + 2)
                product1(b + 2)
            turn_inner(b)
            product2(b)

    return dict(sync=sync, gpsimd=gpsimd, vector=vector, scalar=scalar, tensor=tensor)


Q_PIECE = (0, 1, 2, 0, 1, 0)
K_PIECE = (0, 0, 0, 1, 1, 2)
SLOTS = len(Q_PIECE)
SLOT_RUNS = ((0, 3), (3, 2), (5, 1))
RING = 3
HB = 4


def split_in_three(dve, ch, full, rest, pieces):
    ch.step(dve.tensor_copy(pieces[0], full))
    ch.wait()
    ch.step(dve.tensor_tensor(rest, full, pieces[0], ALU.subtract))
    ch.wait()
    ch.step(dve.tensor_copy(pieces[1], rest))
    ch.wait()
    ch.step(dve.tensor_tensor(pieces[2], rest, pieces[1], ALU.subtract))


class HeadAttention:

    def __init__(self, nc, core, sb, sem, name, heads, scale, q3, k3, v_t, mask=None):
        self.core, self.H, self.scale, self.v_t, self.mask = core, heads, scale, v_t, mask
        self.out_read = None
        self.DH = DH = P // heads
        self.q3, self.k3 = q3, k3
        self.K = K = SLOTS * DH
        self.NB = heads // HB
        self.LEAD, self.TURN_AT = 4, 2 * self.NB - 2
        self.q_dram = nc.dram_tensor(f"{name}_q_pieces", [B, 3, DH, heads, D], BF16, kind="Internal").ap()
        self.k_dram = nc.dram_tensor(f"{name}_k_pieces", [B, 3, DH, heads, D], BF16, kind="Internal").ap()
        self.qs = sb(f"{name}_qs", [K + 3, RING, heads, D], BF16)
        self.ks = sb(f"{name}_ks", [K + 3, RING, heads, D], BF16)
        self.v_ones = sb(f"{name}_v_ones", [P, 2, DC, heads, 32], F32)
        self.peak = sb(f"{name}_peak", [P, 2, heads, DC], F32)
        self.peak_rest = sb(f"{name}_peak_rest", [P, heads, DC], F32)
        self.peak3 = sb(f"{name}_peak3", [P, 3, heads, DC], BF16)
        self.peak_rows = sb(f"{name}_peak_rows", [3 * heads * DC, 2, P], BF16)
        self.pt = sb(f"{name}_pt", [P, 2, HB, D], F32)
        self.o_sb = sb(f"{name}_o", [P, self.NB, D], F32)
        self.o_hi = sb(f"{name}_o_hi", [P, 2, self.NB, D], F32R)
        self.o_lo = sb(f"{name}_o_lo", [P, 2, self.NB, D], F32R)
        self.recip = sb(f"{name}_recip", [P, D], F32)
        self.o_norm = sb(f"{name}_o_norm", [P, 2, D], F32)
        s = lambda n: sem(f"{name}_{n}")
        self.pieces_stored = [s(f"pieces_stored{i}") for i in range(2)]
        self.stacks_loaded = [s(f"stacks_loaded{i}") for i in range(RING)]
        self.peak_loaded = [s(f"peak_loaded{i}") for i in range(RING)]
        self.v_ones_ready = s("v_ones_ready")
        self.pieces_ready, self.ones_ready, self.v_ready = s("pieces_ready"), s("ones_ready"), s("v_ready")
        self.s_done, self.max_done, self.peak3_ready = s("s_done"), s("max_done"), s("peak3_ready")
        self.peak_turned, self.peak_rows_ready = s("peak_turned"), s("peak_rows_ready")
        self.st_done, self.exp_done, self.pv_done, self.o_ready = s("st_done"), s("exp_done"), s("pv_done"), s("o_ready")
        self.o_hi_ready, self.o_lo_ready = s("o_hi_ready"), s("o_lo_ready")
        self.parts_done, self.norm_ready, self.recip_ready = s("parts_done"), s("norm_ready"), s("recip_ready")

    def s_ps(self, n):
        return self.core.psum[:, n % 2, :].rearrange("p (h k) -> p h k", h=2)

    def st_ps(self, n):
        return self.core.psum[:, 2 + 2 * (n % 2):4 + 2 * (n % 2), :].rearrange("p a (h q) -> p (a h) q", h=2)

    def o_ps(self, g):
        return self.core.psum[:, 7, (g % 2) * D:(g % 2 + 1) * D]

    def peak_ps(self):
        return self.core.psum[0:3 * self.H * DC, 0, :].bitcast(BF16)[:, 0:P]

    def num_ps(self):
        return self.core.psum[:, 6, 0:D]

    def den_ps(self):
        return self.core.psum[:, 6, D:2 * D]

    def sync(self, sp):
        H, DH, K = self.H, self.DH, self.K

        def store(b):
            sp.wait_ge(self.pieces_ready, b + 1)
            for dram, pieces in ((self.q_dram, self.q3), (self.k_dram, self.k3)):
                for s in range(3):
                    sp.dma_start(dram[b, s].rearrange("d h t -> h d t"), pieces[:, b, s]).then_inc(self.pieces_stored[b % 2], 16)

        def load(b):
            j = b % RING
            if b == 0:
                sp.wait_ge(self.ones_ready, 1)
            sp.wait_ge(self.pieces_stored[b % 2], 16 * 6 * (b // 2 + 1))
            if b >= RING:
                sp.wait_ge(self.st_done, 2 * self.NB * (b - RING + 1))
            for first, count in SLOT_RUNS:
                to = slice(first * DH, (first + count) * DH)
                q, k = (dram[b].rearrange("s d h t -> s d (h t)") for dram in (self.q_dram, self.k_dram))
                sp.dma_start(self.qs[to, j].rearrange("p h t -> p (h t)"), q[0:count]).then_inc(self.stacks_loaded[j], 16)
                piece = K_PIECE[first]
                sp.dma_start(self.ks[to, j].rearrange("p h t -> p (h t)"),
                             k[piece:piece + 1].to_broadcast([count, DH, H * D])).then_inc(self.stacks_loaded[j], 16)

        def load_peak(b):
            sp.wait_ge(self.peak_rows_ready, b + 1)
            sp.dma_start(self.qs[K:K + 3, b % RING].rearrange("s h (c q) -> s (h c) q", c=DC),
                         self.peak_rows[:, b % 2, :]).then_inc(self.peak_loaded[b % RING], 16)

        store(0)
        store(1)
        load(0)
        load(1)
        store(2)
        load(2)
        load_peak(0)
        for b in range(B):
            if b + 1 < B:
                load_peak(b + 1)
            if b + RING < B:
                store(b + RING)
                load(b + RING)

    def gpsimd(self, pool):
        pool.memset(self.v_ones[:], 1.0).then_inc(self.v_ones_ready, 1)
        pool.wait_ge(self.v_ones_ready, 1)

        def spread_v(b):
            j = b % 2
            if b >= 2:
                pool.wait_ge(self.pv_done, 2 * self.NB * (b - 1))
            for c in range(DC):
                last = pool.tensor_copy(self.v_ones[:, j, c, :, 0:self.DH],
                                        self.v_t(b, c).rearrange("p (h d) -> p h d", h=self.H))
            last.then_inc(self.v_ready, 1)

        spread_v(0)
        spread_v(1)
        for b in range(B):
            for pair in range(self.NB // 2):
                blocks = slice(2 * pair, 2 * pair + 2)
                pool.wait_ge(self.o_hi_ready, b * self.NB // 2 + pair + 1)
                pool.tensor_tensor(self.o_lo[:, b % 2, blocks], self.o_sb[:, blocks], self.o_hi[:, b % 2, blocks].bitcast(F32), ALU.subtract)\
                    .then_inc(self.o_lo_ready, 1)
            if b + 2 < B:
                spread_v(b + 2)

    def vector_ones(self, dve):
        base = self.K - self.K % 32
        dve.memset(self.ks[base:self.K + 3], 1.0).then_inc(self.ones_ready, 1)

    def maxima(self, dve, ch, b):
        j = b % 2
        for n in range(self.H):
            c, pair = divmod(n, self.H // 2)
            dve.wait_ge(self.s_done, b * self.H + n + 1)
            last = dve.tensor_reduce(self.peak[:, j, 2 * pair:2 * pair + 2, c], self.s_ps(n), AXX, ALU.max)
            last.then_inc(self.max_done, 1)
        dve.wait_ge(self.max_done, (b + 1) * self.H)
        if b >= 1:
            dve.wait_ge(self.peak_turned, b)
        peak, rest, three = self.peak[:, j], self.peak_rest, self.peak3
        ch.step(dve.tensor_scalar(three[:, 0], peak, -1.0, None, ALU.mult))
        ch.wait()
        ch.step(dve.scalar_tensor_tensor(rest[:], peak, -1.0, three[:, 0], ALU.mult, ALU.subtract))
        ch.wait()
        ch.step(dve.tensor_copy(three[:, 1], rest[:]))
        ch.wait()
        dve.tensor_tensor(three[:, 2], rest[:], three[:, 1], ALU.subtract).then_inc(self.peak3_ready, 1)
        dve.wait_ge(self.peak_turned, b + 1)
        if b >= 2:
            dve.wait_ge(self.peak_loaded[(b - 2) % RING], 16 * ((b - 2) // RING + 1))
        dve.tensor_copy(self.peak_rows[:, j, :], self.peak_ps())\
            .then_inc(self.peak_rows_ready, 1)

    def vector(self, dve, ch, finish):
        self.maxima(dve, ch, 0)
        for b in range(B):
            if b + 1 < B:
                self.maxima(dve, ch, b + 1)
            if b:
                for step in finish:
                    step(b - 1)
        for step in finish:
            step(B - 1)

    def normalize(self, dve, ch, b):
        dve.wait_ge(self.parts_done, b + 1)
        dve.reciprocal(self.recip[:, :], self.den_ps()).then_inc(self.recip_ready, 1)
        dve.wait_ge(self.recip_ready, b + 1)
        dve.tensor_tensor(self.o_norm[:, b % 2, :], self.num_ps(), self.recip[:, :], ALU.mult).then_inc(self.norm_ready, 1)

    def exponentials(self, act, b):
        for n in range(2 * self.NB):
            m = b * 2 * self.NB + n
            act.wait_ge(self.st_done, m + 1)
            if m >= 2:
                act.wait_ge(self.pv_done, m - 1)
            act.activation(self.pt[:, n % 2], self.st_ps(n), ACT.Exp, scale=self.scale).then_inc(self.exp_done, 1)
            if n % 4 == 0 and n:
                self.take_sums(act, b, n // 4 - 1)
        self.take_sums(act, b, self.NB // 2 - 1)

    def take_sums(self, act, b, pair):
        act.wait_ge(self.pv_done, b * 2 * self.NB + 4 * pair + 4)
        if b >= 2:
            act.wait_ge(self.parts_done, b - 1)
        if b:
            act.wait_ge(self.o_lo_ready, (b - 1) * self.NB // 2 + pair + 1)
        blocks = slice(2 * pair, 2 * pair + 2)
        act.activation(self.o_sb[:, blocks].rearrange("p g q -> p (g q)"), self.core.psum[:, 7, :], ACT.Copy).then_inc(self.o_ready, 1)
        act.wait_ge(self.o_ready, b * self.NB // 2 + pair + 1)
        act.activation(self.o_hi[:, b % 2, blocks], self.o_sb[:, blocks], ACT.Copy).then_inc(self.o_hi_ready, 1)

    def scores_by_query(self, pe, b, n):
        j, K = b % RING, self.K
        c, pair = divmod(n, self.H // 2)
        if n == 0:
            pe.wait_ge(self.stacks_loaded[j], 16 * 2 * len(SLOT_RUNS) * (b // RING + 1))
        if n < 2 and b:
            pe.wait_ge(self.peak_rows_ready, b)
        if b * self.H + n >= 2:
            pe.wait_ge(self.max_done, b * self.H + n - 1)
        for i in range(2):
            h = 2 * pair + i
            last = pe.matmul(self.s_ps(n)[:, i, :], self.qs[0:K, j, h, c * P:(c + 1) * P], self.ks[0:K, j, h, :],
                             start=True, stop=self.mask is None)
            if self.mask:
                last = pe.matmul(self.s_ps(n)[:, i, :], self.core.ident_bf[:, :], self.mask[0][:, c, :], start=False, stop=True)
        last.then_inc(self.s_done, 1)

    def turn_peak(self, pe, b):
        pe.wait_ge(self.peak3_ready, b + 1)
        pe.transpose(self.peak_ps(), self.peak3[:].rearrange("p s h c -> p (s h c)"), self.core.ident_bf[:, :])\
            .then_inc(self.peak_turned, 1)

    def scores_by_key(self, pe, b, n):
        j, g, c, K = b % RING, n // 2, n % 2, self.K
        m = b * 2 * self.NB + n
        if n == 0:
            pe.wait_ge(self.ones_ready, 1)
            pe.wait_ge(self.peak_loaded[j], 16 * (b // RING + 1))
        if m >= 2:
            pe.wait_ge(self.exp_done, m - 1)
        for i in range(HB):
            h = g * HB + i
            last = pe.matmul(self.st_ps(n)[:, i, :], self.ks[0:K + 3, j, h, c * P:(c + 1) * P], self.qs[0:K + 3, j, h, :],
                             start=True, stop=self.mask is None)
            if self.mask:
                last = pe.matmul(self.st_ps(n)[:, i, :], self.core.ident_bf[:, :], self.mask[1][:, c, :], start=False, stop=True)
        last.then_inc(self.st_done, 1)

    def weighted_sums(self, pe, b, n):
        j, g, c = b % 2, n // 2, n % 2
        if n == 0:
            pe.wait_ge(self.v_ready, b + 1)
        if n % 4 == 0 and b * self.NB + g >= 2:
            pe.wait_ge(self.o_ready, (b * self.NB + g) // 2)
        pe.wait_ge(self.exp_done, b * 2 * self.NB + n + 1)
        for i in range(HB):
            last = pe.matmul(self.o_ps(g)[32 * i:32 * i + 32, :], self.v_ones[:, j, c, g * HB + i, :], self.pt[:, n % 2, i, :],
                             start=(c == 0), stop=(c == 1), skip_group_check=True)
        last.then_inc(self.pv_done, 1)

    def split_sums(self, pe, b, picks):
        pe.wait_ge(self.o_lo_ready, (b + 1) * self.NB // 2)
        if b:
            pe.wait_ge(self.norm_ready, b)
            if self.out_read:
                pe.wait_ge(self.out_read, b)
        for ps, pick in ((self.num_ps(), picks[0]), (self.den_ps(), picks[1])):
            for g in range(self.NB):
                for o in (self.o_hi, self.o_lo):
                    last = pe.matmul(ps, pick[:, g, :], o[:, b % 2, g, :], start=(g == 0 and o is self.o_hi),
                                     stop=(g == self.NB - 1 and o is self.o_lo))
        last.then_inc(self.parts_done, 1)

    def tensor(self, pe, picks, after=None):
        H, steps = self.H, 2 * self.NB
        for n in range(H):
            self.scores_by_query(pe, 0, n)
        self.turn_peak(pe, 0)
        for b in range(B):
            for n in range(steps):
                self.scores_by_key(pe, b, n)
                if n == 1 and b:
                    self.split_sums(pe, b - 1, picks)
                if b + 1 < B:
                    for i in range(self.LEAD * n, min(self.LEAD * (n + 1), H)):
                        self.scores_by_query(pe, b + 1, i)
                if n:
                    self.weighted_sums(pe, b, n - 1)
                if n == self.TURN_AT and b + 1 < B:
                    self.turn_peak(pe, b + 1)
            self.weighted_sums(pe, b, steps - 1)
            if b and after:
                after(b - 1)
        self.split_sums(pe, B - 1, picks)
        if after:
            after(B - 1)


def channel_attention_layer(nc, core, layer, ins, sb, sem):
    H = 8
    xn = sb("ca_xn", [P, B, D], F32)
    rest = sb("ca_rest", [P, B, D], F32)
    q3 = sb("ca_q3", [P, B, 3, D], BF16)
    k3 = sb("ca_k3", [P, B, 3, D], BF16)
    picks = sb("ca_picks", [P, 2, H // HB, P], F32)
    picks_r = sb("ca_picks_r", [P, 2, H // HB, P], F32R)
    picks_ready = sem("ca_picks_ready")
    picks_loaded, dve_step, pool_step = sem("ca_picks_loaded"), sem("ca_dve"), sem("ca_pool")
    att = HeadAttention(nc, core, sb, sem, "ca", H, 0.25, q3, k3,
                        lambda b, c: core.ctx_t[:, c, b, :])

    def sync(sp):
        sp.wait_ge(core.x_stats, (layer + 1) * B)
        sp.dma_start(picks[:], ins["picks8"]).then_inc(picks_loaded, 16)
        att.sync(sp)

    def gpsimd(pool):
        ch = Chain(pool, pool_step)
        for b in range(B):
            rstd_row(pool, ch, core, layer, b)
        pool.wait_ge(core.ctx_t_loaded, 16)
        att.gpsimd(pool)

    def vector(dve):
        ch = Chain(dve, dve_step)
        att.vector_ones(dve)
        dve.wait_ge(core.ctx_loaded, 16)
        for b in range(B):
            split_in_three(dve, ch, core.ctx[:, b], rest[:, b], [k3[:, b, s] for s in range(3)])
            dve.wait_ge(core.rstd_ready, layer * B + b + 1)
            ch.step(dve.tensor_scalar(xn[:, b], core.x_sb[:, b], core.mean_var[:, b, 0:1], core.rstd[:, b],
                                      ALU.subtract, ALU.mult))
            ch.wait()
            split_in_three(dve, ch, xn[:, b], rest[:, b], [q3[:, b, s] for s in range(3)])
            ch.wait()
            dve.sem_inc(att.pieces_ready, 1)
        def add_to_x(b):
            att.normalize(dve, ch, b)
            dve.wait_ge(att.norm_ready, b + 1)
            ch.step(dve.tensor_tensor(core.x_sb[:, b], core.x_sb[:, b], att.o_norm[:, b % 2], ALU.add))

        def prepare_fp8(b):
            core.fp8_weights.vector(dve, ch, b)

        def statistics(b):
            ch.wait()
            layer_norm_rows(dve, ch, core, b)

        att.vector(dve, ch, (add_to_x, prepare_fp8, statistics))

    def scalar(act):
        act.wait_ge(picks_loaded, 16)
        act.activation(picks_r[:], picks[:], ACT.Copy).then_inc(picks_ready, 1)
        for b in range(B):
            att.exponentials(act, b)

    def tensor(pe):
        pe.wait_ge(picks_ready, 1)
        att.tensor(pe, (picks_r[:, 0], picks_r[:, 1]))

    return dict(sync=sync, gpsimd=gpsimd, vector=vector, scalar=scalar, tensor=tensor)


F8 = 704
F8_SIZES = [P] * (F8 // P) + [F8 % P]
F8_CHUNKS = len(F8_SIZES)
F8_MAX = 448.0
EXPONENT_BITS = 0x7F800000


class Fp8Weights:

    NW = 2 * F8_CHUNKS + DC
    STEPS = 8

    def __init__(self, nc, core, ins, sb, sem):
        self.ins = ins
        self.idx = sb("f8_idx", [P, F8_CHUNKS], I32)
        self.w_rows = sb("f8_w_rows", [P, 2, F8_CHUNKS, D], F32)
        self.wd_rows = sb("f8_wd_rows", [P, DC, F8], F32)
        self.magic = sb("f8_magic", [P, F8_CHUNKS * D // 2], F32)
        self.w_q = sb("f8_w_q", [P, 2, F8_CHUNKS, D], BF16)
        self.wd_q = sb("f8_wd_q", [P, DC, F8], BF16)
        self.w_max = sb("f8_w_max", [P, self.NW], F32)
        self.w_scale = sb("f8_w_scale", [P, self.NW], F32)
        self.w_inv = sb("f8_w_inv", [P, self.NW], F32)
        self.idx_loaded, self.wd_loaded, self.pad_set = sem("f8_idx_loaded"), sem("f8_wd_loaded"), sem("f8_pad_set")
        self.rows_loaded, self.quantized = sem("f8_rows_loaded"), sem("f8_quantized")

    def sync(self, sp):
        sp.dma_start(self.idx[:, 0:F8_CHUNKS - 1], self.ins["f8_idx"]).then_inc(self.idx_loaded, 16)
        sp.dma_start(self.idx[0:F8_SIZES[-1], F8_CHUNKS - 1:F8_CHUNKS], self.ins["f8_idx_rest"]).then_inc(self.idx_loaded, 16)
        sp.dma_start(self.wd_rows[:], self.ins["f8_down"].rearrange("(c p) f -> p c f", p=P)).then_inc(self.wd_loaded, 16)

    def gather(self, pool):
        pool.memset(self.w_rows[:, :, F8_CHUNKS - 1, :], 1.0).then_inc(self.pad_set, 1)
        pool.wait_ge(self.pad_set, 1)
        pool.wait_ge(self.idx_loaded, 32)
        for m, name in enumerate(("f8_gate", "f8_up")):
            for c, size in enumerate(F8_SIZES):
                pool.indirect_dma_start(out=self.w_rows[0:size, m, c, :], out_offset=None, in_=self.ins[name],
                                        in_offset=bass.IndirectOffsetOnAxis(ap=self.idx[0:size, c:c + 1], axis=0))\
                    .then_inc(self.rows_loaded, 16)

    def vector(self, dve, ch, step):
        C2 = 2 * F8_CHUNKS
        if step == 0:
            dve.wait_ge(self.rows_loaded, 16 * C2)
            dve.wait_ge(self.pad_set, 1)
            dve.wait_ge(self.wd_loaded, 16)
            ch.step(dve.tensor_reduce(self.w_max[:, 0:C2], self.w_rows[:].rearrange("p m c d -> p (m c) d"), AXX, ALU.max,
                                      apply_absolute_value=True))
        elif step == 1:
            ch.step(dve.tensor_reduce(self.w_max[:, C2:], self.wd_rows[:], AXX, ALU.max, apply_absolute_value=True))
            ch.wait()
            ch.step(dve.tensor_scalar(self.w_scale[:, :], self.w_max[:, :], 1.0 / F8_MAX, None, ALU.mult))
            ch.wait()
            ch.step(dve.reciprocal(self.w_inv[:, :], self.w_scale[:, :]))
            ch.wait()
        else:
            if step < 6:
                half, n = F8_CHUNKS // 2, (step - 2) * (F8_CHUNKS // 2)
                rows = self.w_rows[:].rearrange("p m c d -> p (m c) d")[:, n:n + half]
                out = self.w_q[:].rearrange("p m c d -> p (m c) d")[:, n:n + half]
                for i in range(half):
                    ch.step(dve.tensor_scalar(rows[:, i], rows[:, i], self.w_inv[:, n + i:n + i + 1], None, ALU.mult))
                rows, out = rows.rearrange("p c d -> p (c d)"), out.rearrange("p c d -> p (c d)")
            else:
                rows, out, n = self.wd_rows[:, step - 6], self.wd_q[:, step - 6], C2 + step - 6
                ch.step(dve.tensor_scalar(rows, rows, self.w_inv[:, n:n + 1], None, ALU.mult))
            ch.wait()
            round_fp8(dve, ch, rows, self.magic[:, 0:rows.shape[-1]], out).then_inc(self.quantized, 1)
            dve.wait_ge(self.quantized, step - 1)


def round_fp8(dve, ch, v, m, out):
    ch.step(dve.tensor_scalar(m.bitcast(I32), v.bitcast(I32), EXPONENT_BITS, None, ALU.bitwise_and))
    ch.wait()
    ch.step(dve.tensor_scalar(m, m, 2.0 ** -6, 1.5 * 2.0 ** 20, ALU.max, ALU.mult))
    ch.wait()
    ch.step(dve.tensor_tensor(v, v, m, ALU.add))
    ch.wait()
    return dve.tensor_tensor(out, v, m, ALU.subtract)


def fp8_ffn_layer(nc, core, layer, ins, sb, sem):
    def chunks(width):
        return [(n, min(512, width - n)) for n in range(0, width, 512)]

    weights = core.fp8_weights
    NW, w_q, wd_q, w_scale = weights.NW, weights.w_q, weights.wd_q, weights.w_scale
    w_t = sb("f8_w_t", [P, 2, DC, F8_CHUNKS * P], BF16)
    wd_t = sb("f8_wd_t", [P, F8_CHUNKS, D], BF16)
    diag = sb("f8_diag", [P, 2, P], F32)
    w_back = sb("f8_w_back", [P, NW, P], F32)
    xn = sb("f8_xn", [P, 2, D], F32)
    xm = sb("f8_xm", [P, 2, D], F32)
    xq = sb("f8_xq", [P, 2, D], BF16)
    xq_t = sb("f8_xq_t", [P, 2, DC, P], BF16)
    st = sb("f8_st", [P, 2, 4], F32)
    st2 = sb("f8_st2", [P, 2, 4], F32)
    g = sb("f8_g", [P, 2, F8], F32)
    sg = sb("f8_sg", [P, 2, F8], F32)
    u = sb("f8_u", [P, 2, F8], F32)
    t = sb("f8_t", [P, 2, F8], F32)
    tv = sb("f8_tv", [P, 2, F8], F32)
    tm = sb("f8_tm", [P, 2, F8], F32)
    tq = sb("f8_tq", [P, 2, F8], BF16)
    a_t = sb("f8_a_t", [P, 2, F8_CHUNKS, P], BF16)
    out_rows = sb("f8_out", [P, 2, D], F32)

    dve_step, pool_step = sem("f8_dve"), sem("f8_pool")
    w_turned, w_t_ready = sem("f8_w_turned"), sem("f8_w_t_ready")
    diag_ready, back_done, back_ready = sem("f8_diag_ready"), sem("f8_back_done"), sem("f8_back_ready")
    xq_ready, xq_turned, xq_t_ready = sem("f8_xq_ready"), sem("f8_xq_turned"), sem("f8_xq_t_ready")
    gu_done, g_ready, u_ready, sg_ready, t_ready = (
        sem("f8_gu_done"), sem("f8_g_ready"), sem("f8_u_ready"), sem("f8_sg_ready"), sem("f8_t_ready"))
    inv_ready, tv_ready, tq_ready, a_turned, a_t_ready, y_done = (
        sem("f8_inv_ready"), sem("f8_tv_ready"), sem("f8_tq_ready"), sem("f8_a_turned"), sem("f8_a_t_ready"), sem("f8_y_done"))

    def gu_ps(which):
        return core.psum[:, 2 * which:2 * which + 2, :].rearrange("p n f -> p (n f)")

    xq_ps = core.psum[:, 4, :].bitcast(BF16)
    a_ps = core.psum[:, 5, :].bitcast(BF16)
    y_ps = core.psum[:, 6, 0:D]

    def turn_bank(n):
        return core.psum[:, 4 + n % 4, :].bitcast(BF16)

    def sync(sp):
        pass

    def gpsimd(pool):
        ch = Chain(pool, pool_step)
        for b in range(B):
            rstd_row(pool, ch, core, layer, b)
        for b in range(B):
            j = b % 2
            pool.wait_ge(sg_ready, b + 1)
            pool.wait_ge(u_ready, b + 1)
            if b >= 2:
                pool.wait_ge(tv_ready, b - 1)
            pool.tensor_tensor(t[:, j, :], sg[:, j, :], u[:, j, :], ALU.mult).then_inc(t_ready, 1)

    def vector(dve):
        ch = Chain(dve, dve_step)
        for n in range(NW):
            if n >= 2:
                dve.wait_ge(back_done, n - 1)
            dve.tensor_scalar(diag[:, n % 2, :], core.ident[:, :], w_scale[:, n:n + 1], None, ALU.mult).then_inc(diag_ready, 1)

        def quantize_x(b):
            j = b % 2
            dve.wait_ge(core.rstd_ready, layer * B + b + 1)
            ch.step(dve.tensor_scalar(xn[:, j, :], core.x_sb[:, b, :], core.mean_var[:, b, 0:1], core.rstd[:, b, :],
                                      ALU.subtract, ALU.mult))
            ch.wait()
            ch.step(dve.tensor_reduce(st[:, j, 0:1], xn[:, j, :], AXX, ALU.max, apply_absolute_value=True))
            ch.wait()
            ch.step(dve.tensor_scalar(st[:, j, 1:2], st[:, j, 0:1], 1.0 / F8_MAX, None, ALU.mult))
            ch.wait()
            ch.step(dve.reciprocal(st[:, j, 2:3], st[:, j, 1:2]))
            ch.wait()
            ch.step(dve.tensor_scalar(xn[:, j, :], xn[:, j, :], st[:, j, 2:3], None, ALU.mult))
            ch.wait()
            if b >= 2:
                dve.wait_ge(xq_turned, b - 1)
            round_fp8(dve, ch, xn[:, j, :], xm[:, j, :], xq[:, j, :]).then_inc(xq_ready, 1)

        def scale_products(b):
            j = b % 2
            dve.wait_ge(gu_done, b + 1)
            if b >= 2:
                dve.wait_ge(sg_ready, b - 1)
            back = w_back[:].rearrange("p n q -> p (n q)")
            dve.scalar_tensor_tensor(g[:, j, :], gu_ps(0)[:, 0:F8], st[:, j, 1:2], back[:, 0:F8], ALU.mult, ALU.mult)\
                .then_inc(g_ready, 1)
            if b >= 2:
                dve.wait_ge(t_ready, b - 1)
            dve.scalar_tensor_tensor(u[:, j, :], gu_ps(1)[:, 0:F8], st[:, j, 1:2], back[:, F8_CHUNKS * P:F8_CHUNKS * P + F8],
                                     ALU.mult, ALU.mult).then_inc(u_ready, 1)

        def quantize_inner(b):
            j = b % 2
            dve.wait_ge(t_ready, b + 1)
            ch.step(dve.tensor_reduce(st2[:, j, 0:1], t[:, j, :], AXX, ALU.max, apply_absolute_value=True))
            ch.wait()
            ch.step(dve.tensor_scalar(st2[:, j, 1:2], st2[:, j, 0:1], 1.0 / F8_MAX, None, ALU.mult))
            ch.wait()
            if b >= 2:
                dve.wait_ge(tv_ready, b - 1)
            dve.reciprocal(st2[:, j, 2:3], st2[:, j, 1:2]).then_inc(inv_ready, 1)
            if b:
                add_to_x(b - 1)
            dve.wait_ge(tv_ready, b + 1)
            if b >= 2:
                dve.wait_ge(a_turned, b - 1)
            round_fp8(dve, ch, tv[:, j, :], tm[:, j, :], tq[:, j, :]).then_inc(tq_ready, 1)

        def add_to_x(b):
            j = b % 2
            dve.wait_ge(y_done, b + 1)
            back = w_back[:, 2 * F8_CHUNKS:NW, :].rearrange("p n q -> p (n q)")
            ch.step(dve.scalar_tensor_tensor(out_rows[:, j, :], y_ps, st2[:, j, 1:2], back, ALU.mult, ALU.mult))
            ch.wait()
            ch.step(dve.tensor_tensor(core.x_sb[:, b, :], core.x_sb[:, b, :], out_rows[:, j, :], ALU.add))
            ch.wait()
            layer_norm_rows(dve, ch, core, b)

        quantize_x(0)
        quantize_x(1)
        dve.wait_ge(back_ready, NW)
        scale_products(0)
        for b in range(B):
            if b + 1 < B:
                scale_products(b + 1)
            if b + 2 < B:
                quantize_x(b + 2)
            quantize_inner(b)
        add_to_x(B - 1)

    def scalar(act):
        for n in range(3):
            act.wait_ge(w_turned, n + 1)
            for i in range(8):
                m, c, r = (8 * n + i) // (DC * F8_CHUNKS), ((8 * n + i) // DC) % F8_CHUNKS, (8 * n + i) % DC
                last = act.activation(w_t[:, m, r, c * P:(c + 1) * P], turn_bank(n)[:, i * P:(i + 1) * P], ACT.Copy)
            last.then_inc(w_t_ready, 1)
        for n in range(3, 5):
            act.wait_ge(w_turned, n + 1)
            for i in range(8 if n == 3 else 4):
                c, r = divmod(8 * (n - 3) + i, DC)
                last = act.activation(wd_t[0:F8_SIZES[c], c, r * P:(r + 1) * P], turn_bank(n)[0:F8_SIZES[c], i * P:(i + 1) * P], ACT.Copy)
            last.then_inc(w_t_ready, 1)
        for n in range(NW):
            act.wait_ge(back_done, n + 1)
            act.activation(w_back[:, n, :], core.psum[:, n % 4, 0:P], ACT.Copy).then_inc(back_ready, 1)

        def turned_x(b):
            act.wait_ge(xq_turned, b + 1)
            if b >= 2:
                act.wait_ge(gu_done, b - 1)
            act.activation(xq_t[:, b % 2].rearrange("p a b -> p (a b)"), xq_ps[:, 0:D], ACT.Copy).then_inc(xq_t_ready, 1)

        def silu(b):
            j = b % 2
            act.wait_ge(g_ready, b + 1)
            if b >= 2:
                act.wait_ge(t_ready, b - 1)
            act.activation(sg[:, j, :], g[:, j, :], ACT.Silu).then_inc(sg_ready, 1)

        def scaled(b):
            j = b % 2
            act.wait_ge(inv_ready, b + 1)
            if b >= 2:
                act.wait_ge(tq_ready, b - 1)
            act.activation(tv[:, j, :], t[:, j, :], ACT.Copy, scale=st2[:, j, 2:3]).then_inc(tv_ready, 1)

        def turned_inner(b):
            act.wait_ge(a_turned, b + 1)
            if b >= 2:
                act.wait_ge(y_done, b - 1)
            full = F8_CHUNKS - 1
            act.activation(a_t[:, b % 2, 0:full].rearrange("p a b -> p (a b)"), a_ps[:, 0:full * P], ACT.Copy)
            act.activation(a_t[0:F8_SIZES[-1], b % 2, full, :], a_ps[0:F8_SIZES[-1], full * P:(full + 1) * P], ACT.Copy)\
                .then_inc(a_t_ready, 1)

        turned_x(0)
        turned_x(1)
        silu(0)
        for b in range(B):
            if b + 1 < B:
                silu(b + 1)
            if b + 2 < B:
                turned_x(b + 2)
            scaled(b)
            turned_inner(b)

    def tensor(pe):
        pe.wait_ge(weights.quantized, weights.STEPS - 2)
        for n in range(3):
            for i in range(8):
                m, c, r = (8 * n + i) // (DC * F8_CHUNKS), ((8 * n + i) // DC) % F8_CHUNKS, (8 * n + i) % DC
                last = pe.transpose(turn_bank(n)[:, i * P:(i + 1) * P], w_q[:, m, c, r * P:(r + 1) * P], core.ident_bf[:, :])
            last.then_inc(w_turned, 1)
        for n in range(3, 5):
            if n == 4:
                pe.wait_ge(w_t_ready, 1)
            for i in range(8 if n == 3 else 4):
                c, r = divmod(8 * (n - 3) + i, DC)
                last = pe.transpose(turn_bank(n)[0:F8_SIZES[c], i * P:(i + 1) * P], wd_q[:, r, c * P:c * P + F8_SIZES[c]],
                                    core.ident_bf[:, :])
            last.then_inc(w_turned, 1)
        for n in range(NW):
            pe.wait_ge(diag_ready, n + 1)
            if n >= 4:
                pe.wait_ge(back_ready, n - 3)
            pe.matmul(core.psum[:, n % 4, 0:P], core.ones[:, :], diag[:, n % 2, :], start=True, stop=True).then_inc(back_done, 1)
        pe.wait_ge(w_t_ready, 5)
        pe.wait_ge(back_ready, NW)

        def turn_x(b):
            pe.wait_ge(xq_ready, b + 1)
            if b:
                pe.wait_ge(xq_t_ready, b)
            for c in range(DC):
                last = pe.transpose(xq_ps[:, c * P:(c + 1) * P], xq[:, b % 2, c * P:(c + 1) * P], core.ident_bf[:, :])
            last.then_inc(xq_turned, 1)

        def product1(b):
            pe.wait_ge(xq_t_ready, b + 1)
            if b:
                pe.wait_ge(u_ready, b)
            for m in range(2):
                for n, size in chunks(F8):
                    for c in range(DC):
                        last = pe.matmul(gu_ps(m)[:, n:n + size], xq_t[:, b % 2, c, :], w_t[:, m, c, n:n + size],
                                         start=(c == 0), stop=(c == DC - 1))
            last.then_inc(gu_done, 1)

        def turn_inner(b):
            pe.wait_ge(tq_ready, b + 1)
            if b:
                pe.wait_ge(a_t_ready, b)
            for c, size in enumerate(F8_SIZES):
                last = pe.transpose(a_ps[0:size, c * P:(c + 1) * P], tq[:, b % 2, c * P:c * P + size], core.ident_bf[:, :])
            last.then_inc(a_turned, 1)

        def product2(b):
            pe.wait_ge(a_t_ready, b + 1)
            if b:
                pe.wait_ge(core.x_stats, (layer + 1) * B + b)
            for c, size in enumerate(F8_SIZES):
                last = pe.matmul(y_ps, a_t[0:size, b % 2, c, :], wd_t[0:size, c, :], start=(c == 0), stop=(c == F8_CHUNKS - 1))
            last.then_inc(y_done, 1)

        turn_x(0)
        product1(0)
        turn_x(1)
        product1(1)
        for b in range(B):
            if b + 2 < B:
                turn_x(b + 2)
                product1(b + 2)
            turn_inner(b)
            product2(b)

    return dict(sync=sync, gpsimd=gpsimd, vector=vector, scalar=scalar, tensor=tensor)


def memory_attention_layer(nc, core, layer, ins, sb, sem):
    HALF = B // 2
    xn = sb("ma_xn", [P, B, D], F32)
    xn_t = sb("ma_xn_t", [P, 2, DC, HALF, T], F32)
    mask_u8 = sb("ma_mask_u8", [P, B * T], U8)
    mask = sb("ma_mask", [P, B, T], F32)
    mask_fill = sb("ma_mask_fill", [P, B, T], F32)
    valid = sb("ma_valid", [P, B], F32)
    s = sb("ma_s", [P, 2, HALF, T], F32)
    e = sb("ma_e", [P, 2, HALF, T], F32)
    e_t = sb("ma_e_t", [P, 2, HALF, T], F32)
    peak = sb("ma_peak", [P, 2, HALF], F32)
    total = sb("ma_total", [P, 2, HALF], F32)
    weight = sb("ma_weight", [P, 2, HALF], F32)

    mask_loaded, dve_step, pool_step = sem("ma_mask_loaded"), sem("ma_dve"), sem("ma_pool")
    xn_ready, xn_turned, xn_t_ready, s_done = sem("ma_xn_ready"), sem("ma_xn_turned"), sem("ma_xn_t_ready"), sem("ma_s_done")
    s_ready, e_ready, e_turned, e_t_ready, o_done = (
        sem("ma_s_ready"), sem("ma_e_ready"), sem("ma_e_turned"), sem("ma_e_t_ready"), sem("ma_o_done"))

    def xn_ps(c):
        return core.psum[:, c, :].rearrange("p (b t) -> p b t", t=T)

    def s_ps(n):
        return core.psum[:, 2 + n, :].rearrange("p (b t) -> p b t", t=T)

    def e_ps(n):
        return core.psum[:, 4 + n, :].rearrange("p (b t) -> p b t", t=T)

    def o_ps(i):
        return core.psum[:, 6 + i // 2, (i % 2) * D:(i % 2 + 1) * D]

    def sync(sp):
        sp.wait_ge(core.x_stats, (layer + 1) * B)
        sp.dma_start(mask_u8[:, :], ins["mask_mem"].to_broadcast([P, B * T])).then_inc(mask_loaded, 16)

    def gpsimd(pool):
        ch = Chain(pool, pool_step)
        for b in range(B):
            rstd_row(pool, ch, core, layer, b)

    def vector(dve):
        ch = Chain(dve, dve_step)
        dve.wait_ge(mask_loaded, 16)
        dve.wait_ge(core.x_stats, (layer + 1) * B)
        ch.step(dve.tensor_copy(mask[:].rearrange("p b t -> p (b t)"), mask_u8[:, :]))
        ch.wait()
        ch.step(dve.tensor_scalar(mask_fill[:], mask[:], 1.0, 1e30, ALU.subtract, ALU.mult))
        ch.step(dve.tensor_reduce(valid[:, :], mask[:], AXX, ALU.max))
        for b in range(B):
            dve.wait_ge(core.rstd_ready, layer * B + b + 1)
            dve.tensor_scalar(xn[:, b, :], core.x_sb[:, b, :], core.mean_var[:, b, 0:1], core.rstd[:, b, :],
                              ALU.subtract, ALU.mult).then_inc(xn_ready, 1)
        for n in range(2):
            own = slice(HALF * n, HALF * n + HALF)
            dve.wait_ge(s_done, n + 1)
            ch.step(dve.scalar_tensor_tensor(s[:, n], s_ps(n), 1.0 / 16.0, mask[:, own], ALU.mult, ALU.mult))
            ch.wait()
            ch.step(dve.tensor_tensor(s[:, n], s[:, n], mask_fill[:, own], ALU.add))
            ch.wait()
            ch.step(dve.tensor_reduce(peak[:, n], s[:, n], AXX, ALU.max))
            ch.wait()
            dve.tensor_tensor(s[:, n], s[:, n], peak[:, n].to_broadcast([P, HALF, T]), ALU.subtract).then_inc(s_ready, 1)
        for n in range(2):
            dve.wait_ge(e_ready, n + 1)
            ch.step(dve.tensor_reduce(total[:, n], e[:, n], AXX, ALU.add))
            ch.wait()
            ch.step(dve.reciprocal(total[:, n], total[:, n]))
            ch.wait()
            ch.step(dve.tensor_tensor(weight[:, n], total[:, n], valid[:, HALF * n:HALF * n + HALF], ALU.mult))
            ch.wait()
            dve.wait_ge(o_done, n + 1)
            for i in range(HALF):
                b = HALF * n + i
                ch.step(dve.scalar_tensor_tensor(core.x_sb[:, b], o_ps(i), weight[:, n, i:i + 1], core.x_sb[:, b],
                                                 ALU.mult, ALU.add))
                ch.wait()
                layer_norm_rows(dve, ch, core, b)

    def scalar(act):
        for n in range(2):
            act.wait_ge(xn_turned, n + 1)
            for c in range(DC):
                act.activation(xn_t[:, n, c], xn_ps(c), ACT.Copy).then_inc(xn_t_ready, 1)
        for n in range(2):
            act.wait_ge(s_ready, n + 1)
            act.activation(e[:, n], s[:, n], ACT.Exp).then_inc(e_ready, 1)
            act.wait_ge(e_turned, n + 1)
            act.activation(e_t[:, n], e_ps(n), ACT.Copy).then_inc(e_t_ready, 1)

    def tensor(pe):
        pe.wait_ge(core.ctx_t_loaded, 16)
        for n in range(2):
            if n:
                pe.wait_ge(xn_t_ready, DC)
            for i in range(HALF):
                pe.wait_ge(xn_ready, HALF * n + i + 1)
                for c in range(DC):
                    last = pe.transpose(xn_ps(c)[:, i, :], xn[:, HALF * n + i, c * P:(c + 1) * P], core.ident[:, :])
            last.then_inc(xn_turned, 1)
            pe.wait_ge(xn_t_ready, DC * (n + 1))
            for i in range(HALF):
                for c in range(DC):
                    last = pe.matmul(s_ps(n)[:, i, :], xn_t[:, n, c, i, :], core.ctx_t[:, c, HALF * n + i, :],
                                     start=(c == 0), stop=(c == DC - 1))
            last.then_inc(s_done, 1)
        pe.wait_ge(core.ctx_loaded, 16)
        for n in range(2):
            pe.wait_ge(e_ready, n + 1)
            for i in range(HALF):
                last = pe.transpose(e_ps(n)[:, i, :], e[:, n, i, :], core.ident[:, :])
            last.then_inc(e_turned, 1)
            pe.wait_ge(e_t_ready, n + 1)
            if n:
                pe.wait_ge(core.x_stats, (layer + 1) * B + HALF)
            for i in range(HALF):
                last = pe.matmul(o_ps(i), e_t[:, n, i, :], core.ctx[:, HALF * n + i, :], start=True, stop=True)
            last.then_inc(o_done, 1)

    return dict(sync=sync, gpsimd=gpsimd, vector=vector, scalar=scalar, tensor=tensor)


TOKENS = B * T
EW = 2 * D + D


def in_turn(engine, count):
    yield 0, 0
    yield 1, 1
    with engine.Fori(1, count // 2 - 1) as pair:
        for j in range(2):
            yield pair * 2 + j, j
    yield count - 2, 0
    yield count - 1, 1


def experts_layer(nc, core, layer, ins, sb, sem, name, E, choose):
    xn = sb(f"{name}_xn", [P, B, D], F32)
    x_t = sb(f"{name}_x_t", [P, DC, TOKENS], F32)
    x_hi = sb(f"{name}_x_hi", [P, DC, TOKENS], F32R)
    x_lo = sb(f"{name}_x_lo", [P, DC, TOKENS], F32R)
    router = sb(f"{name}_router", [P, DC, E], F32)
    logits = sb(f"{name}_logits", [P, B, E], F32)
    combine = sb(f"{name}_combine", [P, B, E], F32)
    combine_t = sb(f"{name}_combine_t", [E, TOKENS], F32)
    combine_dram = nc.dram_tensor(f"{name}_combine_dram", [E, TOKENS], F32, kind="Internal").ap()
    w = sb(f"{name}_w", [P, 2, EW], F32)
    w_hi = sb(f"{name}_w_hi", [P, 2, EW], F32R)
    w_lo = sb(f"{name}_w_lo", [P, 2, EW], F32R)
    row = sb(f"{name}_row", [1, 2, TOKENS], F32)
    waited = sb(f"{name}_waited", [1, 1], F32)
    rows = sb(f"{name}_rows", [P, 2, TOKENS], F32)
    sg = sb(f"{name}_sg", [P, 2, 512], F32)
    a = sb(f"{name}_a", [P, 2, 512], F32)
    a_hi = sb(f"{name}_a_hi", [P, 2, 512], F32R)
    a_lo = sb(f"{name}_a_lo", [P, 2, 512], F32R)
    out_t = sb(f"{name}_out_t", [P, DC, TOKENS], F32)

    def s(what):
        return sem(f"{name}_{what}")

    router_loaded, dve_step, pool_step = s("router_loaded"), s("dve"), s("pool")
    xn_ready, xn_turned, xt_ready, hi_ready, logits_done, logits_ready = (
        s("xn_ready"), s("xn_turned"), s("xt_ready"), s("hi_ready"), s("logits_done"), s("logits_ready"))
    combine_ready, combine_turned, combine_t_ready, combine_stored = (
        s("combine_ready"), s("combine_turned"), s("combine_t_ready"), s("combine_stored"))
    w_loaded, row_loaded = [s("w_loaded0"), s("w_loaded1")], [s("row_loaded0"), s("row_loaded1")]
    gu_hi_ready, gu_lo_ready, rows_ready = s("gu_hi_ready"), s("gu_lo_ready"), s("rows_ready")
    down_hi_ready, down_lo_ready = s("down_hi_ready"), s("down_lo_ready")
    gu_done, silu_ready, gated_ready, a_ready, a_hi_ready, a_lo_ready, down_done = (
        s("gu_done"), s("silu_ready"), s("gated_ready"), s("a_ready"), s("a_hi_ready"), s("a_lo_ready"), s("down_done"))
    out_t_ready, out_turned = s("out_t_ready"), s("out_turned")

    def xt_ps(n):
        return core.psum[:, n % 4, :].rearrange("p (b c t) -> p b c t", c=DC, t=T)

    logits_ps = core.psum[:, 4, 0:B * E].rearrange("p (b e) -> p b e", e=E)

    def combine_ps(n):
        return core.psum[0:E, 6 + n, :]

    def half_ps(n, which):
        return core.psum[:, 2 * n + which, :]

    def out_ps(c, n):
        return core.psum[:, 4 + 2 * c + n, :]

    GU, DOWN = slice(0, 2 * D), slice(2 * D, 3 * D)

    def later(e):
        return not isinstance(e, int) or e >= 1

    def loads(e, j):
        return (e // 2 + 1) * 16 if isinstance(e, int) else (e - j) * 8 + 16

    def out_rows(b):
        return core.psum[:, b // 2, (b % 2) * D:(b % 2 + 1) * D]

    def sync(sp):
        sp.wait_ge(core.x_stats, (layer + 1) * B)
        sp.dma_start(router[:], ins[f"{name}_router"].rearrange("(c p) e -> p c e", p=P)).then_inc(router_loaded, 16)
        for e in range(2):
            sp.dma_start(w[:, e, :], ins[f"{name}_experts"][e]).then_inc(w_loaded[e], 16)
        sp.wait_ge(combine_t_ready, 1)
        sp.dma_start(combine_dram, combine_t[:, :]).then_inc(combine_stored, 16)
        sp.wait_ge(combine_stored, 16)
        for e in range(2):
            sp.dma_start(row[0:1, e, :], combine_dram[e:e + 1, :]).then_inc(row_loaded[e], 16)
        with sp.Fori(1, E // 2) as pair:
            for j in range(2):
                sp.wait_ge(down_lo_ready, pair * 2 + (j - 1))
                sp.dma_start(w[:, j, :], ins[f"{name}_experts"][pair * 2 + j]).then_inc(w_loaded[j], 16)
                sp.wait_ge(rows_ready, pair * 2 + (j - 1))
                sp.dma_start(row[0:1, j, :], combine_dram[bass.ds(pair * 2 + j, 1), :]).then_inc(row_loaded[j], 16)

    def gpsimd(pool):
        ch = Chain(pool, pool_step)
        for b in range(B):
            rstd_row(pool, ch, core, layer, b)
        for e, j in in_turn(pool, E):
            pool.wait_ge(row_loaded[j], loads(e, j))
            if not (isinstance(e, int) and e < 2):
                pool.wait_ge(a_ready, e * 2 - 2)
            if not (isinstance(e, int) and e < 1):
                pool.wait_ge(rows_ready, e)
            pool.tensor_tensor(waited[:, :], core.minus_half[0:1, :], core.minus_half[0:1, :], ALU.mult)
            pool.partition_broadcast(rows[:, j, :], row[0:1, j, :]).then_inc(rows_ready, 1)

    def vector(dve):
        ch = Chain(dve, dve_step)
        for b in range(B):
            dve.wait_ge(core.rstd_ready, layer * B + b + 1)
            dve.tensor_scalar(xn[:, b, :], core.x_sb[:, b, :], core.mean_var[:, b, 0:1], core.rstd[:, b, :],
                              ALU.subtract, ALU.mult).then_inc(xn_ready, 1)
        for n in range(B // 2):
            own = slice(2 * n * T, 2 * (n + 1) * T)
            dve.wait_ge(xt_ready, n + 1)
            ch.step(dve.tensor_copy(x_hi[:, :, own], x_t[:, :, own]))
            ch.wait()
            dve.tensor_tensor(x_lo[:, :, own], x_t[:, :, own], x_hi[:, :, own].bitcast(F32), ALU.subtract).then_inc(hi_ready, 1)

        def low_gate_up(e, j):
            dve.wait_ge(gu_hi_ready, e + 1)
            dve.tensor_tensor(w_lo[:, j, GU], w[:, j, GU], w_hi[:, j, GU].bitcast(F32), ALU.subtract).then_inc(gu_lo_ready, 1)

        def low_down(e, j):
            dve.wait_ge(down_hi_ready, e + 1)
            dve.tensor_tensor(w_lo[:, j, DOWN], w[:, j, DOWN], w_hi[:, j, DOWN].bitcast(F32), ALU.subtract).then_inc(down_lo_ready, 1)

        def gated(e, j, n):
            dve.wait_ge(silu_ready, e * 2 + (n + 1))
            dve.tensor_tensor(sg[:, n, :], sg[:, n, :], half_ps(n, 1), ALU.mult).then_inc(gated_ready, 1)
            if n == 0:
                dve.wait_ge(rows_ready, e + 1)
            dve.wait_ge(gated_ready, e * 2 + (n + 1))
            dve.tensor_tensor(a[:, n, :], sg[:, n, :], rows[:, j, n * 512:(n + 1) * 512], ALU.mult).then_inc(a_ready, 1)

        def low_a(e, n):
            dve.wait_ge(a_hi_ready, e * 2 + (n + 1))
            dve.tensor_tensor(a_lo[:, n, :], a[:, n, :], a_hi[:, n, :].bitcast(F32), ALU.subtract).then_inc(a_lo_ready, 1)

        low_gate_up(0, 0)
        dve.wait_ge(logits_done, 1)
        ch.step(dve.tensor_copy(logits[:], logits_ps))
        ch.wait()
        choose(dve, ch, logits, combine)
        ch.wait()
        dve.sem_inc(combine_ready, 1)
        dve.wait_ge(combine_turned, 1)
        for n in range(2):
            last = dve.tensor_copy(combine_t[:, n * 512:(n + 1) * 512], combine_ps(n))
        last.then_inc(combine_t_ready, 1)
        for e, j in in_turn(dve, E):
            gated(e, j, 0)
            if not (isinstance(e, int) and e == E - 1):
                low_gate_up(e + 1, 1 - j)
            low_a(e, 0)
            gated(e, j, 1)
            low_down(e, j)
            low_a(e, 1)
        for b in range(B):
            if b % 2 == 0:
                dve.wait_ge(out_turned, b // 2 + 1)
            ch.step(dve.tensor_tensor(core.x_sb[:, b, :], core.x_sb[:, b, :], out_rows(b), ALU.add))
            ch.wait()
            layer_norm_rows(dve, ch, core, b)

    def scalar(act):
        for n in range(B // 2):
            act.wait_ge(xn_turned, n + 1)
            for i in range(2):
                last = act.activation(x_t[:, :, (2 * n + i) * T:(2 * n + i + 1) * T], xt_ps(n)[:, i], ACT.Copy)
            last.then_inc(xt_ready, 1)

        def high_gate_up(e, j):
            act.wait_ge(w_loaded[j], loads(e, j))
            if not (isinstance(e, int) and e < 2):
                act.wait_ge(gu_done, e * 2 - 2)
            act.activation(w_hi[:, j, GU], w[:, j, GU], ACT.Copy).then_inc(gu_hi_ready, 1)

        def high_down(e, j):
            if not (isinstance(e, int) and e < 2):
                act.wait_ge(down_done, e * 2 - 2)
            act.activation(w_hi[:, j, DOWN], w[:, j, DOWN], ACT.Copy).then_inc(down_hi_ready, 1)

        def silu(e, n):
            act.wait_ge(gu_done, e * 2 + (n + 1))
            if later(e):
                act.wait_ge(a_ready, e * 2 + (n - 1))
            act.activation(sg[:, n, :], half_ps(n, 0), ACT.Silu).then_inc(silu_ready, 1)

        def high_a(e, n):
            act.wait_ge(a_ready, e * 2 + (n + 1))
            if later(e):
                act.wait_ge(down_done, e * 2 + (n - 1))
            act.activation(a_hi[:, n, :], a[:, n, :], ACT.Copy).then_inc(a_hi_ready, 1)

        high_gate_up(0, 0)
        choose.scalar(act)
        for e, j in in_turn(act, E):
            silu(e, 0)
            if not (isinstance(e, int) and e == E - 1):
                high_gate_up(e + 1, 1 - j)
            high_a(e, 0)
            silu(e, 1)
            high_down(e, j)
            high_a(e, 1)
        act.wait_ge(down_done, 2 * E)
        for c in range(DC):
            for n in range(2):
                act.activation(out_t[:, c, n * 512:(n + 1) * 512], out_ps(c, n), ACT.Copy).then_inc(out_t_ready, 1)

    def tensor(pe):
        for n in range(B // 2):
            for i in range(2):
                pe.wait_ge(xn_ready, 2 * n + i + 1)
                for c in range(DC):
                    last = pe.transpose(xt_ps(n)[:, i, c, :], xn[:, 2 * n + i, c * P:(c + 1) * P], core.ident[:, :])
            last.then_inc(xn_turned, 1)
        pe.wait_ge(router_loaded, 16)
        for b in range(B):
            pe.wait_ge(xt_ready, b // 2 + 1)
            for c in range(DC):
                last = pe.matmul(logits_ps[:, b, :], x_t[:, c, b * T:(b + 1) * T], router[:, c, :], start=(c == 0), stop=(c == DC - 1))
        last.then_inc(logits_done, 1)
        def gate_up(e, j, n):
            if n == 0:
                pe.wait_ge(gu_lo_ready, e + 1)
            if later(e):
                pe.wait_ge(gated_ready, e * 2 + (n - 1))
            own = slice(n * 512, (n + 1) * 512)
            for which in range(2):
                k = 0
                for c in range(DC):
                    col = slice((which * DC + c) * P, (which * DC + c + 1) * P)
                    for wp, xp in ((w_hi, x_hi), (w_hi, x_lo), (w_lo, x_hi)):
                        last = pe.matmul(half_ps(n, which), wp[:, j, col], xp[:, c, own], start=(k == 0), stop=(k == 3 * DC - 1))
                        k += 1
            last.then_inc(gu_done, 1)

        def down(e, j, n):
            if n == 0:
                pe.wait_ge(down_lo_ready, e + 1)
            pe.wait_ge(a_lo_ready, e * 2 + (n + 1))
            if n == 0 and not later(e):
                pe.wait_ge(combine_t_ready, 1)
            begins, ends = isinstance(e, int) and e == 0, isinstance(e, int) and e == E - 1
            for c in range(DC):
                col = slice(2 * D + c * P, 2 * D + (c + 1) * P)
                for k, (wp, ap) in enumerate(((w_hi, a_hi), (w_hi, a_lo), (w_lo, a_hi))):
                    last = pe.matmul(out_ps(c, n), wp[:, j, col], ap[:, n, :], start=begins and k == 0, stop=ends and k == 2)
            last.then_inc(down_done, 1)

        pe.wait_ge(hi_ready, B // 2)
        for n in range(2):
            gate_up(0, 0, n)
        pe.wait_ge(combine_ready, 1)
        for b in range(B):
            last = pe.transpose(combine_ps(b // 4)[:, (b % 4) * T:(b % 4 + 1) * T], combine[:, b, :], core.ident[:, :])
        last.then_inc(combine_turned, 1)
        for e, j in in_turn(pe, E):
            for n in range(2):
                if later(e):
                    gate_up(e, j, n)
                if later(e):
                    down(e - 1, 1 - j, n)
        for n in range(2):
            down(E - 1, 1, n)
        for b in range(B):
            pe.wait_ge(out_t_ready, b // 4 + 3)
            for c in range(DC):
                last = pe.transpose(out_rows(b)[:, c * P:(c + 1) * P], out_t[:, c, b * T:(b + 1) * T], core.ident[:, :])
            if b % 2:
                last.then_inc(out_turned, 1)

    return dict(sync=sync, gpsimd=gpsimd, vector=vector, scalar=scalar, tensor=tensor)


def top8_experts_layer(nc, core, layer, ins, sb, sem):
    E = 64
    best = sb("e64_best", [P, B, 8], F32)
    left = sb("e64_left", [P, B, E], F32)
    chosen = sb("e64_chosen", [P, B, E], F32)
    exps = sb("e64_exps", [P, B, E], F32)
    total = sb("e64_total", [P, B], F32)
    shifted_ready, exps_ready = sem("e64_shifted_ready"), sem("e64_exps_ready")

    def choose(dve, ch, logits, combine):
        for b in range(B):
            ch.step(dve.max(best[:, b, :], logits[:, b, :]))
            ch.wait()
            ch.step(dve.match_replace(left[:, b, :], best[:, b, :], logits[:, b, :], -3e38))
        dve.tensor_tensor(exps[:], logits[:], best[:, :, 0].to_broadcast([P, B, E]), ALU.subtract).then_inc(shifted_ready, 1)
        ch.wait()
        ch.step(dve.tensor_tensor(chosen[:], logits[:], left[:], ALU.not_equal))
        ch.wait()
        dve.wait_ge(exps_ready, 1)
        ch.step(dve.tensor_tensor(exps[:], exps[:], chosen[:], ALU.mult))
        ch.wait()
        ch.step(dve.tensor_reduce(total[:, :], exps[:], AXX, ALU.add))
        ch.wait()
        ch.step(dve.reciprocal(total[:, :], total[:, :]))
        ch.wait()
        ch.step(dve.tensor_tensor(combine[:], exps[:], total[:, :].to_broadcast([P, B, E]), ALU.mult))

    def choose_scalar(act):
        act.wait_ge(shifted_ready, 1)
        act.activation(exps[:], exps[:], ACT.Exp).then_inc(exps_ready, 1)

    choose.scalar = choose_scalar
    return experts_layer(nc, core, layer, ins, sb, sem, "e64", E, choose)


def top2_experts_layer(nc, core, layer, ins, sb, sem):
    E = 16
    best = sb("e16_best", [P, B, 8], F32)
    index = sb("e16_index", [P, B, 8], mybir.dt.uint32)
    index_f = sb("e16_index_f", [P, B, 2], F32)
    sigmoids = sb("e16_sigmoids", [P, B, 2], F32)
    total = sb("e16_total", [P, B], F32)
    weight = sb("e16_weight", [P, B, 2], F32)
    second = sb("e16_second", [P, B, E], F32)
    best_ready, sigmoids_ready, numbers_ready = sem("e16_best_ready"), sem("e16_sigmoids_ready"), sem("e16_numbers_ready")
    numbers = sb("e16_numbers", [P, E], F32)
    numbers_loaded = sem("e16_numbers_loaded")

    def choose(dve, ch, logits, combine):
        for b in range(B):
            ch.step(dve.max(best[:, b, :], logits[:, b, :]))
            ch.wait()
            ch.step(dve.max_index(index[:, b, :], best[:, b, :], logits[:, b, :]))
        ch.wait()
        dve.tensor_copy(index_f[:], index[:, :, 0:2]).then_inc(best_ready, 1)
        dve.wait_ge(best_ready, 1)
        dve.wait_ge(sigmoids_ready, 1)
        dve.wait_ge(numbers_loaded, 16)
        ch.step(dve.tensor_tensor(total[:, :], sigmoids[:, :, 0], sigmoids[:, :, 1], ALU.add))
        ch.wait()
        ch.step(dve.reciprocal(total[:, :], total[:, :]))
        ch.wait()
        ch.step(dve.tensor_tensor(weight[:], sigmoids[:], total[:, :].to_broadcast([P, B, 2]), ALU.mult))
        ch.wait()
        for b in range(B):
            ch.step(dve.tensor_scalar(combine[:, b, :], numbers[:, :], index_f[:, b, 0:1], weight[:, b, 0:1], ALU.is_equal, ALU.mult))
            ch.step(dve.tensor_scalar(second[:, b, :], numbers[:, :], index_f[:, b, 1:2], weight[:, b, 1:2], ALU.is_equal, ALU.mult))
        ch.wait()
        ch.step(dve.tensor_tensor(combine[:], combine[:], second[:], ALU.add))

    def choose_scalar(act):
        act.wait_ge(best_ready, 1)
        act.activation(sigmoids[:], best[:, :, 0:2], ACT.Sigmoid).then_inc(sigmoids_ready, 1)

    choose.scalar = choose_scalar
    programs = experts_layer(nc, core, layer, ins, sb, sem, "e16", E, choose)
    experts_sync = programs["sync"]

    def sync(sp):
        sp.wait_ge(core.x_stats, (layer + 1) * B)
        sp.dma_start(numbers[:, :], ins["e16_numbers"].to_broadcast([P, E])).then_inc(numbers_loaded, 16)
        experts_sync(sp)

    programs["sync"] = sync
    return programs


RA_HEADS = 16
RA_DH = P // RA_HEADS
ROPE = RA_DH // 2
MASKED = -2.0 ** 100


def rotary_rows(a):
    by_head = a.reshape(RA_HEADS, RA_DH, *a.shape[1:])
    half = ROPE // 2
    return np.concatenate([by_head[:, half:ROPE], by_head[:, :half], by_head[:, ROPE:]], axis=1).reshape(a.shape)


def rotary_table():
    theta = (1.0 / np.float32(10000.0) ** (np.arange(0, ROPE, 2, dtype=np.float32) / ROPE)).astype(np.float32)
    angle = (np.arange(D, dtype=np.float32)[None, :] * theta[:, None]).astype(np.float32)
    head = np.zeros((RA_DH, 2, D), np.float32)
    head[:, 0] = 1.0
    for half, sign in ((0, -1.0), (ROPE // 2, 1.0)):
        head[half:half + ROPE // 2, 0] = np.cos(angle)
        head[half:half + ROPE // 2, 1] = sign * np.sin(angle)
    return np.tile(head, (RA_HEADS, 1, 1))


def rotary_attention_layer(nc, core, layer, ins, sb, sem):
    H = RA_HEADS
    xn = sb("ra_xn", [P, 4, D], F32)
    weights = sb("ra_weights", [P, 6, P], F32)
    biases = sb("ra_biases", [P, 5], F32)
    bv_row = sb("ra_bv_row", [1, P], F32)
    table = sb("ra_table", [P, 2, D], F32)
    mask_i = sb("ra_mask_i", [P, 2, DC, D], I32)
    mask = sb("ra_mask", [P, 2, DC, D], BF16)
    picks = sb("ra_picks", [P, 2, H // HB, P], F32)
    picks_r = sb("ra_picks_r", [P, 2, H // HB, P], F32R)
    picks_ready = sem("ra_picks_ready")
    own = sb("ra_own", [P, 2, 2, D], F32)
    partner = sb("ra_partner", [P, 2, 2, D], F32)
    rest = sb("ra_rest", [P, 2, D], F32)
    v_t = sb("ra_v_t", [P, B, DC, P], F32)
    qk3 = sb("ra_qk3", [P, B, 3, 2, D], BF16)
    weights_loaded, small_loaded = sem("ra_weights_loaded"), [sem(f"ra_small_loaded{i}") for i in range(5)]
    dve_step, pool_step, mask_ready = sem("ra_dve"), sem("ra_pool"), sem("ra_mask_ready")
    xn_ready, proj_done, proj_read, v_read = sem("ra_xn_ready"), sem("ra_proj_done"), sem("ra_proj_read"), sem("ra_v_read")
    turned_ready, rotated_used = sem("ra_turned_ready"), sem("ra_rotated_used")
    out_done, out_read = sem("ra_out_done"), sem("ra_out_read")
    att = HeadAttention(nc, core, sb, sem, "ra", H, float(RA_DH) ** -0.5, qk3[:, :, :, 0], qk3[:, :, :, 1],
                        lambda b, c: v_t[:, b, c, :], mask=(mask[:, 0], mask[:, 1]))
    att.out_read = out_read

    def bank(j, i):
        return core.psum[:, 3 * j + i, :].rearrange("p (a t) -> p a t", a=2)

    def out_ps():
        return core.psum[:, 6, 0:D]

    def sync(sp):
        sp.wait_ge(core.x_stats, (layer + 1) * B)
        sp.dma_start(weights[:], ins["ra_weights"]).then_inc(weights_loaded, 16)
        for s, (to, name) in zip(small_loaded, ((biases, "ra_biases"), (bv_row, "ra_bv"), (table, "ra_table"),
                                                (picks, "picks16"), (mask_i, "ra_mask"))):
            sp.dma_start(to[:], ins[name]).then_inc(s, 16)
        att.sync(sp)

    def gpsimd(pool):
        ch = Chain(pool, pool_step)
        for b in range(B):
            rstd_row(pool, ch, core, layer, b)
        pool.wait_ge(small_loaded[2], 16)
        for b in range(B):
            j = b % 2
            pool.wait_ge(proj_read, b + 1)
            for i in range(2):
                last = pool.tensor_tensor(partner[:, j, i], partner[:, j, i], table[:, 1], ALU.mult)
            last.then_inc(turned_ready, 1)
        pool.wait_ge(v_read, B)
        att.gpsimd(pool)

    def vector(dve):
        ch = Chain(dve, dve_step)
        att.vector_ones(dve)
        for b in range(B):
            dve.wait_ge(core.rstd_ready, layer * B + b + 1)
            if b >= 4:
                dve.wait_ge(proj_done, b - 3)
            dve.tensor_scalar(xn[:, b % 4], core.x_sb[:, b], core.mean_var[:, b, 0:1], core.rstd[:, b],
                              ALU.subtract, ALU.mult).then_inc(xn_ready, 1)
        dve.wait_ge(small_loaded[4], 16)
        dve.tensor_scalar(mask[:], mask_i[:], 0.0, MASKED, ALU.is_equal, ALU.mult).then_inc(mask_ready, 1)
        dve.wait_ge(small_loaded[2], 16)
        for b in range(B):
            j = b % 2
            dve.wait_ge(proj_read, b + 1)
            for i in range(2):
                last = ch.step(dve.tensor_tensor(own[:, j, i], own[:, j, i], table[:, 0], ALU.mult))
            ch.wait()
            dve.wait_ge(turned_ready, b + 1)
            ch.step(dve.tensor_tensor(own[:, j], own[:, j], partner[:, j], ALU.add))
            ch.wait()
            split_in_three(dve, ch, own[:, j], rest[:], [qk3[:, b, s] for s in range(3)])
            ch.wait()
            dve.sem_inc(rotated_used, 1)
            dve.sem_inc(att.pieces_ready, 1)
        dve.wait_ge(small_loaded[0], 16)

        def normalize(b):
            att.normalize(dve, ch, b)

        def add_to_x(b):
            dve.wait_ge(out_done, b + 1)
            dve.scalar_tensor_tensor(core.x_sb[:, b], out_ps(), biases[:, 4:5], core.x_sb[:, b], ALU.add, ALU.add)\
                .then_inc(out_read, 1)
            dve.wait_ge(out_read, b + 1)
            layer_norm_rows(dve, ch, core, b)

        att.vector(dve, ch, (normalize, add_to_x))

    def scalar(act):
        act.wait_ge(small_loaded[0], 16)
        for b in range(B):
            j = b % 2
            act.wait_ge(proj_done, b + 1)
            if b >= 2:
                act.wait_ge(rotated_used, b - 1)
            for to, i in ((own, 0), (partner, 1)):
                for a in range(2):
                    last = act.activation(to[:, j, a], bank(j, i)[:, a], ACT.Identity, bias=biases[:, 2 * i + a:2 * i + a + 1])
            last.then_inc(proj_read, 1)
            act.activation(v_t[:, b].rearrange("p c o -> p (c o)"), core.psum[:, 3 * j + 2, 0:DC * P], ACT.Copy).then_inc(v_read, 1)
        act.wait_ge(small_loaded[3], 16)
        act.activation(picks_r[:], picks[:], ACT.Copy).then_inc(picks_ready, 1)
        for b in range(B):
            att.exponentials(act, b)

    def tensor(pe):
        pe.wait_ge(weights_loaded, 16)
        pe.wait_ge(small_loaded[1], 16)
        for b in range(B):
            j = b % 2
            if b >= 2:
                pe.wait_ge(proj_read, b - 1)
                pe.wait_ge(v_read, b - 1)
            pe.wait_ge(xn_ready, b + 1)
            for i in range(2):
                for a, source in enumerate((xn, core.ctx)):
                    pe.matmul(bank(j, i)[:, a], weights[:, 2 * i + a, :], source[:, b % 4 if source is xn else b, :],
                              start=True, stop=True)
            for c in range(DC):
                v_ps = core.psum[:, 3 * j + 2, c * P:(c + 1) * P]
                pe.matmul(v_ps, core.ctx[:, b, c * P:(c + 1) * P], weights[:, 4, :], start=True, stop=False)
                last = pe.matmul(v_ps, core.ones[0:1, :], bv_row[:, :], start=False, stop=True)
            last.then_inc(proj_done, 1)
        pe.wait_ge(v_read, B)
        pe.wait_ge(picks_ready, 1)
        pe.wait_ge(mask_ready, 1)

        def after(b):
            pe.wait_ge(att.norm_ready, b + 1)
            pe.matmul(out_ps(), weights[:, 5, :], att.o_norm[:, b % 2, :], start=True, stop=True).then_inc(out_done, 1)

        att.tensor(pe, (picks_r[:, 0], picks_r[:, 1]), after)

    return dict(sync=sync, gpsimd=gpsimd, vector=vector, scalar=scalar, tensor=tensor)


class Core:
    pass


def build(nc, ins, out, layers):
    core = Core()
    with ExitStack() as ctx:
        def sem(name):
            return ctx.enter_context(nc.semaphore(name))

        def sb_of(stack):
            return lambda name, shape, dtype: stack.enter_context(nc.sbuf_tensor(name, shape, dtype))

        sb = sb_of(ctx)
        core.psum = ctx.enter_context(nc.psum_tensor("psum", [P, 8, 512], F32))
        core.x_sb = sb("x_sb", [P, B, D], F32)
        core.ctx = sb("ctx", [P, B, D], F32)
        core.ctx_t = sb("ctx_t", [P, DC, B, T], F32)
        core.ident = sb("ident", [P, P], F32)
        core.ident_bf = sb("ident_bf", [P, P], BF16)
        core.bn = sb("bn", [P, B, 6], F32)
        core.mean_var = sb("mean_var", [P, B, 2], F32)
        core.var_eps = sb("var_eps", [P, B, 1], F32)
        core.rstd = sb("rstd", [P, B, 1], F32)
        core.minus_half = sb("minus_half", [P, 1], F32)
        core.ones = sb("ones", [P, P], F32)
        core.x_loaded = [sem(f"x_loaded{i}") for i in range(B // 2)]
        core.ctx_loaded, core.ctx_t_loaded, core.const_loaded = sem("ctx_loaded"), sem("ctx_t_loaded"), sem("const_loaded")
        core.x_stats, core.rstd_ready = sem("x_stats"), sem("rstd_ready")
        core.consts_set, core.out_stored = sem("consts_set"), sem("out_stored")

        core.stats_step, core.ident_bf_ready = sem("stats_step"), sem("ident_bf_ready")

        for part in (range(0, min(SPLIT, len(layers))), range(SPLIT, len(layers))):
            if not part:
                continue
            begins, ends = part[0] == 0, part[-1] == len(layers) - 1
            if not begins:
                nc.all_engine_barrier()
                nc.clear_and_free_semaphores(used)
                nc.all_engine_barrier()
            semaphores = used = []

            def layer_sem(name):
                semaphores.append(nc.alloc_semaphore(name=name))
                return semaphores[-1]

            programs = []
            part_scope = ExitStack()
            keep = sb_of(part_scope)
            if part[0] == 0:
                core.fp8_weights = Fp8Weights(nc, core, ins, keep, layer_sem)
            for n in part:
                with ExitStack() as scope:
                    programs.append(layers[n](nc, core, n, ins, sb_of(scope), layer_sem))
            part_scope.close()

            with nc.Block() as block:

                @block.vector
                def _(dve):
                    if begins:
                        dve.memset(core.ones[:, :], 1.0).then_inc(core.consts_set, 1)
                        ch = Chain(dve, core.stats_step)
                        for b in range(B):
                            if b % 2 == 0:
                                dve.wait_ge(core.x_loaded[b // 2], 16)
                            layer_norm_rows(dve, ch, core, b)
                        dve.wait_ge(core.const_loaded, 16)
                        dve.tensor_copy(core.ident_bf[:, :], core.ident[:, :]).then_inc(core.ident_bf_ready, 1)
                    for p, layer in zip(programs, part):
                        if layer:
                            dve.wait_ge(core.x_stats, (layer + 1) * B)
                        p["vector"](nc.vector)

                @block.sync
                def _(sp):
                    if begins:
                        for i in range(B // 2):
                            sp.dma_start(core.x_sb[:, 2 * i:2 * i + 2, :], ins["x"][:, 2 * i:2 * i + 2, :]).then_inc(core.x_loaded[i], 16)
                        sp.dma_start(core.ident[:, :], ins["ident"]).then_inc(core.const_loaded, 16)
                        sp.dma_start(core.ctx_t[:], ins["ctx_t"]).then_inc(core.ctx_t_loaded, 16)
                        sp.dma_start(core.ctx[:], ins["ctx"]).then_inc(core.ctx_loaded, 16)
                        core.fp8_weights.sync(sp)
                    for p in programs:
                        p["sync"](nc.sync)
                    if ends:
                        sp.wait_ge(core.x_stats, (len(layers) + 1) * B)
                        sp.dma_start(out, core.x_sb[:]).then_inc(core.out_stored, 16)
                        sp.wait_ge(core.out_stored, 16)

                @block.gpsimd
                def _(pool):
                    if begins:
                        pool.memset(core.minus_half[:, :], -0.5).then_inc(core.consts_set, 1)
                        pool.wait_ge(core.consts_set, 2)
                    for p, layer in zip(programs, part):
                        if layer:
                            pool.wait_ge(core.x_stats, (layer + 1) * B)
                        p["gpsimd"](nc.gpsimd)
                        if layer == 0:
                            core.fp8_weights.gather(nc.gpsimd)

                @block.scalar
                def _(act):
                    for p, layer in zip(programs, part):
                        if layer:
                            act.wait_ge(core.x_stats, (layer + 1) * B)
                        p["scalar"](nc.scalar)

                @block.tensor
                def _(pe):
                    if begins:
                        pe.wait_ge(core.consts_set, 2)
                    for p, layer in zip(programs, part):
                        if layer:
                            pe.wait_ge(core.x_stats, (layer + 1) * B)
                        p["tensor"](nc.tensor)


def head_picks(heads):
    width = P // heads
    picks = np.zeros((P, 2, heads // HB, P), np.float32)
    for h in range(heads):
        for d in range(width):
            for part in range(2):
                picks[32 * (h % HB) + part * width + d, part, h // HB, h * width + d] = 1.0
    return picks


def pack_experts(gate, up, down):
    by_chunk = [w.reshape(len(w), DC, P, P).transpose(0, 2, 1, 3).reshape(len(w), P, DC * P) for w in (gate, up)]
    return np.concatenate([*by_chunk, down], axis=2)


def layouts(inputs):
    a = {k: np.asarray(v) for k, v in inputs.items()}
    x, ctx, mask = a["x"], a["ctx_2048"], a["mask_1x1x2048x2048_if1"].reshape(D, D)
    return {
        "x": x.transpose(1, 0, 2),
        "ctx": ctx.transpose(1, 0, 2),
        "ctx_t": ctx.transpose(2, 0, 1).reshape(DC, P, B, T).transpose(1, 0, 2, 3),
        "td": a["L0_xattn_time_decay"].reshape(DC, P).T,
        "tf": a["L0_xattn_time_first"].reshape(DC, P).T,
        "w1_t": a["L0_ffn_w1"].T.reshape(DC, P, FF).transpose(1, 0, 2),
        "w2_t": a["L0_ffn_w2"].T.reshape(FC, P, D).transpose(1, 0, 2),
        "b1": a["L0_ffn_b1"].reshape(1, FF),
        "b2": a["L0_ffn_b2"].reshape(1, D),
        "f8_idx": a["L1_ffn_down_reorder_index"][:F8 // P * P].reshape(F8 // P, P).T,
        "f8_idx_rest": a["L1_ffn_down_reorder_index"][F8 // P * P:].reshape(F8 % P, 1),
        "f8_gate": a["L1_ffn_w_gate"],
        "f8_up": a["L1_ffn_w_up"],
        "f8_down": a["L1_ffn_w_down"],
        "mask_mem": a["mask_BxS2_bk0"].reshape(1, B * T),
        "e64_router": a["L2_ffn_w_router"],
        "e64_experts": pack_experts(a["L2_ffn_w_gate"], a["L2_ffn_w_up"], a["L2_ffn_w_down"]),
        "e16_router": a["L3_ffn_gate_w"].T,
        "e16_experts": pack_experts(a["L3_ffn_gate_up_proj"][:, :, :P], a["L3_ffn_gate_up_proj"][:, :, P:], a["L3_ffn_down_proj"]),
        "e16_numbers": np.arange(16, dtype=np.float32).reshape(1, 16),
        "ra_weights": np.stack([a["L3_xattn_wq"].T, a["L3_xattn_wk"].T, rotary_rows(a["L3_xattn_wq"]).T,
                                rotary_rows(a["L3_xattn_wk"]).T, a["L3_xattn_wv"].T, a["L3_xattn_wo"].T], axis=1),
        "ra_biases": np.stack([a["L3_xattn_bq"], a["L3_xattn_bk"], rotary_rows(a["L3_xattn_bq"]),
                               rotary_rows(a["L3_xattn_bk"]), a["L3_xattn_bo"]], axis=1),
        "ra_bv": a["L3_xattn_bv"].reshape(1, P),
        "ra_table": rotary_table(),
        "ra_mask": np.stack([m.reshape(DC, P, D).transpose(1, 0, 2) for m in (mask, mask.T)], axis=1),
        "picks8": head_picks(8),
        "picks16": head_picks(16),
        "ident": np.eye(P, dtype=np.float32),
    }


SPLIT = 5
LAYERS = [wkv_layer, ternary_ffn_layer, channel_attention_layer, fp8_ffn_layer, memory_attention_layer, top8_experts_layer, rotary_attention_layer, top2_experts_layer]


def kernel(**inputs):
    import concourse.bacc as bacc
    from concourse.bass_utils import run_bass_kernel_spmd

    nc = bacc.Bacc("TRN2", target_bir_lowering=False, num_devices=1)
    arrays = {f"in_{name}": np.ascontiguousarray(a) for name, a in layouts(inputs).items()}
    ins = {name[3:]: nc.dram_tensor(name, a.shape, mybir.dt.from_np(a.dtype), kind="ExternalInput").ap()
           for name, a in arrays.items()}
    out = nc.dram_tensor("out_0", (T, B, D), F32, kind="ExternalOutput").ap()
    build(nc, ins, out, LAYERS)
    result = run_bass_kernel_spmd(nc, [arrays], core_ids=[0])
    return result.results[0]["out_0"].transpose(1, 0, 2)
```

```python
from contextlib import ExitStack

import numpy as np
import concourse.bass as bass
from concourse import mybir

F32 = mybir.dt.float32
F32R = mybir.dt.float32r
BF16 = mybir.dt.bfloat16
I32 = mybir.dt.int32
U8 = mybir.dt.uint8
ALU = mybir.AluOpType
ACT = mybir.ActivationFunctionType
AXX = mybir.AxisListType.X

P = 128
B, T, D = 8, 128, 256
DC = D // P
EPS = 1e-5
ROUND = 1.5 * 2.0 ** 23
LOWEST = -1e38
FF = 1024
FC = FF // P


class Chain:

    def __init__(self, engine, semaphore, start=0):
        self.engine, self.semaphore, self.value = engine, semaphore, start

    def step(self, instruction):
        instruction.then_inc(self.semaphore, 1)
        self.value = self.value + 1
        return self

    def wait(self):
        self.engine.wait_ge(self.semaphore, self.value)


def layer_norm_rows(dve, chain, core, b):
    chain.step(dve.bn_stats(core.bn[:, b, :], core.x_sb[:, b, :]))
    chain.wait()
    dve.bn_aggr(core.mean_var[:, b, :], core.bn[:, b, :]).then_inc(core.x_stats, 1)


def rstd_row(pool, chain, core, layer, b, scale=1.0, shift=EPS):
    pool.wait_ge(core.x_stats, layer * B + b + 1)
    chain.step(pool.tensor_scalar(core.var_eps[:, b, :], core.mean_var[:, b, 1:2], scale, shift, ALU.mult, ALU.add))
    chain.wait()
    pool.tensor_tensor(core.rstd[:, b, :], core.var_eps[:, b, :], core.minus_half[:, 0:1], ALU.pow)\
        .then_inc(core.rstd_ready, 1)


def wkv_layer(nc, core, layer, ins, sb, sem):
    TP = T + 1
    k_pad = sb("wkv_k", [P, DC, B, TP], F32)
    decay = sb("wkv_decay", [P, DC, B, TP], F32)
    peak = sb("wkv_peak", [P, DC, B, TP], F32)
    e_old = sb("wkv_e_old", [P, B, TP], F32)
    e_new = sb("wkv_e_new", [P, B, TP], F32)
    ev_new = sb("wkv_ev_new", [P, B, TP], F32)
    aa = sb("wkv_aa", [P, B, TP], F32)
    bb = sb("wkv_bb", [P, B, TP], F32)
    d_old = sb("wkv_d_old", [P, B, T], F32)
    d_new = sb("wkv_d_new", [P, B, T], F32)
    q_max = sb("wkv_q_max", [P, B, T], F32)
    o_old = sb("wkv_o_old", [P, B, T], F32)
    o_bb = sb("wkv_o_bb", [P, B, T], F32)
    o_new = sb("wkv_o_new", [P, B, T], F32)
    ov_new = sb("wkv_ov_new", [P, B, T], F32)
    recip = sb("wkv_recip", [P, B, T], F32)
    y_t = sb("wkv_y", [P, DC, B, T], F32)
    xn = sb("wkv_xn", [P, B, D], F32)
    td_tf = sb("wkv_td_tf", [P, 2, DC], F32)
    w_exp = sb("wkv_w_exp", [P, DC], F32)

    td_loaded, dve_step, act_step, pool_step = sem("wkv_td_loaded"), sem("wkv_dve"), sem("wkv_act"), sem("wkv_pool")
    xn_ready, xn_turned, k_ready = sem("wkv_xn_ready"), sem("wkv_xn_turned"), sem("wkv_k_ready")
    decay_written = sem("wkv_decay_written")
    w_ready, decay_ready = sem("wkv_w_ready"), sem("wkv_decay_ready")
    diff_ready, exp_ready, new_v_ready = sem("wkv_diff_ready"), sem("wkv_exp_ready"), sem("wkv_new_v_ready")
    y_ready, y_turned, chunk_done = sem("wkv_y_ready"), sem("wkv_y_turned"), sem("wkv_chunk_done")

    def turned(c):
        return core.psum[:, 2 * c:2 * c + 2, :].rearrange("p n (b t) -> p (n b) t", t=T)

    def y_rows(b):
        return core.psum[:, 4 + b // 2, (b % 2) * D:(b % 2 + 1) * D]

    def sync(sp):
        sp.dma_start(td_tf[:, 0, :], ins["td"]).then_inc(td_loaded, 16)
        sp.dma_start(td_tf[:, 1, :], ins["tf"]).then_inc(td_loaded, 16)

    def gpsimd(pool):
        ch = Chain(pool, pool_step)
        ch.step(pool.memset(e_new[:, :, :], 0.0))
        ch.step(pool.memset(k_pad[:, :, :, 0:1], LOWEST))
        ch.step(pool.memset(e_old[:, :, 0:1], 0.0))
        for b in range(B):
            rstd_row(pool, ch, core, layer, b)
        pool.wait_ge(decay_written, DC)
        pool.memset(decay[:, :, :, 0:1], 2 * LOWEST).then_inc(decay_ready, 1)
        pool.wait_ge(core.ctx_t_loaded, 16)
        for c in range(DC):
            v = core.ctx_t[:, c, :, :]
            pool.wait_ge(exp_ready, 4 * c + 2)
            if c:
                pool.wait_ge(dve_step, core.wkv_scanned_aa)
            ch.step(pool.tensor_tensor(ev_new[:, :, 1:TP], e_new[:, :, 1:TP], v, ALU.mult))
            pool.memset(ev_new[:, :, 0:1], 0.0).then_inc(new_v_ready, 1)
            pool.wait_ge(exp_ready, 4 * c + 4)
            pool.tensor_tensor(ov_new[:, :, :], o_new[:, :, :], v, ALU.mult).then_inc(new_v_ready, 1)
            if c == 0:
                core.fp8_weights.gather(pool)
        core.context_pieces.gpsimd(pool, range(5))

    def vector(dve):
        ch = Chain(dve, dve_step)
        for b in range(B):
            dve.wait_ge(core.rstd_ready, layer * B + b + 1)
            dve.tensor_scalar(xn[:, b, :], core.x_sb[:, b, :], core.mean_var[:, b, 0:1], core.rstd[:, b, :],
                              ALU.subtract, ALU.mult).then_inc(xn_ready, 1)
        dve.wait_ge(k_ready, 0 + 4)
        dve.tensor_scalar(w_exp[:, :], w_exp[:, :], -1.0, None, ALU.mult).then_inc(w_ready, 1)
        dve.wait_ge(decay_ready, 1)
        dve.wait_ge(td_loaded, 32)
        for c in range(DC):
            u, w = td_tf[:, 1, c:c + 1], w_exp[:, c:c + 1]
            k, pp, pp_next = k_pad[:, c, :, 1:TP], peak[:, c, :, 0:T], peak[:, c, :, 1:TP]
            ch.step(dve.tensor_tensor_scan(peak[:, c].rearrange("p b t -> p (b t)"), decay[:, c].rearrange("p b t -> p (b t)"),
                                           k_pad[:, c].rearrange("p b t -> p (b t)"), LOWEST, ALU.add, ALU.max))
            ch.wait()
            if c:
                dve.wait_ge(exp_ready, 4 * c)
            dve.scalar_tensor_tensor(d_old[:, :, :], pp, w, pp_next, ALU.add, ALU.subtract).then_inc(diff_ready, 1)
            dve.tensor_tensor(d_new[:, :, :], k, pp_next, ALU.subtract).then_inc(diff_ready, 1)
            ch.step(dve.scalar_tensor_tensor(q_max[:, :, :], k, u, pp, ALU.add, ALU.max))
            ch.wait()
            dve.wait_ge(exp_ready, 4 * c + 2)
            dve.tensor_tensor(d_old[:, :, :], pp, q_max[:, :, :], ALU.subtract).then_inc(diff_ready, 1)
            dve.scalar_tensor_tensor(d_new[:, :, :], k, u, q_max[:, :, :], ALU.add, ALU.subtract).then_inc(diff_ready, 1)
            ch.step(dve.tensor_tensor_scan(bb[:].rearrange("p b t -> p (b t)"), e_old[:].rearrange("p b t -> p (b t)"),
                                           e_new[:].rearrange("p b t -> p (b t)"), 0.0, ALU.mult, ALU.add))
            ch.wait()
            dve.wait_ge(exp_ready, 4 * c + 4)
            ch.step(dve.tensor_tensor(o_bb[:, :, :], o_old[:, :, :], bb[:, :, 0:T], ALU.mult))
            ch.wait()
            ch.step(dve.tensor_tensor(o_bb[:, :, :], o_bb[:, :, :], o_new[:, :, :], ALU.add))
            if c == 1:
                core.ternary_weights.vector(dve, ch)
            ch.wait()
            ch.step(dve.reciprocal(recip[:, :, :], o_bb[:, :, :]))
            dve.wait_ge(new_v_ready, 2 * c + 1)
            ch.step(dve.tensor_tensor_scan(aa[:].rearrange("p b t -> p (b t)"), e_old[:].rearrange("p b t -> p (b t)"),
                                           ev_new[:].rearrange("p b t -> p (b t)"), 0.0, ALU.mult, ALU.add))
            ch.wait()
            if c == 0:
                core.wkv_scanned_aa = ch.value
            ch.step(dve.tensor_tensor(o_old[:, :, :], o_old[:, :, :], aa[:, :, 0:T], ALU.mult))
            ch.wait()
            dve.wait_ge(new_v_ready, 2 * c + 2)
            ch.step(dve.tensor_tensor(o_old[:, :, :], o_old[:, :, :], ov_new[:, :, :], ALU.add))
            ch.wait()
            dve.tensor_tensor(y_t[:, c], o_old[:, :, :], recip[:, :, :], ALU.mult).then_inc(y_ready, 1)
        core.ternary_weights.clip(dve)
        for b in range(B):
            if b % 2 == 0:
                dve.wait_ge(y_turned, b // 2 + 1)
            ch.step(dve.tensor_tensor(core.x_sb[:, b, :], core.x_sb[:, b, :], y_rows(b), ALU.add))
            ch.wait()
            layer_norm_rows(dve, ch, core, b)

    def scalar(act):
        act.wait_ge(td_loaded, 32)
        act.activation(w_exp[:, :], td_tf[:, 0, :], ACT.Exp).then_inc(act_step, 1)
        act.wait_ge(pool_step, 2)
        for half in range(2):
            act.wait_ge(xn_turned, half + 1)
            for c in range(DC):
                act.activation(k_pad[:, c, 4 * half:4 * half + 4, 1:TP], turned(c)[:, 4 * half:4 * half + 4, :],
                               ACT.Copy).then_inc(k_ready, 1)
        act.wait_ge(w_ready, 1)
        for c in range(DC):
            act.activation(decay[:, c], e_new[:, :, :], ACT.Identity, bias=w_exp[:, c:c + 1]).then_inc(decay_written, 1)
        for c in range(DC):
            if c:
                act.wait_ge(y_ready, c)
            act.wait_ge(diff_ready, 4 * c + 1)
            act.activation(e_old[:, :, 1:TP], d_old[:, :, :], ACT.Exp).then_inc(exp_ready, 1)
            act.wait_ge(diff_ready, 4 * c + 2)
            act.activation(e_new[:, :, 1:TP], d_new[:, :, :], ACT.Exp).then_inc(exp_ready, 1)
            act.wait_ge(diff_ready, 4 * c + 3)
            act.activation(o_old[:, :, :], d_old[:, :, :], ACT.Exp).then_inc(exp_ready, 1)
            act.wait_ge(diff_ready, 4 * c + 4)
            act.activation(o_new[:, :, :], d_new[:, :, :], ACT.Exp).then_inc(exp_ready, 1)
            if c == 0:
                core.ternary_weights.scalar(act)
        core.ternary_weights.round_up(act)
        core.ternary_weights.round_down(act)

    def tensor(pe):
        pe.wait_ge(core.const_loaded, 16)
        for b in range(B):
            pe.wait_ge(xn_ready, b + 1)
            for c in range(DC):
                last = pe.transpose(turned(c)[:, b, :], xn[:, b, c * P:(c + 1) * P], core.ident[:, :])
            if b % 4 == 3:
                last.then_inc(xn_turned, 1)
        pe.wait_ge(k_ready, 4)
        core.ternary_weights.tensor(pe)
        pe.wait_ge(y_ready, DC)
        for b in range(B):
            for c in range(DC):
                last = pe.transpose(y_rows(b)[:, c * P:(c + 1) * P], y_t[:, c, b, :], core.ident[:, :])
            if b % 2:
                last.then_inc(y_turned, 1)

    return dict(sync=sync, gpsimd=gpsimd, vector=vector, scalar=scalar, tensor=tensor)


class TernaryWeights:

    PIECES = 4

    def __init__(self, nc, core, ins, sb, sem):
        self.core, self.ins = core, ins
        self.w = [sb("w1", [P, DC * FF], F32), sb("w2", [P, FC * D], F32)]
        self.w_abs = sb("w_abs", [P, DC * FF // self.PIECES], F32)
        self.w1_q = sb("w1_q", [P, DC, FF], BF16)
        self.w2_q = sb("w2_q", [P, FC, D], BF16)
        self.sums = sb("w_sums", [P, self.PIECES, 2], F32)
        self.scale = sb("w_scale", [P, 2], F32)
        self.inv = sb("w_inv", [P, 2], F32)
        self.loaded = [sem("bf_w1_loaded"), sem("bf_w2_loaded")]
        self.sum_step, self.totals_ready, self.inv_ready = sem("bf_sum_step"), sem("bf_totals"), sem("bf_inv")
        self.rounds = sb("bf_rounds", [P, 2], F32)
        self.rounds_set, self.rounded, self.clipped, self.ready = (
            sem("bf_rounds_set"), sem("bf_rounded"), sem("bf_clipped"), sem("bf_w_ready"))

    def sync(self, sp):
        for w, name, loaded in zip(self.w, ("w1_t", "w2_t"), self.loaded):
            sp.dma_start(w[:, :], self.ins[name].rearrange("p a b -> p (a b)")).then_inc(loaded, 16)

    def totals_ps(self):
        return self.core.psum[:, 0, 0:2]

    def scalar(self, act):
        ch = Chain(act, self.sum_step)
        for i, w in enumerate(self.w):
            act.wait_ge(self.loaded[i], 16)
            for n in range(self.PIECES):
                size = self.w_abs.shape[-1]
                if i or n:
                    ch.wait()
                ch.step(act.activation(self.w_abs[:, :], w[:, n * size:(n + 1) * size], ACT.Abs,
                                       accum_out=self.sums[:, n, i:i + 1]))

    def tensor(self, pe):
        pe.wait_ge(self.sum_step, 2 * self.PIECES)
        for n in range(self.PIECES):
            last = pe.matmul(self.totals_ps(), self.core.ones[:, :], self.sums[:, n, :], start=(n == 0), stop=(n == self.PIECES - 1))
        last.then_inc(self.totals_ready, 1)

    def vector(self, dve, ch):
        ch.step(dve.memset(self.rounds[:, 0:1], ROUND))
        ch.step(dve.memset(self.rounds[:, 1:2], -ROUND))
        ch.wait()
        dve.sem_inc(self.rounds_set, 1)
        dve.wait_ge(self.totals_ready, 1)
        ch.step(dve.tensor_scalar(self.scale[:, :], self.totals_ps(), 1.0 / (FF * D), 1e-8, ALU.mult, ALU.max))
        ch.wait()
        dve.reciprocal(self.inv[:, :], self.scale[:, :]).then_inc(self.inv_ready, 1)

    def round_up(self, act):
        act.wait_ge(self.rounds_set, 1)
        act.wait_ge(self.inv_ready, 1)
        for i, w in enumerate(self.w):
            act.activation(w[:, :], w[:, :], ACT.Identity, bias=self.rounds[:, 0:1], scale=self.inv[:, i:i + 1])\
                .then_inc(self.rounded, 1)

    def clip(self, dve):
        for i, w in enumerate(self.w):
            dve.wait_ge(self.rounded, i + 1)
            dve.tensor_scalar(w[:, :], w[:, :], ROUND + 1.0, ROUND - 1.0, ALU.min, ALU.max).then_inc(self.clipped, 1)

    def round_down(self, act):
        for i, (w, q) in enumerate(zip(self.w, (self.w1_q, self.w2_q))):
            act.wait_ge(self.clipped, i + 1)
            act.activation(q[:].rearrange("p a b -> p (a b)"), w[:, :], ACT.Identity, bias=self.rounds[:, 1:2])\
                .then_inc(self.ready, 1)


def ternary_ffn_layer(nc, core, layer, ins, sb, sem):
    weights = core.ternary_weights
    w1_q, w2_q, w_scale = weights.w1_q, weights.w2_q, weights.scale
    b1 = sb("b1_rows", [P, FF], F32)
    b2 = sb("b2_rows", [P, D], F32)
    xc = sb("bf_xc", [P, B, D], F32)
    xq = sb("bf_xq", [P, B, D], BF16)
    xq_t = sb("bf_xq_t", [P, 2, DC, P], BF16)
    stat = sb("bf_stat", [P, 3, B], F32)
    stat2 = sb("bf_stat2", [P, 2, 8], F32)
    back1 = sb("bf_back1", [P, B], F32)
    back2 = sb("bf_back2", [P, 2, 1], F32)
    h = sb("bf_h", [P, 2, FF], F32)
    g = sb("bf_g", [P, 2, FF], F32)
    gc = sb("bf_gc", [P, 2, FF], F32)
    a_t = sb("bf_a_t", [P, 2, FC, P], BF16)
    bn2 = sb("bf_bn2", [P, 2, 2, 6], F32)
    mv2 = sb("bf_mv2", [P, 2, 2], F32)
    ve2 = sb("bf_ve2", [P, 2, 1], F32)
    r2 = sb("bf_r2", [P, 2, 1], F32)
    neg_mean = sb("bf_neg_mean", [P, 2, 1], F32)
    out_rows = sb("bf_out", [P, 2, D], F32)

    loaded = [sem(f"bf_loaded{i}") for i in range(2)]
    dve_step, pool_step = sem("bf_dve"), sem("bf_pool")
    xq_ready, xq_turned, xq_t_ready, h_done = sem("bf_xq_ready"), sem("bf_xq_turned"), sem("bf_xq_t_ready"), sem("bf_h_done")
    h_ready, g_ready, mv_ready, r2_ready, mean_ready, gc_ready = (
        sem("bf_h_ready"), sem("bf_g_ready"), sem("bf_mv_ready"), sem("bf_r2_ready"), sem("bf_mean_ready"), sem("bf_gc_ready"))
    aq_ready, a_turned, a_t_ready, y_done = sem("bf_aq_ready"), sem("bf_a_turned"), sem("bf_a_t_ready"), sem("bf_y_done")

    def h_ps(j):
        return core.psum[:, 2 * j:2 * j + 2, :].rearrange("p n f -> p (n f)")

    a_ps = core.psum[:, 4:6, :].rearrange("p n (k t) -> p (n k) t", t=P)
    xq_ps = core.psum[:, 6, :].bitcast(BF16)
    y_ps = core.psum[:, 7, 0:D]

    def sync(sp):
        sp.wait_ge(core.x_stats, (layer + 1) * B)
        sp.dma_start(b1[:, :], ins["b1"].to_broadcast([P, FF])).then_inc(loaded[0], 16)
        sp.dma_start(b2[:, :], ins["b2"].to_broadcast([P, D])).then_inc(loaded[1], 16)
        core.context_pieces.sync(sp)

    def gpsimd(pool):
        ch = Chain(pool, pool_step)
        for b in range(B):
            rstd_row(pool, ch, core, layer, b, 1.0 + EPS, EPS * EPS)
        core.context_pieces.gpsimd(pool, range(5, B))
        for b in range(B):
            j = b % 2
            pool.wait_ge(mv_ready, b + 1)
            ch.step(pool.tensor_scalar(ve2[:, j, :], mv2[:, j, 1:2], EPS, None, ALU.add))
            ch.wait()
            pool.tensor_tensor(r2[:, j, :], ve2[:, j, :], core.minus_half[:, 0:1], ALU.pow).then_inc(r2_ready, 1)

    def scales(dve, ch, st, absmax, rstd, back, w_scale_col):
        ch.step(dve.tensor_scalar(st[:, 1:2], absmax, rstd, 1e-5, ALU.mult, ALU.max))
        ch.wait()
        ch.step(dve.reciprocal(st[:, 3:4], st[:, 1:2]))
        ch.step(dve.tensor_scalar(back, st[:, 1:2], w_scale_col, 1.0 / 127.0, ALU.mult, ALU.mult))
        ch.wait()
        ch.step(dve.tensor_scalar(st[:, 2:3], st[:, 3:4], rstd, 127.0, ALU.mult, ALU.mult))
        ch.wait()

    def vector(dve):
        ch = Chain(dve, dve_step)
        def quantize_x(first, count):
            tiles = slice(first, first + count)
            rstd = core.rstd[:, tiles, 0]
            for b in range(first, first + count):
                ch.step(dve.tensor_scalar(xc[:, b, :], core.x_sb[:, b, :], core.mean_var[:, b, 0:1], None, ALU.subtract))
            ch.wait()
            ch.step(dve.tensor_reduce(stat[:, 0, tiles], xc[:, tiles, :], AXX, ALU.max, apply_absolute_value=True))
            ch.wait()
            dve.wait_ge(core.rstd_ready, layer * B + first + count)
            ch.step(dve.tensor_tensor(stat[:, 1, tiles], stat[:, 0, tiles], rstd, ALU.mult))
            ch.wait()
            ch.step(dve.tensor_scalar(stat[:, 1, tiles], stat[:, 1, tiles], 1e-5, None, ALU.max))
            ch.wait()
            ch.step(dve.reciprocal(stat[:, 2, tiles], stat[:, 1, tiles]))
            ch.step(dve.tensor_scalar(back1[:, tiles], stat[:, 1, tiles], w_scale[:, 0:1], 1.0 / 127.0, ALU.mult, ALU.mult))
            ch.wait()
            ch.step(dve.scalar_tensor_tensor(stat[:, 2, tiles], stat[:, 2, tiles], 127.0, rstd, ALU.mult, ALU.mult))
            ch.wait()
            for b in range(first, first + count):
                ch.step(dve.tensor_scalar(xc[:, b, :], xc[:, b, :], stat[:, 2, b:b + 1], ROUND, ALU.mult, ALU.add))
            ch.wait()
            dve.tensor_scalar(xq[:, tiles, :], xc[:, tiles, :], ROUND, None, ALU.subtract).then_inc(xq_ready, 1)

        def add_bias(b):
            j = b % 2
            dve.wait_ge(h_done, b + 1)
            if b >= 2:
                dve.wait_ge(g_ready, b - 1)
            dve.scalar_tensor_tensor(h[:, j, :], h_ps(j), back1[:, b:b + 1], b1[:, :], ALU.mult, ALU.add).then_inc(h_ready, 1)

        def quantize_inner(b):
            j = b % 2
            dve.wait_ge(g_ready, b + 1)
            for n in range(2):
                ch.step(dve.bn_stats(bn2[:, j, n, :], g[:, j, n * 512:(n + 1) * 512]))
            ch.wait()
            if b >= 2:
                dve.wait_ge(gc_ready, b - 1)
            dve.bn_aggr(mv2[:, j, :], bn2[:, j].rearrange("p a b -> p (a b)")).then_inc(mv_ready, 1)
            dve.wait_ge(mv_ready, b + 1)
            dve.tensor_scalar(neg_mean[:, j, :], mv2[:, j, 0:1], -1.0, None, ALU.mult).then_inc(mean_ready, 1)
            dve.wait_ge(gc_ready, b + 1)
            ch.step(dve.tensor_reduce(stat2[:, j, 0:1], gc[:, j, :], AXX, ALU.max, apply_absolute_value=True))
            ch.wait()
            dve.wait_ge(r2_ready, b + 1)
            scales(dve, ch, stat2[:, j, :], stat2[:, j, 0:1], r2[:, j, :], back2[:, j, :], w_scale[:, 1:2])
            dve.tensor_scalar(gc[:, j, :], gc[:, j, :], stat2[:, j, 2:3], ROUND, ALU.mult, ALU.add).then_inc(aq_ready, 1)

        def add_to_x(b):
            j = b % 2
            dve.wait_ge(y_done, b + 1)
            ch.step(dve.scalar_tensor_tensor(out_rows[:, j, :], y_ps, back2[:, j, :], b2[:, :], ALU.mult, ALU.add))
            ch.wait()
            ch.step(dve.tensor_tensor(core.x_sb[:, b, :], core.x_sb[:, b, :], out_rows[:, j, :], ALU.add))
            ch.wait()
            layer_norm_rows(dve, ch, core, b)

        dve.wait_ge(loaded[0], 16)
        dve.wait_ge(loaded[1], 16)
        quantize_x(0, 2)
        add_bias(0)
        for b in range(B):
            if b + 1 < B:
                add_bias(b + 1)
            if b == 0:
                quantize_x(2, B - 2)
            quantize_inner(b)
            if b:
                add_to_x(b - 1)
        add_to_x(B - 1)

    def scalar(act):
        def turned_x(b):
            act.wait_ge(xq_turned, b + 1)
            if b >= 2:
                act.wait_ge(h_done, b - 1)
            act.activation(xq_t[:, b % 2].rearrange("p a b -> p (a b)"), xq_ps[:, 0:D], ACT.Copy).then_inc(xq_t_ready, 1)

        def gelu(b):
            j = b % 2
            act.wait_ge(h_ready, b + 1)
            if b >= 2:
                act.wait_ge(gc_ready, b - 1)
            act.activation(g[:, j, :], h[:, j, :], ACT.Gelu).then_inc(g_ready, 1)

        def center(b):
            j = b % 2
            act.wait_ge(mean_ready, b + 1)
            if b >= 2:
                act.wait_ge(a_turned, b - 1)
            act.activation(gc[:, j, :], g[:, j, :], ACT.Identity, bias=neg_mean[:, j, :]).then_inc(gc_ready, 1)

        def turned_inner(b):
            act.wait_ge(a_turned, b + 1)
            if b >= 2:
                act.wait_ge(y_done, b - 1)
            act.activation(a_t[:, b % 2].rearrange("p a b -> p (a b)"), a_ps.rearrange("p a b -> p (a b)"),
                           ACT.Identity, bias=weights.rounds[:, 1:2]).then_inc(a_t_ready, 1)

        turned_x(0)
        turned_x(1)
        gelu(0)
        for b in range(B):
            center(b)
            if b + 2 < B:
                turned_x(b + 2)
            if b + 1 < B:
                gelu(b + 1)
            turned_inner(b)

    def tensor(pe):
        def turn_x(b):
            pe.wait_ge(xq_ready, 1 if b < 2 else 2)
            if b:
                pe.wait_ge(xq_t_ready, b)
            for c in range(DC):
                last = pe.transpose(xq_ps[:, c * P:(c + 1) * P], xq[:, b, c * P:(c + 1) * P], core.ident_bf[:, :])
            last.then_inc(xq_turned, 1)

        def product1(b):
            j = b % 2
            pe.wait_ge(xq_t_ready, b + 1)
            if b >= 2:
                pe.wait_ge(h_ready, b - 1)
            for n in range(2):
                for c in range(DC):
                    last = pe.matmul(h_ps(j)[:, n * 512:(n + 1) * 512], xq_t[:, j, c, :], w1_q[:, c, n * 512:(n + 1) * 512],
                                     start=(c == 0), stop=(c == DC - 1))
            last.then_inc(h_done, 1)

        def turn_inner(b):
            pe.wait_ge(aq_ready, b + 1)
            if b:
                pe.wait_ge(a_t_ready, b)
            for k in range(FC):
                last = pe.transpose(a_ps[:, k, :], gc[:, b % 2, k * P:(k + 1) * P], core.ident[:, :])
            last.then_inc(a_turned, 1)

        def product2(b):
            pe.wait_ge(a_t_ready, b + 1)
            if b:
                pe.wait_ge(core.x_stats, (layer + 1) * B + b)
            for k in range(FC):
                last = pe.matmul(y_ps, a_t[:, b % 2, k, :], w2_q[:, k, :], start=(k == 0), stop=(k == FC - 1))
            last.then_inc(y_done, 1)

        pe.wait_ge(core.ident_bf_ready, 1)
        turn_x(0)
        pe.wait_ge(weights.ready, 2)
        product1(0)
        turn_x(1)
        product1(1)
        for b in range(B):
            if b + 2 < B:
                turn_x(b + 2)
                product1(b + 2)
            turn_inner(b)
            product2(b)

    return dict(sync=sync, gpsimd=gpsimd, vector=vector, scalar=scalar, tensor=tensor)


Q_PIECE = (0, 1, 2, 0, 1, 0)
K_PIECE = (0, 0, 0, 1, 1, 2)
SLOTS = len(Q_PIECE)
SLOT_RUNS = ((0, 3), (3, 2), (5, 1))
RING = 3
HB = 4


def split_in_three(dve, ch, full, rest, pieces):
    ch.step(dve.tensor_copy(pieces[0], full))
    ch.wait()
    ch.step(dve.tensor_tensor(rest, full, pieces[0], ALU.subtract))
    ch.wait()
    ch.step(dve.tensor_copy(pieces[1], rest))
    ch.wait()
    ch.step(dve.tensor_tensor(pieces[2], rest, pieces[1], ALU.subtract))


class HeadAttention:

    def __init__(self, nc, core, sb, sem, name, heads, scale, q3, k3, v_t, mask=None, k_dram=None):
        self.core, self.H, self.scale, self.v_t, self.mask = core, heads, scale, v_t, mask
        self.out_read = None
        self.DH = DH = P // heads
        self.q3, self.k3 = q3, k3
        self.K = K = SLOTS * DH
        self.NB = heads // HB
        self.LEAD, self.TURN_AT = 4, 2 * self.NB - 3
        self.q_dram = nc.dram_tensor(f"{name}_q_pieces", [B, 3, DH, heads, D], BF16, kind="Internal").ap()
        self.k_stored = k_dram is not None
        self.k_dram = k_dram if self.k_stored else nc.dram_tensor(f"{name}_k_pieces", [B, 3, DH, heads, D], BF16, kind="Internal").ap()
        self.qs = sb(f"{name}_qs", [K + 3, RING, heads, D], BF16)
        self.ks = sb(f"{name}_ks", [K + 3, RING, heads, D], BF16)
        self.ones_row = sb(f"{name}_ones_row", [3, D], BF16)
        self.v_ones = sb(f"{name}_v_ones", [P, 2, DC, heads, 32], F32)
        self.peak = sb(f"{name}_peak", [P, 2, heads, DC], F32)
        self.peak_rest = sb(f"{name}_peak_rest", [P, heads, DC], F32)
        self.peak3 = sb(f"{name}_peak3", [P, 3, heads, DC], BF16)
        self.peak_rows = sb(f"{name}_peak_rows", [3 * heads * DC, 2, P], BF16)
        self.pt = sb(f"{name}_pt", [P, 2, HB, D], F32)
        self.o_sb = sb(f"{name}_o", [P, self.NB, D], F32)
        self.o_hi = sb(f"{name}_o_hi", [P, 2, self.NB, D], F32R)
        self.o_lo = sb(f"{name}_o_lo", [P, 2, self.NB, D], F32R)
        self.recip = sb(f"{name}_recip", [P, D], F32)
        self.o_norm = sb(f"{name}_o_norm", [P, 2, D], F32)

        def s(what):
            return sem(f"{name}_{what}")

        self.pieces_stored = [s(f"pieces_stored{i}") for i in range(2)]
        self.stacks_loaded = [s(f"stacks_loaded{i}") for i in range(RING)]
        self.peak_loaded = [s(f"peak_loaded{i}") for i in range(RING)]
        self.v_ones_ready, self.ones_loaded = s("v_ones_ready"), s("ones_loaded")
        self.pieces_ready, self.ones_ready, self.v_ready = s("pieces_ready"), s("ones_ready"), s("v_ready")
        self.s_done, self.max_done, self.peak3_ready = s("s_done"), s("max_done"), s("peak3_ready")
        self.peak_turned, self.peak_rows_ready = s("peak_turned"), s("peak_rows_ready")
        self.st_done, self.exp_done, self.pv_done, self.o_ready = s("st_done"), s("exp_done"), s("pv_done"), s("o_ready")
        self.o_hi_ready, self.o_lo_ready = s("o_hi_ready"), s("o_lo_ready")
        self.parts_done, self.norm_ready, self.recip_ready = s("parts_done"), s("norm_ready"), s("recip_ready")

    def s_ps(self, n):
        return self.core.psum[:, n % 2, :].rearrange("p (h k) -> p h k", h=2)

    def st_ps(self, n):
        return self.core.psum[:, 2 + 2 * (n % 2):4 + 2 * (n % 2), :].rearrange("p a (h q) -> p (a h) q", h=2)

    def o_ps(self, g):
        return self.core.psum[:, 7, (g % 2) * D:(g % 2 + 1) * D]

    def peak_ps(self):
        return self.core.psum[0:3 * self.H * DC, 0, :].bitcast(BF16)[:, 0:P]

    def num_ps(self):
        return self.core.psum[:, 6, 0:D]

    def den_ps(self):
        return self.core.psum[:, 6, D:2 * D]

    def sync(self, sp):
        H, DH, K = self.H, self.DH, self.K

        def store(b):
            sp.wait_ge(self.pieces_ready, b + 1)
            for dram, pieces in ((self.q_dram, self.q3), (self.k_dram, self.k3))[:1 if self.k_stored else 2]:
                for s in range(3):
                    sp.dma_start(dram[b, s].rearrange("d h t -> h d t"), pieces[:, b, s]).then_inc(self.pieces_stored[b % 2], 16)

        def load(b):
            j = b % RING
            sp.wait_ge(self.pieces_stored[b % 2], 16 * (3 if self.k_stored else 6) * (b // 2 + 1))
            if b >= RING:
                sp.wait_ge(self.st_done, 2 * self.NB * (b - RING + 1))
            for first, count in SLOT_RUNS:
                to = slice(first * DH, (first + count) * DH)
                q, k = (dram[b].rearrange("s d h t -> s d (h t)") for dram in (self.q_dram, self.k_dram))
                sp.dma_start(self.qs[to, j].rearrange("p h t -> p (h t)"), q[0:count]).then_inc(self.stacks_loaded[j], 16)
                piece = K_PIECE[first]
                sp.dma_start(self.ks[to, j].rearrange("p h t -> p (h t)"),
                             k[piece:piece + 1].to_broadcast([count, DH, H * D])).then_inc(self.stacks_loaded[j], 16)

        def load_peak(b):
            sp.wait_ge(self.peak_rows_ready, b + 1)
            sp.dma_start(self.qs[K:K + 3, b % RING].rearrange("s h (c q) -> s (h c) q", c=DC),
                         self.peak_rows[:, b % 2, :]).then_inc(self.peak_loaded[b % RING], 16)

        sp.wait_ge(self.ones_ready, 1)
        sp.dma_start(self.ks[K:K + 3].rearrange("s j h t -> s (j h) t"),
                     self.ones_row[:, :].unsqueeze(1).to_broadcast([3, RING * H, D])).then_inc(self.ones_loaded, 16)
        store(0)
        store(1)
        load(0)
        load(1)
        store(2)
        load(2)
        load_peak(0)
        for b in range(B):
            if b + 1 < B:
                load_peak(b + 1)
            if b + RING < B:
                store(b + RING)
                load(b + RING)

    def gpsimd(self, pool, aside=None):
        pool.memset(self.v_ones[:], 1.0).then_inc(self.v_ones_ready, 1)
        pool.wait_ge(self.v_ones_ready, 1)

        def spread_v(b):
            j = b % 2
            if b >= 2:
                pool.wait_ge(self.pv_done, 2 * self.NB * (b - 1))
            for c in range(DC):
                last = pool.tensor_copy(self.v_ones[:, j, c, :, 0:self.DH],
                                        self.v_t(b, c).rearrange("p (h d) -> p h d", h=self.H))
            last.then_inc(self.v_ready, 1)

        spread_v(0)
        spread_v(1)
        for b in range(B):
            for pair in range(self.NB // 2):
                blocks = slice(2 * pair, 2 * pair + 2)
                pool.wait_ge(self.o_hi_ready, b * self.NB // 2 + pair + 1)
                pool.tensor_tensor(self.o_lo[:, b % 2, blocks], self.o_sb[:, blocks], self.o_hi[:, b % 2, blocks].bitcast(F32), ALU.subtract)\
                    .then_inc(self.o_lo_ready, 1)
            if b + 2 < B:
                spread_v(b + 2)
            if aside:
                aside(b)

    def vector_ones(self, dve):
        dve.memset(self.ones_row[:, :], 1.0).then_inc(self.ones_ready, 1)

    def maxima(self, dve, ch, b):
        j = b % 2
        for n in range(self.H):
            c, pair = divmod(n, self.H // 2)
            dve.wait_ge(self.s_done, b * self.H + n + 1)
            last = dve.tensor_reduce(self.peak[:, j, 2 * pair:2 * pair + 2, c], self.s_ps(n), AXX, ALU.max)
            last.then_inc(self.max_done, 1)
        dve.wait_ge(self.max_done, (b + 1) * self.H)
        if b >= 1:
            dve.wait_ge(self.peak_turned, b)
        peak, rest, three = self.peak[:, j], self.peak_rest, self.peak3
        ch.step(dve.tensor_scalar(three[:, 0], peak, -1.0, None, ALU.mult))
        ch.wait()
        ch.step(dve.scalar_tensor_tensor(rest[:], peak, -1.0, three[:, 0], ALU.mult, ALU.subtract))
        ch.wait()
        ch.step(dve.tensor_copy(three[:, 1], rest[:]))
        ch.wait()
        dve.tensor_tensor(three[:, 2], rest[:], three[:, 1], ALU.subtract).then_inc(self.peak3_ready, 1)
        dve.wait_ge(self.peak_turned, b + 1)
        if b >= 2:
            dve.wait_ge(self.peak_loaded[(b - 2) % RING], 16 * ((b - 2) // RING + 1))
        dve.tensor_copy(self.peak_rows[:, j, :], self.peak_ps())\
            .then_inc(self.peak_rows_ready, 1)

    def vector(self, dve, ch, finish):
        self.maxima(dve, ch, 0)
        for b in range(B):
            if b + 1 < B:
                self.maxima(dve, ch, b + 1)
            if b:
                for step in finish:
                    step(b - 1)
        for step in finish:
            step(B - 1)

    def normalize(self, dve, ch, b):
        dve.wait_ge(self.parts_done, b + 1)
        dve.reciprocal(self.recip[:, :], self.den_ps()).then_inc(self.recip_ready, 1)
        dve.wait_ge(self.recip_ready, b + 1)
        dve.tensor_tensor(self.o_norm[:, b % 2, :], self.num_ps(), self.recip[:, :], ALU.mult).then_inc(self.norm_ready, 1)

    def exponentials(self, act, b):
        for n in range(2 * self.NB):
            m = b * 2 * self.NB + n
            act.wait_ge(self.st_done, m + 1)
            if m >= 2:
                act.wait_ge(self.pv_done, m - 1)
            act.activation(self.pt[:, n % 2], self.st_ps(n), ACT.Exp, scale=self.scale).then_inc(self.exp_done, 1)
            if n % 4 == 0 and n:
                self.take_sums(act, b, n // 4 - 1)
        self.take_sums(act, b, self.NB // 2 - 1)

    def take_sums(self, act, b, pair):
        act.wait_ge(self.pv_done, b * 2 * self.NB + 4 * pair + 4)
        if b >= 2:
            act.wait_ge(self.parts_done, b - 1)
        if b:
            act.wait_ge(self.o_lo_ready, (b - 1) * self.NB // 2 + pair + 1)
        blocks = slice(2 * pair, 2 * pair + 2)
        act.activation(self.o_sb[:, blocks].rearrange("p g q -> p (g q)"), self.core.psum[:, 7, :], ACT.Copy).then_inc(self.o_ready, 1)
        act.wait_ge(self.o_ready, b * self.NB // 2 + pair + 1)
        act.activation(self.o_hi[:, b % 2, blocks], self.o_sb[:, blocks], ACT.Copy).then_inc(self.o_hi_ready, 1)

    def scores_by_query(self, pe, b, n):
        j, K = b % RING, self.K
        c, pair = divmod(n, self.H // 2)
        if n == 0:
            pe.wait_ge(self.stacks_loaded[j], 16 * 2 * len(SLOT_RUNS) * (b // RING + 1))
        if n < 2 and b:
            pe.wait_ge(self.peak_rows_ready, b)
        if b * self.H + n >= 2:
            pe.wait_ge(self.max_done, b * self.H + n - 1)
        for i in range(2):
            h = 2 * pair + i
            last = pe.matmul(self.s_ps(n)[:, i, :], self.qs[0:K, j, h, c * P:(c + 1) * P], self.ks[0:K, j, h, :],
                             start=True, stop=self.mask is None)
            if self.mask:
                last = pe.matmul(self.s_ps(n)[:, i, :], self.core.ident_bf[:, :], self.mask[0][:, c, :], start=False, stop=True)
        last.then_inc(self.s_done, 1)

    def turn_peak(self, pe, b):
        pe.wait_ge(self.peak3_ready, b + 1)
        pe.transpose(self.peak_ps(), self.peak3[:].rearrange("p s h c -> p (s h c)"), self.core.ident_bf[:, :])\
            .then_inc(self.peak_turned, 1)

    def scores_by_key(self, pe, b, n):
        j, g, c, K = b % RING, n // 2, n % 2, self.K
        m = b * 2 * self.NB + n
        if n == 0:
            pe.wait_ge(self.ones_loaded, 16)
            pe.wait_ge(self.peak_loaded[j], 16 * (b // RING + 1))
        if m >= 2:
            pe.wait_ge(self.exp_done, m - 1)
        for i in range(HB):
            h = g * HB + i
            last = pe.matmul(self.st_ps(n)[:, i, :], self.ks[0:K + 3, j, h, c * P:(c + 1) * P], self.qs[0:K + 3, j, h, :],
                             start=True, stop=self.mask is None)
            if self.mask:
                last = pe.matmul(self.st_ps(n)[:, i, :], self.core.ident_bf[:, :], self.mask[1][:, c, :], start=False, stop=True)
        last.then_inc(self.st_done, 1)

    def weighted_sums(self, pe, b, n):
        j, g, c = b % 2, n // 2, n % 2
        if n == 0:
            pe.wait_ge(self.v_ready, b + 1)
        if n % 4 == 0 and b * self.NB + g >= 2:
            pe.wait_ge(self.o_ready, (b * self.NB + g) // 2)
        pe.wait_ge(self.exp_done, b * 2 * self.NB + n + 1)
        for i in range(HB):
            last = pe.matmul(self.o_ps(g)[32 * i:32 * i + 32, :], self.v_ones[:, j, c, g * HB + i, :], self.pt[:, n % 2, i, :],
                             start=(c == 0), stop=(c == 1), skip_group_check=True)
        last.then_inc(self.pv_done, 1)

    def split_sums(self, pe, b, picks):
        pe.wait_ge(self.o_lo_ready, (b + 1) * self.NB // 2)
        if b:
            pe.wait_ge(self.norm_ready, b)
            if self.out_read:
                pe.wait_ge(self.out_read, b)
        for ps, pick in ((self.num_ps(), picks[0]), (self.den_ps(), picks[1])):
            for g in range(self.NB):
                for o in (self.o_hi, self.o_lo):
                    last = pe.matmul(ps, pick[:, g, :], o[:, b % 2, g, :], start=(g == 0 and o is self.o_hi),
                                     stop=(g == self.NB - 1 and o is self.o_lo))
        last.then_inc(self.parts_done, 1)

    def tensor(self, pe, picks, after=None):
        H, steps = self.H, 2 * self.NB
        for n in range(H):
            self.scores_by_query(pe, 0, n)
        self.turn_peak(pe, 0)
        for b in range(B):
            for n in range(steps):
                self.scores_by_key(pe, b, n)
                if n == 1 and b:
                    self.split_sums(pe, b - 1, picks)
                if b + 1 < B:
                    for i in range(self.LEAD * n, min(self.LEAD * (n + 1), H)):
                        self.scores_by_query(pe, b + 1, i)
                if n:
                    self.weighted_sums(pe, b, n - 1)
                if n == self.TURN_AT and b + 1 < B:
                    self.turn_peak(pe, b + 1)
            self.weighted_sums(pe, b, steps - 1)
            if b and after:
                after(b - 1)
        self.split_sums(pe, B - 1, picks)
        if after:
            after(B - 1)


class ContextPieces:

    def __init__(self, nc, core, sb, sem, heads):
        self.core = core
        self.dram = nc.dram_tensor("ca_k_pieces", [B, 3, P // heads, heads, D], BF16, kind="Internal").ap()
        self.stored = sem("ca_k_stored")
        self.k3 = sb("ca_k3", [P, B, 3, D], BF16)
        self.rest = sb("ca_k_rest", [P, D], F32)
        self.step, self.ready = sem("ca_k_step"), sem("ca_k_ready")

    def sync(self, sp):
        for b in range(B):
            sp.wait_ge(self.ready, b + 1)
            for s in range(3):
                sp.dma_start(self.dram[b, s].rearrange("d h t -> h d t"), self.k3[:, b, s]).then_inc(self.stored, 16)
        sp.wait_ge(self.stored, 16 * 3 * B)

    def gpsimd(self, pool, batches):
        ch = Chain(pool, self.step, start=4 * batches[0])
        pool.wait_ge(self.core.ctx_loaded, 16)
        for b in batches:
            split_in_three(pool, ch, self.core.ctx[:, b], self.rest[:, :], [self.k3[:, b, s] for s in range(3)])
            ch.wait()
            pool.sem_inc(self.ready, 1)


def channel_attention_layer(nc, core, layer, ins, sb, sem):
    H = 8
    xn = sb("ca_xn", [P, B, D], F32)
    rest = sb("ca_rest", [P, B, D], F32)
    q3 = sb("ca_q3", [P, B, 3, D], BF16)
    k3 = core.context_pieces.k3
    picks = sb("ca_picks", [P, 2, H // HB, P], F32)
    picks_r = sb("ca_picks_r", [P, 2, H // HB, P], F32R)
    picks_ready = sem("ca_picks_ready")
    picks_loaded, dve_step, pool_step = sem("ca_picks_loaded"), sem("ca_dve"), sem("ca_pool")
    att = HeadAttention(nc, core, sb, sem, "ca", H, 0.25, q3, k3,
                        lambda b, c: core.ctx_t[:, c, b, :], k_dram=core.context_pieces.dram)

    def sync(sp):
        sp.wait_ge(core.x_stats, (layer + 1) * B)
        sp.dma_start(picks[:], ins["picks8"]).then_inc(picks_loaded, 16)
        att.sync(sp)

    def gpsimd(pool):
        ch = Chain(pool, pool_step)
        for b in range(B):
            rstd_row(pool, ch, core, layer, b)
        pool.wait_ge(core.ctx_t_loaded, 16)

        def round_fp8_weights(b):
            if b:
                core.fp8_weights.gpsimd(pool, b - 1)

        att.gpsimd(pool, round_fp8_weights)
        core.fp8_weights.gpsimd(pool, B - 1)

    def vector(dve):
        ch = Chain(dve, dve_step)
        att.vector_ones(dve)

        def prepare(b):
            dve.wait_ge(core.rstd_ready, layer * B + b + 1)
            ch.step(dve.tensor_scalar(xn[:, b], core.x_sb[:, b], core.mean_var[:, b, 0:1], core.rstd[:, b],
                                      ALU.subtract, ALU.mult))
            ch.wait()
            split_in_three(dve, ch, xn[:, b], rest[:, b], [q3[:, b, s] for s in range(3)])
            ch.wait()
            dve.sem_inc(att.pieces_ready, 1)

        def add_to_x(b):
            att.normalize(dve, ch, b)
            dve.wait_ge(att.norm_ready, b + 1)
            ch.step(dve.tensor_tensor(core.x_sb[:, b], core.x_sb[:, b], att.o_norm[:, b % 2], ALU.add))

        def prepare_fp8(b):
            core.fp8_weights.vector(dve, ch, b)

        def statistics(b):
            ch.wait()
            layer_norm_rows(dve, ch, core, b)

        for b in range(B):
            prepare(b)
        att.vector(dve, ch, (add_to_x, prepare_fp8, statistics))

    def scalar(act):
        act.wait_ge(picks_loaded, 16)
        act.activation(picks_r[:], picks[:], ACT.Copy).then_inc(picks_ready, 1)
        for b in range(B):
            att.exponentials(act, b)

    def tensor(pe):
        pe.wait_ge(picks_ready, 1)
        att.tensor(pe, (picks_r[:, 0], picks_r[:, 1]))

    return dict(sync=sync, gpsimd=gpsimd, vector=vector, scalar=scalar, tensor=tensor)


F8 = 704
F8_SIZES = [P] * (F8 // P) + [F8 % P]
F8_CHUNKS = len(F8_SIZES)
F8_MAX = 448.0
EXPONENT_BITS = 0x7F800000


class Fp8Weights:

    NW = 2 * F8_CHUNKS + DC
    STEPS = 8

    def __init__(self, nc, core, ins, sb, sem):
        self.ins = ins
        self.idx = sb("f8_idx", [P, F8_CHUNKS], I32)
        self.w_rows = sb("f8_w_rows", [P, 2, F8_CHUNKS, D], F32)
        self.wd_rows = sb("f8_wd_rows", [P, DC, F8], F32)
        self.magic = sb("f8_magic", [P, 2, F8_CHUNKS * D // 2], F32)
        self.w_q = sb("f8_w_q", [P, 2, F8_CHUNKS, D], BF16)
        self.wd_q = sb("f8_wd_q", [P, DC, F8], BF16)
        self.w_max = sb("f8_w_max", [P, self.NW], F32)
        self.w_scale = sb("f8_w_scale", [P, self.NW], F32)
        self.w_inv = sb("f8_w_inv", [P, self.NW], F32)
        self.core = core
        self.diag = sb("f8_diag", [P, self.NW * P], F32)
        self.diag_ready = sem("f8_diag_ready")
        self.idx_loaded, self.wd_loaded, self.pad_set = sem("f8_idx_loaded"), sem("f8_wd_loaded"), sem("f8_pad_set")
        self.magic_ready, self.added = sem("f8_magic_ready"), sem("f8_added")
        self.rows_loaded, self.quantized = sem("f8_rows_loaded"), sem("f8_quantized")

    def sync(self, sp):
        sp.dma_start(self.idx[:, 0:F8_CHUNKS - 1], self.ins["f8_idx"]).then_inc(self.idx_loaded, 16)
        sp.dma_start(self.idx[0:F8_SIZES[-1], F8_CHUNKS - 1:F8_CHUNKS], self.ins["f8_idx_rest"]).then_inc(self.idx_loaded, 16)
        sp.dma_start(self.wd_rows[:], self.ins["f8_down"].rearrange("(c p) f -> p c f", p=P)).then_inc(self.wd_loaded, 16)

    def gather(self, pool):
        pool.memset(self.w_rows[:, :, F8_CHUNKS - 1, :], 1.0).then_inc(self.pad_set, 1)
        pool.wait_ge(self.pad_set, 1)
        pool.wait_ge(self.idx_loaded, 32)
        for m, name in enumerate(("f8_gate", "f8_up")):
            for c, size in enumerate(F8_SIZES):
                pool.indirect_dma_start(out=self.w_rows[0:size, m, c, :], out_offset=None, in_=self.ins[name],
                                        in_offset=bass.IndirectOffsetOnAxis(ap=self.idx[0:size, c:c + 1], axis=0))\
                    .then_inc(self.rows_loaded, 16)

    def vector(self, dve, ch, step):
        C2 = 2 * F8_CHUNKS
        if step == 0:
            dve.wait_ge(self.rows_loaded, 16 * C2)
            dve.wait_ge(self.pad_set, 1)
            dve.wait_ge(self.wd_loaded, 16)
            ch.step(dve.tensor_reduce(self.w_max[:, 0:C2], self.w_rows[:].rearrange("p m c d -> p (m c) d"), AXX, ALU.max,
                                      apply_absolute_value=True))
        elif step == 1:
            ch.step(dve.tensor_reduce(self.w_max[:, C2:], self.wd_rows[:], AXX, ALU.max, apply_absolute_value=True))
            ch.wait()
            ch.step(dve.tensor_scalar(self.w_scale[:, :], self.w_max[:, :], 1.0 / F8_MAX, None, ALU.mult))
            ch.wait()
            ch.step(dve.reciprocal(self.w_inv[:, :], self.w_scale[:, :]))
            ch.wait()
            for n in range(self.NW):
                last = dve.tensor_scalar(self.diag[:, n * P:(n + 1) * P], self.core.ident[:, :], self.w_scale[:, n:n + 1],
                                         None, ALU.mult)
            last.then_inc(self.diag_ready, 1)
        else:
            if step < 6:
                half, n = F8_CHUNKS // 2, (step - 2) * (F8_CHUNKS // 2)
                rows = self.w_rows[:].rearrange("p m c d -> p (m c) d")[:, n:n + half]
                out = self.w_q[:].rearrange("p m c d -> p (m c) d")[:, n:n + half]
                for i in range(half):
                    ch.step(dve.tensor_scalar(rows[:, i], rows[:, i], self.w_inv[:, n + i:n + i + 1], None, ALU.mult))
                rows, out = rows.rearrange("p c d -> p (c d)"), out.rearrange("p c d -> p (c d)")
            else:
                rows, out, n = self.wd_rows[:, step - 6], self.wd_q[:, step - 6], C2 + step - 6
                ch.step(dve.tensor_scalar(rows, rows, self.w_inv[:, n:n + 1], None, ALU.mult))
            ch.wait()
            if step > 3:
                dve.wait_ge(self.quantized, step - 3)
            magic_of(dve, ch, rows, self.magic[:, step % 2, 0:rows.shape[-1]]).then_inc(self.magic_ready, 1)

    def gpsimd(self, pool, step):
        if step < 2:
            return
        if step < 6:
            half, n = F8_CHUNKS // 2, (step - 2) * (F8_CHUNKS // 2)
            rows, out = (a[:].rearrange("p m c d -> p (m c) d")[:, n:n + half].rearrange("p c d -> p (c d)")
                         for a in (self.w_rows, self.w_q))
        else:
            rows, out = self.wd_rows[:, step - 6], self.wd_q[:, step - 6]
        magic = self.magic[:, step % 2, 0:rows.shape[-1]]
        pool.wait_ge(self.magic_ready, step - 1)
        pool.tensor_tensor(rows, rows, magic, ALU.add).then_inc(self.added, 1)
        pool.wait_ge(self.added, step - 1)
        pool.tensor_tensor(out, rows, magic, ALU.subtract).then_inc(self.quantized, 1)


def magic_of(dve, ch, v, m):
    ch.step(dve.tensor_scalar(m.bitcast(I32), v.bitcast(I32), EXPONENT_BITS, None, ALU.bitwise_and))
    ch.wait()
    return dve.tensor_scalar(m, m, 2.0 ** -6, 1.5 * 2.0 ** 20, ALU.max, ALU.mult)


def round_fp8(dve, ch, v, m, out):
    ch.step(magic_of(dve, ch, v, m))
    ch.wait()
    ch.step(dve.tensor_tensor(v, v, m, ALU.add))
    ch.wait()
    return dve.tensor_tensor(out, v, m, ALU.subtract)


def fp8_ffn_layer(nc, core, layer, ins, sb, sem):
    def chunks(width):
        return [(n, min(512, width - n)) for n in range(0, width, 512)]

    weights = core.fp8_weights
    NW, w_q, wd_q, w_scale = weights.NW, weights.w_q, weights.wd_q, weights.w_scale
    w_t = sb("f8_w_t", [P, 2, DC, F8_CHUNKS * P], BF16)
    wd_t = sb("f8_wd_t", [P, F8_CHUNKS, D], BF16)
    w_back = sb("f8_w_back", [P, NW, P], F32)
    xn = sb("f8_xn", [P, B, D], F32)
    xm = sb("f8_xm", [P, B, D], F32)
    xq = sb("f8_xq", [P, B, D], BF16)
    xq_t = sb("f8_xq_t", [P, 2, DC, P], BF16)
    st = sb("f8_st", [P, 3, B], F32)
    st2 = sb("f8_st2", [P, 2, 4], F32)
    g = sb("f8_g", [P, 2, F8], F32)
    sg = sb("f8_sg", [P, 2, F8], F32)
    u = sb("f8_u", [P, 2, F8], F32)
    t = sb("f8_t", [P, 2, F8], F32)
    tv = sb("f8_tv", [P, 2, F8], F32)
    tm = sb("f8_tm", [P, 2, F8], F32)
    tq = sb("f8_tq", [P, 2, F8], BF16)
    a_t = sb("f8_a_t", [P, 2, F8_CHUNKS, P], BF16)
    out_rows = sb("f8_out", [P, 2, D], F32)

    dve_step, pool_step = sem("f8_dve"), sem("f8_pool")
    w_turned, w_t_ready = sem("f8_w_turned"), sem("f8_w_t_ready")
    back_done, back_ready = sem("f8_back_done"), sem("f8_back_ready")
    xq_ready, xq_turned, xq_t_ready = sem("f8_xq_ready"), sem("f8_xq_turned"), sem("f8_xq_t_ready")
    gu_done, g_ready, u_ready, sg_ready, t_ready = (
        sem("f8_gu_done"), sem("f8_g_ready"), sem("f8_u_ready"), sem("f8_sg_ready"), sem("f8_t_ready"))
    inv_ready, tv_ready, tq_ready, a_turned, a_t_ready, y_done = (
        sem("f8_inv_ready"), sem("f8_tv_ready"), sem("f8_tq_ready"), sem("f8_a_turned"), sem("f8_a_t_ready"), sem("f8_y_done"))

    def gu_ps(which):
        return core.psum[:, 2 * which:2 * which + 2, :].rearrange("p n f -> p (n f)")

    xq_ps = core.psum[:, 4, :].bitcast(BF16)
    a_ps = core.psum[:, 5, :].bitcast(BF16)
    y_ps = core.psum[:, 6, 0:D]

    def turn_bank(n):
        return core.psum[:, 4 + n % 4, :].bitcast(BF16)

    def sync(sp):
        pass

    def gpsimd(pool):
        ch = Chain(pool, pool_step)
        for b in range(B):
            rstd_row(pool, ch, core, layer, b)
        for b in range(B):
            j = b % 2
            pool.wait_ge(sg_ready, b + 1)
            pool.wait_ge(u_ready, b + 1)
            if b >= 2:
                pool.wait_ge(tv_ready, b - 1)
            pool.tensor_tensor(t[:, j, :], sg[:, j, :], u[:, j, :], ALU.mult).then_inc(t_ready, 1)

    def vector(dve):
        ch = Chain(dve, dve_step)

        def quantize_x(first, count):
            tiles = slice(first, first + count)
            for b in range(first, first + count):
                dve.wait_ge(core.rstd_ready, layer * B + b + 1)
                ch.step(dve.tensor_scalar(xn[:, b, :], core.x_sb[:, b, :], core.mean_var[:, b, 0:1], core.rstd[:, b, :],
                                          ALU.subtract, ALU.mult))
            ch.wait()
            ch.step(dve.tensor_reduce(st[:, 0, tiles], xn[:, tiles, :], AXX, ALU.max, apply_absolute_value=True))
            ch.wait()
            ch.step(dve.tensor_scalar(st[:, 1, tiles], st[:, 0, tiles], 1.0 / F8_MAX, None, ALU.mult))
            ch.wait()
            ch.step(dve.reciprocal(st[:, 2, tiles], st[:, 1, tiles]))
            ch.wait()
            for b in range(first, first + count):
                ch.step(dve.tensor_scalar(xn[:, b, :], xn[:, b, :], st[:, 2, b:b + 1], None, ALU.mult))
            ch.wait()
            flat = [a[:, tiles, :].rearrange("p b d -> p (b d)") for a in (xn, xm, xq)]
            round_fp8(dve, ch, *flat).then_inc(xq_ready, 1)

        def scale_products(b):
            j = b % 2
            dve.wait_ge(gu_done, b + 1)
            if b >= 2:
                dve.wait_ge(sg_ready, b - 1)
            back = w_back[:].rearrange("p n q -> p (n q)")
            dve.scalar_tensor_tensor(g[:, j, :], gu_ps(0)[:, 0:F8], st[:, 1, b:b + 1], back[:, 0:F8], ALU.mult, ALU.mult)\
                .then_inc(g_ready, 1)
            if b >= 2:
                dve.wait_ge(t_ready, b - 1)
            dve.scalar_tensor_tensor(u[:, j, :], gu_ps(1)[:, 0:F8], st[:, 1, b:b + 1], back[:, F8_CHUNKS * P:F8_CHUNKS * P + F8],
                                     ALU.mult, ALU.mult).then_inc(u_ready, 1)

        def quantize_inner(b):
            j = b % 2
            dve.wait_ge(t_ready, b + 1)
            ch.step(dve.tensor_reduce(st2[:, j, 0:1], t[:, j, :], AXX, ALU.max, apply_absolute_value=True))
            ch.wait()
            ch.step(dve.tensor_scalar(st2[:, j, 1:2], st2[:, j, 0:1], 1.0 / F8_MAX, None, ALU.mult))
            ch.wait()
            if b >= 2:
                dve.wait_ge(tv_ready, b - 1)
            dve.reciprocal(st2[:, j, 2:3], st2[:, j, 1:2]).then_inc(inv_ready, 1)
            if b:
                add_to_x(b - 1)
            dve.wait_ge(tv_ready, b + 1)
            if b >= 2:
                dve.wait_ge(a_turned, b - 1)
            round_fp8(dve, ch, tv[:, j, :], tm[:, j, :], tq[:, j, :]).then_inc(tq_ready, 1)

        def add_to_x(b):
            j = b % 2
            dve.wait_ge(y_done, b + 1)
            back = w_back[:, 2 * F8_CHUNKS:NW, :].rearrange("p n q -> p (n q)")
            ch.step(dve.scalar_tensor_tensor(out_rows[:, j, :], y_ps, st2[:, j, 1:2], back, ALU.mult, ALU.mult))
            ch.wait()
            ch.step(dve.tensor_tensor(core.x_sb[:, b, :], core.x_sb[:, b, :], out_rows[:, j, :], ALU.add))
            ch.wait()
            layer_norm_rows(dve, ch, core, b)

        quantize_x(0, 2)
        quantize_x(2, B - 2)
        dve.wait_ge(back_ready, 4)
        scale_products(0)
        for b in range(B):
            if b + 1 < B:
                scale_products(b + 1)
            quantize_inner(b)
        add_to_x(B - 1)

    def scalar(act):
        for n, (start, size) in enumerate(chunks(NW * P)):
            act.wait_ge(back_done, n + 1)
            act.activation(w_back[:].rearrange("p n q -> p (n q)")[:, start:start + size], core.psum[:, n, 0:size], ACT.Copy)\
                .then_inc(back_ready, 1)
        for n in range(3):
            act.wait_ge(w_turned, n + 1)
            for i in range(8):
                m, c, r = (8 * n + i) // (DC * F8_CHUNKS), ((8 * n + i) // DC) % F8_CHUNKS, (8 * n + i) % DC
                last = act.activation(w_t[:, m, r, c * P:(c + 1) * P], turn_bank(n)[:, i * P:(i + 1) * P], ACT.Copy)
            last.then_inc(w_t_ready, 1)
        for n in range(3, 5):
            act.wait_ge(w_turned, n + 1)
            for i in range(8 if n == 3 else 4):
                c, r = divmod(8 * (n - 3) + i, DC)
                last = act.activation(wd_t[0:F8_SIZES[c], c, r * P:(r + 1) * P], turn_bank(n)[0:F8_SIZES[c], i * P:(i + 1) * P], ACT.Copy)
            last.then_inc(w_t_ready, 1)

        def turned_x(b):
            act.wait_ge(xq_turned, b + 1)
            if b >= 2:
                act.wait_ge(gu_done, b - 1)
            act.activation(xq_t[:, b % 2].rearrange("p a b -> p (a b)"), xq_ps[:, 0:D], ACT.Copy).then_inc(xq_t_ready, 1)

        def silu(b):
            j = b % 2
            act.wait_ge(g_ready, b + 1)
            if b >= 2:
                act.wait_ge(t_ready, b - 1)
            act.activation(sg[:, j, :], g[:, j, :], ACT.Silu).then_inc(sg_ready, 1)

        def scaled(b):
            j = b % 2
            act.wait_ge(inv_ready, b + 1)
            if b >= 2:
                act.wait_ge(tq_ready, b - 1)
            act.activation(tv[:, j, :], t[:, j, :], ACT.Copy, scale=st2[:, j, 2:3]).then_inc(tv_ready, 1)

        def turned_inner(b):
            act.wait_ge(a_turned, b + 1)
            if b >= 2:
                act.wait_ge(y_done, b - 1)
            full = F8_CHUNKS - 1
            act.activation(a_t[:, b % 2, 0:full].rearrange("p a b -> p (a b)"), a_ps[:, 0:full * P], ACT.Copy)
            act.activation(a_t[0:F8_SIZES[-1], b % 2, full, :], a_ps[0:F8_SIZES[-1], full * P:(full + 1) * P], ACT.Copy)\
                .then_inc(a_t_ready, 1)

        turned_x(0)
        turned_x(1)
        silu(0)
        for b in range(B):
            if b + 1 < B:
                silu(b + 1)
            if b + 2 < B:
                turned_x(b + 2)
            scaled(b)
            turned_inner(b)

    def tensor(pe):
        pe.wait_ge(weights.diag_ready, 1)
        for n, (start, size) in enumerate(chunks(NW * P)):
            pe.matmul(core.psum[:, n, 0:size], core.ones[:, :], weights.diag[:, start:start + size], start=True, stop=True)\
                .then_inc(back_done, 1)
        pe.wait_ge(weights.quantized, weights.STEPS - 2)
        for n in range(3):
            for i in range(8):
                m, c, r = (8 * n + i) // (DC * F8_CHUNKS), ((8 * n + i) // DC) % F8_CHUNKS, (8 * n + i) % DC
                last = pe.transpose(turn_bank(n)[:, i * P:(i + 1) * P], w_q[:, m, c, r * P:(r + 1) * P], core.ident_bf[:, :])
            last.then_inc(w_turned, 1)
        for n in range(3, 5):
            if n == 4:
                pe.wait_ge(w_t_ready, 1)
            for i in range(8 if n == 3 else 4):
                c, r = divmod(8 * (n - 3) + i, DC)
                last = pe.transpose(turn_bank(n)[0:F8_SIZES[c], i * P:(i + 1) * P], wd_q[:, r, c * P:c * P + F8_SIZES[c]],
                                    core.ident_bf[:, :])
            last.then_inc(w_turned, 1)
        pe.wait_ge(w_t_ready, 5)
        pe.wait_ge(back_ready, 4)

        def turn_x(b):
            pe.wait_ge(xq_ready, 1 if b < 2 else 2)
            if b:
                pe.wait_ge(xq_t_ready, b)
            for c in range(DC):
                last = pe.transpose(xq_ps[:, c * P:(c + 1) * P], xq[:, b, c * P:(c + 1) * P], core.ident_bf[:, :])
            last.then_inc(xq_turned, 1)

        def product1(b):
            pe.wait_ge(xq_t_ready, b + 1)
            if b:
                pe.wait_ge(u_ready, b)
            for m in range(2):
                for n, size in chunks(F8):
                    for c in range(DC):
                        last = pe.matmul(gu_ps(m)[:, n:n + size], xq_t[:, b % 2, c, :], w_t[:, m, c, n:n + size],
                                         start=(c == 0), stop=(c == DC - 1))
            last.then_inc(gu_done, 1)

        def turn_inner(b):
            pe.wait_ge(tq_ready, b + 1)
            if b:
                pe.wait_ge(a_t_ready, b)
            for c, size in enumerate(F8_SIZES):
                last = pe.transpose(a_ps[0:size, c * P:(c + 1) * P], tq[:, b % 2, c * P:c * P + size], core.ident_bf[:, :])
            last.then_inc(a_turned, 1)

        def product2(b):
            pe.wait_ge(a_t_ready, b + 1)
            if b:
                pe.wait_ge(core.x_stats, (layer + 1) * B + b)
            for c, size in enumerate(F8_SIZES):
                last = pe.matmul(y_ps, a_t[0:size, b % 2, c, :], wd_t[0:size, c, :], start=(c == 0), stop=(c == F8_CHUNKS - 1))
            last.then_inc(y_done, 1)

        turn_x(0)
        product1(0)
        turn_x(1)
        product1(1)
        for b in range(B):
            if b + 2 < B:
                turn_x(b + 2)
                product1(b + 2)
            turn_inner(b)
            product2(b)

    return dict(sync=sync, gpsimd=gpsimd, vector=vector, scalar=scalar, tensor=tensor)


def memory_attention_layer(nc, core, layer, ins, sb, sem):
    HALF = B // 2
    xn = sb("ma_xn", [P, B, D], F32)
    xn_t = sb("ma_xn_t", [P, 2, DC, HALF, T], F32)
    mask_u8 = sb("ma_mask_u8", [P, B * T], U8)
    mask = sb("ma_mask", [P, B, T], F32)
    mask_fill = sb("ma_mask_fill", [P, B, T], F32)
    valid = sb("ma_valid", [P, B], F32)
    s = sb("ma_s", [P, 2, HALF, T], F32)
    e = sb("ma_e", [P, 2, HALF, T], F32)
    e_t = sb("ma_e_t", [P, 2, HALF, T], F32)
    peak = sb("ma_peak", [P, 2, HALF], F32)
    total = sb("ma_total", [P, 2, HALF], F32)
    weight = sb("ma_weight", [P, 2, HALF], F32)

    mask_loaded, dve_step, pool_step = sem("ma_mask_loaded"), sem("ma_dve"), sem("ma_pool")
    xn_ready, xn_turned, xn_t_ready, s_done = sem("ma_xn_ready"), sem("ma_xn_turned"), sem("ma_xn_t_ready"), sem("ma_s_done")
    s_ready, e_ready, e_turned, e_t_ready, o_done = (
        sem("ma_s_ready"), sem("ma_e_ready"), sem("ma_e_turned"), sem("ma_e_t_ready"), sem("ma_o_done"))

    def xn_ps(c):
        return core.psum[:, c, :].rearrange("p (b t) -> p b t", t=T)

    def s_ps(n):
        return core.psum[:, 2 + n, :].rearrange("p (b t) -> p b t", t=T)

    def e_ps(n):
        return core.psum[:, 4 + n, :].rearrange("p (b t) -> p b t", t=T)

    def o_ps(i):
        return core.psum[:, 6 + i // 2, (i % 2) * D:(i % 2 + 1) * D]

    def sync(sp):
        sp.wait_ge(core.x_stats, (layer + 1) * B)
        sp.dma_start(mask_u8[:, :], ins["mask_mem"].to_broadcast([P, B * T])).then_inc(mask_loaded, 16)

    def gpsimd(pool):
        ch = Chain(pool, pool_step)
        for b in range(B):
            rstd_row(pool, ch, core, layer, b)

    def vector(dve):
        ch = Chain(dve, dve_step)
        dve.wait_ge(mask_loaded, 16)
        dve.wait_ge(core.x_stats, (layer + 1) * B)
        ch.step(dve.tensor_copy(mask[:].rearrange("p b t -> p (b t)"), mask_u8[:, :]))
        ch.wait()
        ch.step(dve.tensor_scalar(mask_fill[:], mask[:], 1.0, 1e30, ALU.subtract, ALU.mult))
        ch.step(dve.tensor_reduce(valid[:, :], mask[:], AXX, ALU.max))
        for b in range(B):
            dve.wait_ge(core.rstd_ready, layer * B + b + 1)
            dve.tensor_scalar(xn[:, b, :], core.x_sb[:, b, :], core.mean_var[:, b, 0:1], core.rstd[:, b, :],
                              ALU.subtract, ALU.mult).then_inc(xn_ready, 1)
        for n in range(2):
            own = slice(HALF * n, HALF * n + HALF)
            dve.wait_ge(s_done, n + 1)
            ch.step(dve.scalar_tensor_tensor(s[:, n], s_ps(n), 1.0 / 16.0, mask[:, own], ALU.mult, ALU.mult))
            ch.wait()
            ch.step(dve.tensor_tensor(s[:, n], s[:, n], mask_fill[:, own], ALU.add))
            ch.wait()
            ch.step(dve.tensor_reduce(peak[:, n], s[:, n], AXX, ALU.max))
            ch.wait()
            dve.tensor_tensor(s[:, n], s[:, n], peak[:, n].to_broadcast([P, HALF, T]), ALU.subtract).then_inc(s_ready, 1)
        for n in range(2):
            dve.wait_ge(e_ready, n + 1)
            ch.step(dve.tensor_reduce(total[:, n], e[:, n], AXX, ALU.add))
            ch.wait()
            ch.step(dve.reciprocal(total[:, n], total[:, n]))
            ch.wait()
            ch.step(dve.tensor_tensor(weight[:, n], total[:, n], valid[:, HALF * n:HALF * n + HALF], ALU.mult))
            ch.wait()
            dve.wait_ge(o_done, n + 1)
            for i in range(HALF):
                b = HALF * n + i
                ch.step(dve.scalar_tensor_tensor(core.x_sb[:, b], o_ps(i), weight[:, n, i:i + 1], core.x_sb[:, b],
                                                 ALU.mult, ALU.add))
                ch.wait()
                layer_norm_rows(dve, ch, core, b)

    def scalar(act):
        for n in range(2):
            act.wait_ge(xn_turned, n + 1)
            for c in range(DC):
                act.activation(xn_t[:, n, c], xn_ps(c), ACT.Copy).then_inc(xn_t_ready, 1)
        for n in range(2):
            act.wait_ge(s_ready, n + 1)
            act.activation(e[:, n], s[:, n], ACT.Exp).then_inc(e_ready, 1)
            act.wait_ge(e_turned, n + 1)
            act.activation(e_t[:, n], e_ps(n), ACT.Copy).then_inc(e_t_ready, 1)

    def tensor(pe):
        pe.wait_ge(core.ctx_t_loaded, 16)
        for n in range(2):
            if n:
                pe.wait_ge(xn_t_ready, DC)
            for i in range(HALF):
                pe.wait_ge(xn_ready, HALF * n + i + 1)
                for c in range(DC):
                    last = pe.transpose(xn_ps(c)[:, i, :], xn[:, HALF * n + i, c * P:(c + 1) * P], core.ident[:, :])
            last.then_inc(xn_turned, 1)
            pe.wait_ge(xn_t_ready, DC * (n + 1))
            for i in range(HALF):
                for c in range(DC):
                    last = pe.matmul(s_ps(n)[:, i, :], xn_t[:, n, c, i, :], core.ctx_t[:, c, HALF * n + i, :],
                                     start=(c == 0), stop=(c == DC - 1))
            last.then_inc(s_done, 1)
        pe.wait_ge(core.ctx_loaded, 16)
        for n in range(2):
            pe.wait_ge(e_ready, n + 1)
            for i in range(HALF):
                last = pe.transpose(e_ps(n)[:, i, :], e[:, n, i, :], core.ident[:, :])
            last.then_inc(e_turned, 1)
            pe.wait_ge(e_t_ready, n + 1)
            if n:
                pe.wait_ge(core.x_stats, (layer + 1) * B + HALF)
            for i in range(HALF):
                last = pe.matmul(o_ps(i), e_t[:, n, i, :], core.ctx[:, HALF * n + i, :], start=True, stop=True)
            last.then_inc(o_done, 1)

    return dict(sync=sync, gpsimd=gpsimd, vector=vector, scalar=scalar, tensor=tensor)


TOKENS = B * T
EW = 2 * D + D


def in_turn(engine, count):
    yield 0, 0
    yield 1, 1
    with engine.Fori(1, count // 2 - 1) as pair:
        for j in range(2):
            yield pair * 2 + j, j
    yield count - 2, 0
    yield count - 1, 1


def experts_layer(nc, core, layer, ins, sb, sem, name, E, choose):
    xn = sb(f"{name}_xn", [P, B, D], F32)
    x_t = sb(f"{name}_x_t", [P, DC, TOKENS], F32)
    x_hi = sb(f"{name}_x_hi", [P, DC, TOKENS], F32R)
    x_lo = sb(f"{name}_x_lo", [P, DC, TOKENS], F32R)
    router = sb(f"{name}_router", [P, DC, E], F32)
    logits = sb(f"{name}_logits", [P, B, E], F32)
    combine = sb(f"{name}_combine", [P, B, E], F32)
    combine_t = sb(f"{name}_combine_t", [E, TOKENS], F32)
    combine_dram = nc.dram_tensor(f"{name}_combine_dram", [E, TOKENS], F32, kind="Internal").ap()
    w = sb(f"{name}_w", [P, 2, EW], F32)
    w_hi = sb(f"{name}_w_hi", [P, 2, EW], F32R)
    w_lo = sb(f"{name}_w_lo", [P, 2, EW], F32R)
    row = sb(f"{name}_row", [1, 2, TOKENS], F32)
    waited = sb(f"{name}_waited", [1, 1], F32)
    rows = sb(f"{name}_rows", [P, 2, TOKENS], F32)
    sg = sb(f"{name}_sg", [P, 2, 512], F32)
    a = sb(f"{name}_a", [P, 2, 512], F32)
    a_hi = sb(f"{name}_a_hi", [P, 2, 512], F32R)
    a_lo = sb(f"{name}_a_lo", [P, 2, 512], F32R)
    out_t = sb(f"{name}_out_t", [P, DC, TOKENS], F32)

    def s(what):
        return sem(f"{name}_{what}")

    router_loaded, dve_step, pool_step = s("router_loaded"), s("dve"), s("pool")
    xn_ready, xn_turned, xt_ready, hi_ready, logits_done, logits_ready = (
        s("xn_ready"), s("xn_turned"), s("xt_ready"), s("hi_ready"), s("logits_done"), s("logits_ready"))
    combine_ready, combine_turned, combine_t_ready, combine_stored = (
        s("combine_ready"), s("combine_turned"), s("combine_t_ready"), s("combine_stored"))
    w_loaded, row_loaded = [s("w_loaded0"), s("w_loaded1")], [s("row_loaded0"), s("row_loaded1")]
    gu_hi_ready, gu_lo_ready, rows_ready = s("gu_hi_ready"), s("gu_lo_ready"), s("rows_ready")
    down_hi_ready, down_lo_ready = s("down_hi_ready"), s("down_lo_ready")
    gu_done, silu_ready, gated_ready, a_ready, a_hi_ready, a_lo_ready, down_done = (
        s("gu_done"), s("silu_ready"), s("gated_ready"), s("a_ready"), s("a_hi_ready"), s("a_lo_ready"), s("down_done"))
    out_t_ready, out_turned = s("out_t_ready"), s("out_turned")

    def xt_ps(n):
        return core.psum[:, n % 4, :].rearrange("p (b c t) -> p b c t", c=DC, t=T)

    logits_ps = core.psum[:, 4, 0:B * E].rearrange("p (b e) -> p b e", e=E)

    def combine_ps(n):
        return core.psum[0:E, 6 + n, :]

    def half_ps(n, which):
        return core.psum[:, 2 * n + which, :]

    def out_ps(c, n):
        return core.psum[:, 4 + 2 * c + n, :]

    GU, DOWN = slice(0, 2 * D), slice(2 * D, 3 * D)

    def later(e):
        return not isinstance(e, int) or e >= 1

    def loads(e, j):
        return (e // 2 + 1) * 16 if isinstance(e, int) else (e - j) * 8 + 16

    def out_rows(b):
        return core.psum[:, b // 2, (b % 2) * D:(b % 2 + 1) * D]

    def sync(sp):
        sp.wait_ge(core.x_stats, (layer + 1) * B)
        sp.dma_start(router[:], ins[f"{name}_router"].rearrange("(c p) e -> p c e", p=P)).then_inc(router_loaded, 16)
        for e in range(2):
            sp.dma_start(w[:, e, :], ins[f"{name}_experts"][e]).then_inc(w_loaded[e], 16)
        sp.wait_ge(combine_t_ready, 1)
        for e in range(2):
            sp.dma_start(row[0:1, e, :], combine_t[e:e + 1, :]).then_inc(row_loaded[e], 16)
        sp.dma_start(combine_dram, combine_t[:, :]).then_inc(combine_stored, 16)
        sp.wait_ge(combine_stored, 16)
        with sp.Fori(1, E // 2) as pair:
            for j in range(2):
                sp.wait_ge(down_lo_ready, pair * 2 + (j - 1))
                sp.dma_start(w[:, j, :], ins[f"{name}_experts"][pair * 2 + j]).then_inc(w_loaded[j], 16)
                sp.wait_ge(rows_ready, pair * 2 + (j - 1))
                sp.dma_start(row[0:1, j, :], combine_dram[bass.ds(pair * 2 + j, 1), :]).then_inc(row_loaded[j], 16)

    def gpsimd(pool):
        ch = Chain(pool, pool_step)
        for b in range(B):
            rstd_row(pool, ch, core, layer, b)
        for e, j in in_turn(pool, E):
            pool.wait_ge(row_loaded[j], loads(e, j))
            if not (isinstance(e, int) and e < 2):
                pool.wait_ge(a_ready, e * 2 - 2)
            if not (isinstance(e, int) and e < 1):
                pool.wait_ge(rows_ready, e)
            pool.tensor_tensor(waited[:, :], core.minus_half[0:1, :], core.minus_half[0:1, :], ALU.mult)
            pool.partition_broadcast(rows[:, j, :], row[0:1, j, :]).then_inc(rows_ready, 1)

    def vector(dve):
        ch = Chain(dve, dve_step)
        for b in range(B):
            dve.wait_ge(core.rstd_ready, layer * B + b + 1)
            dve.tensor_scalar(xn[:, b, :], core.x_sb[:, b, :], core.mean_var[:, b, 0:1], core.rstd[:, b, :],
                              ALU.subtract, ALU.mult).then_inc(xn_ready, 1)
        for n in range(B // 2):
            own = slice(2 * n * T, 2 * (n + 1) * T)
            dve.wait_ge(xt_ready, n + 1)
            ch.step(dve.tensor_copy(x_hi[:, :, own], x_t[:, :, own]))
            ch.wait()
            dve.tensor_tensor(x_lo[:, :, own], x_t[:, :, own], x_hi[:, :, own].bitcast(F32), ALU.subtract).then_inc(hi_ready, 1)

        def low_gate_up(e, j):
            dve.wait_ge(gu_hi_ready, e + 1)
            dve.tensor_tensor(w_lo[:, j, GU], w[:, j, GU], w_hi[:, j, GU].bitcast(F32), ALU.subtract).then_inc(gu_lo_ready, 1)

        def low_down(e, j):
            dve.wait_ge(down_hi_ready, e + 1)
            dve.tensor_tensor(w_lo[:, j, DOWN], w[:, j, DOWN], w_hi[:, j, DOWN].bitcast(F32), ALU.subtract).then_inc(down_lo_ready, 1)

        def gated(e, n):
            dve.wait_ge(silu_ready, e * 2 + (n + 1))
            dve.tensor_tensor(sg[:, n, :], sg[:, n, :], half_ps(n, 1), ALU.mult).then_inc(gated_ready, 1)

        def weighted(e, j, n):
            if n == 0:
                dve.wait_ge(rows_ready, e + 1)
            dve.wait_ge(gated_ready, e * 2 + (n + 1))
            dve.tensor_tensor(a[:, n, :], sg[:, n, :], rows[:, j, n * 512:(n + 1) * 512], ALU.mult).then_inc(a_ready, 1)

        def low_a(e, n):
            dve.wait_ge(a_hi_ready, e * 2 + (n + 1))
            dve.tensor_tensor(a_lo[:, n, :], a[:, n, :], a_hi[:, n, :].bitcast(F32), ALU.subtract).then_inc(a_lo_ready, 1)

        low_gate_up(0, 0)
        dve.wait_ge(logits_done, 1)
        ch.step(dve.tensor_copy(logits[:], logits_ps))
        ch.wait()
        choose(dve, ch, logits, combine)
        ch.wait()
        dve.sem_inc(combine_ready, 1)
        dve.wait_ge(combine_turned, 1)
        for n in range(2):
            last = dve.tensor_copy(combine_t[:, n * 512:(n + 1) * 512], combine_ps(n))
        last.then_inc(combine_t_ready, 1)
        for e, j in in_turn(dve, E):
            gated(e, 0)
            if not later(e):
                low_gate_up(1, 1)
            weighted(e, j, 0)
            if later(e) and not (isinstance(e, int) and e == E - 1):
                low_gate_up(e + 1, 1 - j)
            low_a(e, 0)
            gated(e, 1)
            weighted(e, j, 1)
            low_down(e, j)
            low_a(e, 1)
        for b in range(B):
            if b % 2 == 0:
                dve.wait_ge(out_turned, b // 2 + 1)
            last = dve.tensor_tensor(core.x_sb[:, b, :], core.x_sb[:, b, :], out_rows(b), ALU.add)
            if layer == core.last_layer:
                last.then_inc(core.x_stats, 1)
            else:
                ch.step(last)
                ch.wait()
                layer_norm_rows(dve, ch, core, b)

    def scalar(act):
        for n in range(B // 2):
            act.wait_ge(xn_turned, n + 1)
            for i in range(2):
                last = act.activation(x_t[:, :, (2 * n + i) * T:(2 * n + i + 1) * T], xt_ps(n)[:, i], ACT.Copy)
            last.then_inc(xt_ready, 1)

        def high_gate_up(e, j):
            act.wait_ge(w_loaded[j], loads(e, j))
            if not (isinstance(e, int) and e < 2):
                act.wait_ge(gu_done, e * 2 - 2)
            act.activation(w_hi[:, j, GU], w[:, j, GU], ACT.Copy).then_inc(gu_hi_ready, 1)

        def high_down(e, j):
            if not (isinstance(e, int) and e < 2):
                act.wait_ge(down_done, e * 2 - 2)
            act.activation(w_hi[:, j, DOWN], w[:, j, DOWN], ACT.Copy).then_inc(down_hi_ready, 1)

        def silu(e, n):
            act.wait_ge(gu_done, e * 2 + (n + 1))
            if later(e):
                act.wait_ge(a_ready, e * 2 + (n - 1))
            act.activation(sg[:, n, :], half_ps(n, 0), ACT.Silu).then_inc(silu_ready, 1)

        def high_a(e, n):
            act.wait_ge(a_ready, e * 2 + (n + 1))
            if later(e):
                act.wait_ge(down_done, e * 2 + (n - 1))
            act.activation(a_hi[:, n, :], a[:, n, :], ACT.Copy).then_inc(a_hi_ready, 1)

        high_gate_up(0, 0)
        choose.scalar(act)
        for e, j in in_turn(act, E):
            silu(e, 0)
            if not (isinstance(e, int) and e == E - 1):
                high_gate_up(e + 1, 1 - j)
            high_a(e, 0)
            silu(e, 1)
            high_down(e, j)
            high_a(e, 1)
        act.wait_ge(down_done, 2 * E)
        for c in range(DC):
            for n in range(2):
                act.activation(out_t[:, c, n * 512:(n + 1) * 512], out_ps(c, n), ACT.Copy).then_inc(out_t_ready, 1)

    def tensor(pe):
        for n in range(B // 2):
            for i in range(2):
                pe.wait_ge(xn_ready, 2 * n + i + 1)
                for c in range(DC):
                    last = pe.transpose(xt_ps(n)[:, i, c, :], xn[:, 2 * n + i, c * P:(c + 1) * P], core.ident[:, :])
            last.then_inc(xn_turned, 1)
        pe.wait_ge(router_loaded, 16)
        for b in range(B):
            pe.wait_ge(xt_ready, b // 2 + 1)
            for c in range(DC):
                last = pe.matmul(logits_ps[:, b, :], x_t[:, c, b * T:(b + 1) * T], router[:, c, :], start=(c == 0), stop=(c == DC - 1))
        last.then_inc(logits_done, 1)
        def gate_up(e, j, n):
            if n == 0:
                pe.wait_ge(gu_lo_ready, e + 1)
            if later(e):
                pe.wait_ge(gated_ready, e * 2 + (n - 1))
            own = slice(n * 512, (n + 1) * 512)
            for which in range(2):
                k = 0
                for c in range(DC):
                    col = slice((which * DC + c) * P, (which * DC + c + 1) * P)
                    for wp, xp in ((w_hi, x_hi), (w_hi, x_lo), (w_lo, x_hi)):
                        last = pe.matmul(half_ps(n, which), wp[:, j, col], xp[:, c, own], start=(k == 0), stop=(k == 3 * DC - 1))
                        k += 1
            last.then_inc(gu_done, 1)

        def down(e, j, n):
            if n == 0:
                pe.wait_ge(down_lo_ready, e + 1)
            pe.wait_ge(a_lo_ready, e * 2 + (n + 1))
            if n == 0 and not later(e):
                pe.wait_ge(combine_t_ready, 1)
            begins, ends = isinstance(e, int) and e == 0, isinstance(e, int) and e == E - 1
            for c in range(DC):
                col = slice(2 * D + c * P, 2 * D + (c + 1) * P)
                for k, (wp, ap) in enumerate(((w_hi, a_hi), (w_hi, a_lo), (w_lo, a_hi))):
                    last = pe.matmul(out_ps(c, n), wp[:, j, col], ap[:, n, :], start=begins and k == 0, stop=ends and k == 2)
            last.then_inc(down_done, 1)

        pe.wait_ge(hi_ready, B // 2)
        for n in range(2):
            gate_up(0, 0, n)
        pe.wait_ge(combine_ready, 1)
        for b in range(B):
            last = pe.transpose(combine_ps(b // 4)[:, (b % 4) * T:(b % 4 + 1) * T], combine[:, b, :], core.ident[:, :])
        last.then_inc(combine_turned, 1)
        for e, j in in_turn(pe, E):
            for n in range(2):
                if later(e):
                    gate_up(e, j, n)
                if later(e):
                    down(e - 1, 1 - j, n)
        for n in range(2):
            down(E - 1, 1, n)
        for b in range(B):
            pe.wait_ge(out_t_ready, b // 4 + 3)
            for c in range(DC):
                last = pe.transpose(out_rows(b)[:, c * P:(c + 1) * P], out_t[:, c, b * T:(b + 1) * T], core.ident[:, :])
            if b % 2:
                last.then_inc(out_turned, 1)

    return dict(sync=sync, gpsimd=gpsimd, vector=vector, scalar=scalar, tensor=tensor)


def top8_experts_layer(nc, core, layer, ins, sb, sem):
    E = 64
    best = sb("e64_best", [P, B, 8], F32)
    left = sb("e64_left", [P, B, E], F32)
    chosen = sb("e64_chosen", [P, B, E], F32)
    exps = sb("e64_exps", [P, B, E], F32)
    total = sb("e64_total", [P, B], F32)
    shifted_ready, exps_ready = sem("e64_shifted_ready"), sem("e64_exps_ready")

    def choose(dve, ch, logits, combine):
        for b in range(B):
            ch.step(dve.max(best[:, b, :], logits[:, b, :]))
            ch.wait()
            ch.step(dve.match_replace(left[:, b, :], best[:, b, :], logits[:, b, :], -3e38))
        dve.tensor_tensor(exps[:], logits[:], best[:, :, 0].to_broadcast([P, B, E]), ALU.subtract).then_inc(shifted_ready, 1)
        ch.wait()
        ch.step(dve.tensor_tensor(chosen[:], logits[:], left[:], ALU.not_equal))
        ch.wait()
        dve.wait_ge(exps_ready, 1)
        ch.step(dve.tensor_tensor(exps[:], exps[:], chosen[:], ALU.mult))
        ch.wait()
        ch.step(dve.tensor_reduce(total[:, :], exps[:], AXX, ALU.add))
        ch.wait()
        ch.step(dve.reciprocal(total[:, :], total[:, :]))
        ch.wait()
        ch.step(dve.tensor_tensor(combine[:], exps[:], total[:, :].to_broadcast([P, B, E]), ALU.mult))

    def choose_scalar(act):
        act.wait_ge(shifted_ready, 1)
        act.activation(exps[:], exps[:], ACT.Exp).then_inc(exps_ready, 1)

    choose.scalar = choose_scalar
    return experts_layer(nc, core, layer, ins, sb, sem, "e64", E, choose)


def top2_experts_layer(nc, core, layer, ins, sb, sem):
    E = 16
    best = sb("e16_best", [P, B, 8], F32)
    index = sb("e16_index", [P, B, 8], mybir.dt.uint32)
    index_f = sb("e16_index_f", [P, B, 2], F32)
    sigmoids = sb("e16_sigmoids", [P, B, 2], F32)
    total = sb("e16_total", [P, B], F32)
    weight = sb("e16_weight", [P, B, 2], F32)
    second = sb("e16_second", [P, B, E], F32)
    best_ready, sigmoids_ready, numbers_ready = sem("e16_best_ready"), sem("e16_sigmoids_ready"), sem("e16_numbers_ready")
    numbers = sb("e16_numbers", [P, E], F32)
    numbers_loaded = sem("e16_numbers_loaded")

    def choose(dve, ch, logits, combine):
        for b in range(B):
            ch.step(dve.max(best[:, b, :], logits[:, b, :]))
            ch.wait()
            ch.step(dve.max_index(index[:, b, :], best[:, b, :], logits[:, b, :]))
        ch.wait()
        dve.tensor_copy(index_f[:], index[:, :, 0:2]).then_inc(best_ready, 1)
        dve.wait_ge(best_ready, 1)
        dve.wait_ge(sigmoids_ready, 1)
        dve.wait_ge(numbers_loaded, 16)
        ch.step(dve.tensor_tensor(total[:, :], sigmoids[:, :, 0], sigmoids[:, :, 1], ALU.add))
        ch.wait()
        ch.step(dve.reciprocal(total[:, :], total[:, :]))
        ch.wait()
        ch.step(dve.tensor_tensor(weight[:], sigmoids[:], total[:, :].to_broadcast([P, B, 2]), ALU.mult))
        ch.wait()
        for b in range(B):
            ch.step(dve.tensor_scalar(combine[:, b, :], numbers[:, :], index_f[:, b, 0:1], weight[:, b, 0:1], ALU.is_equal, ALU.mult))
            ch.step(dve.tensor_scalar(second[:, b, :], numbers[:, :], index_f[:, b, 1:2], weight[:, b, 1:2], ALU.is_equal, ALU.mult))
        ch.wait()
        ch.step(dve.tensor_tensor(combine[:], combine[:], second[:], ALU.add))

    def choose_scalar(act):
        act.wait_ge(best_ready, 1)
        act.activation(sigmoids[:], best[:, :, 0:2], ACT.Sigmoid).then_inc(sigmoids_ready, 1)

    choose.scalar = choose_scalar
    programs = experts_layer(nc, core, layer, ins, sb, sem, "e16", E, choose)
    experts_sync = programs["sync"]

    def sync(sp):
        sp.wait_ge(core.x_stats, (layer + 1) * B)
        sp.dma_start(numbers[:, :], ins["e16_numbers"].to_broadcast([P, E])).then_inc(numbers_loaded, 16)
        experts_sync(sp)

    programs["sync"] = sync
    return programs


RA_HEADS = 16
RA_DH = P // RA_HEADS
ROPE = RA_DH // 2
MASKED = -2.0 ** 100


def rotary_rows(a):
    by_head = a.reshape(RA_HEADS, RA_DH, *a.shape[1:])
    half = ROPE // 2
    return np.concatenate([by_head[:, half:ROPE], by_head[:, :half], by_head[:, ROPE:]], axis=1).reshape(a.shape)


def rotary_table():
    theta = (1.0 / np.float32(10000.0) ** (np.arange(0, ROPE, 2, dtype=np.float32) / ROPE)).astype(np.float32)
    angle = (np.arange(D, dtype=np.float32)[None, :] * theta[:, None]).astype(np.float32)
    head = np.zeros((RA_DH, 2, D), np.float32)
    head[:, 0] = 1.0
    for half, sign in ((0, -1.0), (ROPE // 2, 1.0)):
        head[half:half + ROPE // 2, 0] = np.cos(angle)
        head[half:half + ROPE // 2, 1] = sign * np.sin(angle)
    return np.tile(head, (RA_HEADS, 1, 1))


def rotary_attention_layer(nc, core, layer, ins, sb, sem):
    H = RA_HEADS
    xn = sb("ra_xn", [P, 4, D], F32)
    weights = sb("ra_weights", [P, 6, P], F32)
    biases = sb("ra_biases", [P, 5], F32)
    bv_row = sb("ra_bv_row", [1, P], F32)
    table = sb("ra_table", [P, 2, D], F32)
    mask_i = sb("ra_mask_i", [P, 2, DC, D], I32)
    mask = sb("ra_mask", [P, 2, DC, D], BF16)
    picks = sb("ra_picks", [P, 2, H // HB, P], F32)
    picks_r = sb("ra_picks_r", [P, 2, H // HB, P], F32R)
    picks_ready = sem("ra_picks_ready")
    own = sb("ra_own", [P, 2, 2, D], F32)
    partner = sb("ra_partner", [P, 2, 2, D], F32)
    rest = sb("ra_rest", [P, 2, D], F32)
    v_t = sb("ra_v_t", [P, B, DC, P], F32)
    qk3 = sb("ra_qk3", [P, B, 3, 2, D], BF16)
    weights_loaded, small_loaded = sem("ra_weights_loaded"), [sem(f"ra_small_loaded{i}") for i in range(5)]
    dve_step, pool_step, mask_ready = sem("ra_dve"), sem("ra_pool"), sem("ra_mask_ready")
    xn_ready, proj_done, proj_read, v_read = sem("ra_xn_ready"), sem("ra_proj_done"), sem("ra_proj_read"), sem("ra_v_read")
    turned_ready, rotated_used = sem("ra_turned_ready"), sem("ra_rotated_used")
    out_done, out_read = sem("ra_out_done"), sem("ra_out_read")
    att = HeadAttention(nc, core, sb, sem, "ra", H, float(RA_DH) ** -0.5, qk3[:, :, :, 0], qk3[:, :, :, 1],
                        lambda b, c: v_t[:, b, c, :], mask=(mask[:, 0], mask[:, 1]))
    att.out_read = out_read

    def bank(j, i):
        return core.psum[:, 3 * j + i, :].rearrange("p (a t) -> p a t", a=2)

    def out_ps():
        return core.psum[:, 6, 0:D]

    def sync(sp):
        sp.wait_ge(core.x_stats, (layer + 1) * B)
        sp.dma_start(weights[:], ins["ra_weights"]).then_inc(weights_loaded, 16)
        for s, (to, name) in zip(small_loaded, ((biases, "ra_biases"), (bv_row, "ra_bv"), (table, "ra_table"),
                                                (picks, "picks16"), (mask_i, "ra_mask"))):
            sp.dma_start(to[:], ins[name]).then_inc(s, 16)
        att.sync(sp)

    def gpsimd(pool):
        ch = Chain(pool, pool_step)
        for b in range(B):
            rstd_row(pool, ch, core, layer, b)
        pool.wait_ge(small_loaded[2], 16)
        for b in range(B):
            j = b % 2
            pool.wait_ge(proj_read, b + 1)
            for i in range(2):
                last = pool.tensor_tensor(partner[:, j, i], partner[:, j, i], table[:, 1], ALU.mult)
            last.then_inc(turned_ready, 1)
        pool.wait_ge(v_read, B)
        att.gpsimd(pool)

    def vector(dve):
        ch = Chain(dve, dve_step)
        att.vector_ones(dve)

        def normalize_x(b):
            dve.wait_ge(core.rstd_ready, layer * B + b + 1)
            if b >= 4:
                dve.wait_ge(proj_done, b - 3)
            dve.tensor_scalar(xn[:, b % 4], core.x_sb[:, b], core.mean_var[:, b, 0:1], core.rstd[:, b],
                              ALU.subtract, ALU.mult).then_inc(xn_ready, 1)

        for b in range(4):
            normalize_x(b)
        dve.wait_ge(small_loaded[4], 16)
        dve.tensor_scalar(mask[:], mask_i[:], 0.0, MASKED, ALU.is_equal, ALU.mult).then_inc(mask_ready, 1)
        dve.wait_ge(small_loaded[2], 16)
        for b in range(B):
            j = b % 2
            dve.wait_ge(proj_read, b + 1)
            for i in range(2):
                ch.step(dve.tensor_tensor(own[:, j, i], own[:, j, i], table[:, 0], ALU.mult))
            ch.wait()
            dve.wait_ge(turned_ready, b + 1)
            ch.step(dve.tensor_tensor(own[:, j], own[:, j], partner[:, j], ALU.add))
            ch.wait()
            split_in_three(dve, ch, own[:, j], rest[:], [qk3[:, b, s] for s in range(3)])
            ch.wait()
            dve.sem_inc(rotated_used, 1)
            if b + 4 < B:
                normalize_x(b + 4)
            dve.sem_inc(att.pieces_ready, 1)
        dve.wait_ge(small_loaded[0], 16)

        def normalize(b):
            att.normalize(dve, ch, b)

        def add_to_x(b):
            dve.wait_ge(out_done, b + 1)
            dve.scalar_tensor_tensor(core.x_sb[:, b], out_ps(), biases[:, 4:5], core.x_sb[:, b], ALU.add, ALU.add)\
                .then_inc(out_read, 1)
            dve.wait_ge(out_read, b + 1)
            layer_norm_rows(dve, ch, core, b)

        att.vector(dve, ch, (normalize, add_to_x))

    def scalar(act):
        act.wait_ge(small_loaded[0], 16)
        for b in range(B):
            j = b % 2
            act.wait_ge(proj_done, b + 1)
            if b >= 2:
                act.wait_ge(rotated_used, b - 1)
            for to, i in ((own, 0), (partner, 1)):
                for a in range(2):
                    last = act.activation(to[:, j, a], bank(j, i)[:, a], ACT.Identity, bias=biases[:, 2 * i + a:2 * i + a + 1])
            last.then_inc(proj_read, 1)
            act.activation(v_t[:, b].rearrange("p c o -> p (c o)"), core.psum[:, 3 * j + 2, 0:DC * P], ACT.Copy).then_inc(v_read, 1)
        act.wait_ge(small_loaded[3], 16)
        act.activation(picks_r[:], picks[:], ACT.Copy).then_inc(picks_ready, 1)
        for b in range(B):
            att.exponentials(act, b)

    def tensor(pe):
        pe.wait_ge(weights_loaded, 16)
        pe.wait_ge(small_loaded[1], 16)
        for b in range(B):
            j = b % 2
            if b >= 2:
                pe.wait_ge(proj_read, b - 1)
                pe.wait_ge(v_read, b - 1)
            pe.wait_ge(xn_ready, b + 1)
            for i in range(2):
                for a, source in enumerate((xn, core.ctx)):
                    pe.matmul(bank(j, i)[:, a], weights[:, 2 * i + a, :], source[:, b % 4 if source is xn else b, :],
                              start=True, stop=True)
            for c in range(DC):
                v_ps = core.psum[:, 3 * j + 2, c * P:(c + 1) * P]
                pe.matmul(v_ps, core.ctx[:, b, c * P:(c + 1) * P], weights[:, 4, :], start=True, stop=False)
                last = pe.matmul(v_ps, core.ones[0:1, :], bv_row[:, :], start=False, stop=True)
            last.then_inc(proj_done, 1)
        pe.wait_ge(v_read, B)
        pe.wait_ge(picks_ready, 1)
        pe.wait_ge(mask_ready, 1)

        def after(b):
            pe.wait_ge(att.norm_ready, b + 1)
            pe.matmul(out_ps(), weights[:, 5, :], att.o_norm[:, b % 2, :], start=True, stop=True).then_inc(out_done, 1)

        att.tensor(pe, (picks_r[:, 0], picks_r[:, 1]), after)

    return dict(sync=sync, gpsimd=gpsimd, vector=vector, scalar=scalar, tensor=tensor)


class Core:
    pass


def build(nc, ins, out, layers):
    core = Core()
    core.last_layer = len(layers) - 1
    with ExitStack() as ctx:
        def sem(name):
            return ctx.enter_context(nc.semaphore(name))

        def sb_of(stack):
            return lambda name, shape, dtype: stack.enter_context(nc.sbuf_tensor(name, shape, dtype))

        sb = sb_of(ctx)
        core.psum = ctx.enter_context(nc.psum_tensor("psum", [P, 8, 512], F32))
        core.x_sb = sb("x_sb", [P, B, D], F32)
        core.ctx = sb("ctx", [P, B, D], F32)
        core.ctx_t = sb("ctx_t", [P, DC, B, T], F32)
        core.ident = sb("ident", [P, P], F32)
        core.ident_bf = sb("ident_bf", [P, P], BF16)
        core.bn = sb("bn", [P, B, 6], F32)
        core.mean_var = sb("mean_var", [P, B, 2], F32)
        core.var_eps = sb("var_eps", [P, B, 1], F32)
        core.rstd = sb("rstd", [P, B, 1], F32)
        core.minus_half = sb("minus_half", [P, 1], F32)
        core.ones = sb("ones", [P, P], F32)
        core.x_loaded = [sem(f"x_loaded{i}") for i in range(B // 2)]
        core.ctx_loaded, core.ctx_t_loaded, core.const_loaded = sem("ctx_loaded"), sem("ctx_t_loaded"), sem("const_loaded")
        core.x_stats, core.rstd_ready = sem("x_stats"), sem("rstd_ready")
        core.consts_set, core.out_stored = sem("consts_set"), sem("out_stored")

        core.stats_step, core.ident_bf_ready = sem("stats_step"), sem("ident_bf_ready")

        for part in (range(0, min(SPLIT, len(layers))), range(SPLIT, len(layers))):
            if not part:
                continue
            begins, ends = part[0] == 0, part[-1] == len(layers) - 1
            if not begins:
                nc.all_engine_barrier()
                nc.clear_and_free_semaphores(used)
                nc.all_engine_barrier()
            semaphores = used = []

            def layer_sem(name):
                semaphores.append(nc.alloc_semaphore(name=name))
                return semaphores[-1]

            programs = []
            part_scope = ExitStack()
            keep = sb_of(part_scope)
            if part[0] == 0:
                core.context_pieces = ContextPieces(nc, core, keep, layer_sem, 8)
                core.ternary_weights = TernaryWeights(nc, core, ins, keep, layer_sem)
                core.fp8_weights = Fp8Weights(nc, core, ins, keep, layer_sem)
            for n in part:
                with ExitStack() as scope:
                    programs.append(layers[n](nc, core, n, ins, sb_of(scope), layer_sem))
            part_scope.close()

            with nc.Block() as block:

                @block.vector
                def _(dve):
                    if begins:
                        dve.memset(core.ones[:, :], 1.0).then_inc(core.consts_set, 1)
                        ch = Chain(dve, core.stats_step)
                        for b in range(B):
                            if b % 2 == 0:
                                dve.wait_ge(core.x_loaded[b // 2], 16)
                            layer_norm_rows(dve, ch, core, b)
                        dve.wait_ge(core.const_loaded, 16)
                        dve.tensor_copy(core.ident_bf[:, :], core.ident[:, :]).then_inc(core.ident_bf_ready, 1)
                    for p, layer in zip(programs, part):
                        if layer:
                            dve.wait_ge(core.x_stats, (layer + 1) * B)
                        p["vector"](nc.vector)

                @block.sync
                def _(sp):
                    if begins:
                        for i in range(B // 2):
                            sp.dma_start(core.x_sb[:, 2 * i:2 * i + 2, :], ins["x"][:, 2 * i:2 * i + 2, :]).then_inc(core.x_loaded[i], 16)
                        sp.dma_start(core.ident[:, :], ins["ident"]).then_inc(core.const_loaded, 16)
                        sp.dma_start(core.ctx_t[:], ins["ctx_t"]).then_inc(core.ctx_t_loaded, 16)
                        sp.dma_start(core.ctx[:], ins["ctx"]).then_inc(core.ctx_loaded, 16)
                    for p, layer in zip(programs, part):
                        p["sync"](nc.sync)
                        if layer == 0:
                            core.fp8_weights.sync(sp)
                            core.ternary_weights.sync(sp)
                    if ends:
                        for i in range(0, B, B // 2):
                            sp.wait_ge(core.x_stats, len(layers) * B + i + B // 2)
                            sp.dma_start(out[:, i:i + B // 2, :], core.x_sb[:, i:i + B // 2, :]).then_inc(core.out_stored, 16)
                        sp.wait_ge(core.out_stored, 32)

                @block.gpsimd
                def _(pool):
                    if begins:
                        pool.memset(core.minus_half[:, :], -0.5).then_inc(core.consts_set, 1)
                        pool.wait_ge(core.consts_set, 2)
                    for p in programs:
                        p["gpsimd"](nc.gpsimd)

                @block.scalar
                def _(act):
                    for p, layer in zip(programs, part):
                        if layer:
                            act.wait_ge(core.x_stats, (layer + 1) * B)
                        p["scalar"](nc.scalar)

                @block.tensor
                def _(pe):
                    if begins:
                        pe.wait_ge(core.consts_set, 2)
                    for p, layer in zip(programs, part):
                        if layer:
                            pe.wait_ge(core.x_stats, (layer + 1) * B)
                        p["tensor"](nc.tensor)


def head_picks(heads):
    width = P // heads
    picks = np.zeros((P, 2, heads // HB, P), np.float32)
    for h in range(heads):
        for d in range(width):
            for part in range(2):
                picks[32 * (h % HB) + part * width + d, part, h // HB, h * width + d] = 1.0
    return picks


def pack_experts(gate, up, down):
    by_chunk = [w.reshape(len(w), DC, P, P).transpose(0, 2, 1, 3).reshape(len(w), P, DC * P) for w in (gate, up)]
    return np.concatenate([*by_chunk, down], axis=2)


def layouts(inputs):
    a = {k: np.asarray(v) for k, v in inputs.items()}
    x, ctx, mask = a["x"], a["ctx_2048"], a["mask_1x1x2048x2048_if1"].reshape(D, D)
    return {
        "x": x.transpose(1, 0, 2),
        "ctx": ctx.transpose(1, 0, 2),
        "ctx_t": ctx.transpose(2, 0, 1).reshape(DC, P, B, T).transpose(1, 0, 2, 3),
        "td": a["L0_xattn_time_decay"].reshape(DC, P).T,
        "tf": a["L0_xattn_time_first"].reshape(DC, P).T,
        "w1_t": a["L0_ffn_w1"].T.reshape(DC, P, FF).transpose(1, 0, 2),
        "w2_t": a["L0_ffn_w2"].T.reshape(FC, P, D).transpose(1, 0, 2),
        "b1": a["L0_ffn_b1"].reshape(1, FF),
        "b2": a["L0_ffn_b2"].reshape(1, D),
        "f8_idx": a["L1_ffn_down_reorder_index"][:F8 // P * P].reshape(F8 // P, P).T,
        "f8_idx_rest": a["L1_ffn_down_reorder_index"][F8 // P * P:].reshape(F8 % P, 1),
        "f8_gate": a["L1_ffn_w_gate"],
        "f8_up": a["L1_ffn_w_up"],
        "f8_down": a["L1_ffn_w_down"],
        "mask_mem": a["mask_BxS2_bk0"].reshape(1, B * T),
        "e64_router": a["L2_ffn_w_router"],
        "e64_experts": pack_experts(a["L2_ffn_w_gate"], a["L2_ffn_w_up"], a["L2_ffn_w_down"]),
        "e16_router": a["L3_ffn_gate_w"].T,
        "e16_experts": pack_experts(a["L3_ffn_gate_up_proj"][:, :, :P], a["L3_ffn_gate_up_proj"][:, :, P:], a["L3_ffn_down_proj"]),
        "e16_numbers": np.arange(16, dtype=np.float32).reshape(1, 16),
        "ra_weights": np.stack([a["L3_xattn_wq"].T, a["L3_xattn_wk"].T, rotary_rows(a["L3_xattn_wq"]).T,
                                rotary_rows(a["L3_xattn_wk"]).T, a["L3_xattn_wv"].T, a["L3_xattn_wo"].T], axis=1),
        "ra_biases": np.stack([a["L3_xattn_bq"], a["L3_xattn_bk"], rotary_rows(a["L3_xattn_bq"]),
                               rotary_rows(a["L3_xattn_bk"]), a["L3_xattn_bo"]], axis=1),
        "ra_bv": a["L3_xattn_bv"].reshape(1, P),
        "ra_table": rotary_table(),
        "ra_mask": np.stack([m.reshape(DC, P, D).transpose(1, 0, 2) for m in (mask, mask.T)], axis=1),
        "picks8": head_picks(8),
        "picks16": head_picks(16),
        "ident": np.eye(P, dtype=np.float32),
    }


SPLIT = 5
LAYERS = [wkv_layer, ternary_ffn_layer, channel_attention_layer, fp8_ffn_layer, memory_attention_layer, top8_experts_layer, rotary_attention_layer, top2_experts_layer]


def kernel(**inputs):
    import concourse.bacc as bacc
    from concourse.bass_utils import run_bass_kernel_spmd

    nc = bacc.Bacc("TRN2", target_bir_lowering=False, num_devices=1)
    arrays = {f"in_{name}": np.ascontiguousarray(a) for name, a in layouts(inputs).items()}
    ins = {name[3:]: nc.dram_tensor(name, a.shape, mybir.dt.from_np(a.dtype), kind="ExternalInput").ap()
           for name, a in arrays.items()}
    out = nc.dram_tensor("out_0", (T, B, D), F32, kind="ExternalOutput").ap()
    build(nc, ins, out, LAYERS)
    result = run_bass_kernel_spmd(nc, [arrays], core_ids=[0])
    return result.results[0]["out_0"].transpose(1, 0, 2)
```
